# Optimizing a Trainium2 kernel written in Bass

```python
import numpy as np
import jax
import jax.numpy as jnp

def _softmax(x, axis=-1):
    return jax.nn.softmax(x, axis=axis)

def _gelu(x):
    return jax.nn.gelu(x, approximate=True)

def _silu(x):
    return jax.nn.silu(x)

def _sigmoid(x):
    return jax.nn.sigmoid(x)

def _layernorm(x, axis=-1, eps=1e-05):
    m = jnp.mean(x, axis=axis, keepdims=True)
    v = jnp.var(x, axis=axis, keepdims=True)
    return (x - m) / jnp.sqrt(v + eps)

def _scatter_add(tgt, idx, src, axis=0):
    return tgt.at[idx].add(src)

def _segment_sum(src, seg, n):
    return jax.ops.segment_sum(src, seg, n)
kernel_name = 'mk_perceiver_d2_seqx_r4_385a6c'

def setup_inputs(seed: int=0):
    np.random.seed(seed)
    _w = jnp.asarray

    def _rec_inputs():
        import jax
        import jax.numpy as jnp
        _rk = jax.random.key(seed)
        x = 7.22e-05 + 1 * jax.random.normal(jax.random.fold_in(_rk, 1), (16, 64, 256), jnp.float32)
        _lenS = 64 - jax.random.randint(jax.random.fold_in(_rk, 7), (16,), 0, max(1, 64 // 4) + 1, jnp.int32)
        _lenS2 = 1601 - jax.random.randint(jax.random.fold_in(_rk, 8), (16,), 0, max(1, 1601 // 4) + 1, jnp.int32)
        _ctx_768P = jax.random.normal(jax.random.fold_in(_rk, 11), (16, 16, 192), jnp.float32)
        _ctx_768c = jax.random.dirichlet(jax.random.fold_in(_rk, 511), 0.3 * jnp.ones((16,), jnp.float32), (16, 1601))
        _ctx_768t = jnp.einsum('bsk,bkd->bsd', _ctx_768c, _ctx_768P)
        _ctx_768t = _ctx_768t * jax.lax.rsqrt(jnp.mean(jnp.square(_ctx_768t)) + 1e-12) * 0.953939
        ctx_768 = 3.88148e-05 + 0.999967 * (_ctx_768t + 0.3 * jax.random.normal(jax.random.fold_in(_rk, 611), (16, 1601, 192), jnp.float32))
        _validS = jnp.arange(64)[None, :] < _lenS[:, None]
        _validS2 = jnp.arange(1601)[None, :] < _lenS2[:, None]
        _causal = jnp.tril(jnp.ones((64, 64), dtype=bool))
        mask_BxS_bf1 = jnp.ones((16, 64), dtype=bool)
        mask_BxS2_bf1 = jnp.ones((16, 1601), dtype=bool)
        return (x, ctx_768, mask_BxS_bf1, mask_BxS2_bf1)
    x, ctx_768, mask_BxS_bf1, mask_BxS2_bf1 = _rec_inputs()

    def _L0_xattn_setup():
        import jax, jax.numpy as jnp
        import numpy as np
        B, T, DT, G, DV = (16, 128, 256, 144, 192)
        H, DH = (4, 32)
        INNER = H * DH
        HID = 4 * DT
        N_STATE = 64
        K_TOP = 32

        def layernorm(x, g, b, eps=1e-05):
            m = x.mean(-1, keepdims=True)
            v = x.var(-1, keepdims=True)
            return (x - m) * jax.lax.rsqrt(v + eps) * g + b

        def s4d(x, log_dt, A_re, A_im, C_re, C_im, D_skip):
            Bb, L, D = x.shape
            dt = jnp.exp(log_dt)
            A = A_re + 1j * A_im
            C = C_re + 1j * C_im
            dtA = dt[:, None] * A
            dC = C * (jnp.exp(dtA) - 1.0) / A
            powers = jnp.exp(dtA[:, :, None] * jnp.arange(L))
            K = 2.0 * jnp.einsum('dn,dnl->dl', dC, powers).real
            n = 2 * L
            Kf = jnp.fft.rfft(K, n=n, axis=-1)
            xf = jnp.fft.rfft(x, n=n, axis=1)
            y = jnp.fft.irfft(xf * Kf.T[None], n=n, axis=1)[:, :L]
            return y + x * D_skip
        key = jax.random.key(seed)
        ks = jax.random.split(key, 16)
        s = 0.02
        inp = {'x_text': jax.random.normal(ks[0], (B, T, DT), jnp.float32), 'x_vision': jax.random.normal(ks[1], (B, G, DV), jnp.float32), 'text_mask': jnp.ones((B, T), bool), 'vision_mask': jnp.ones((B, G), bool), 'Wq': jax.random.normal(ks[2], (DT, INNER), jnp.float32) * s, 'Wk': jax.random.normal(ks[3], (DV, INNER), jnp.float32) * s, 'Wv': jax.random.normal(ks[4], (DV, DT), jnp.float32) * s, 'W_film_in': jax.random.normal(ks[5], (DT, 2 * DT), jnp.float32) * s, 'b_film_in': jnp.zeros((2 * DT,), jnp.float32), 'W_film_out': jax.random.normal(ks[6], (DT, 2 * DT), jnp.float32) * s, 'b_film_out': jnp.zeros((2 * DT,), jnp.float32), 'g_norm_in': jnp.ones((DT,), jnp.float32), 'b_norm_in': jnp.zeros((DT,), jnp.float32), 'g_norm_out': jnp.ones((DT,), jnp.float32), 'b_norm_out': jnp.zeros((DT,), jnp.float32), 'g_ffn': jnp.ones((DT,), jnp.float32), 'b_ffn': jnp.zeros((DT,), jnp.float32), 'W1': jax.random.normal(ks[7], (DT, HID), jnp.float32) * s, 'b1': jnp.zeros((HID,), jnp.float32), 'W2': jax.random.normal(ks[8], (HID, DT), jnp.float32) * s, 'b2': jnp.zeros((DT,), jnp.float32), 'log_dt': jnp.log(0.001) + jax.random.uniform(ks[9], (DT,), jnp.float32) * (jnp.log(0.1) - jnp.log(0.001)), 'A_re': -0.5 * jnp.ones((DT, N_STATE), jnp.float32), 'A_im': jnp.tile(jnp.pi * jnp.arange(N_STATE, dtype=jnp.float32), (DT, 1)), 'C_re': jax.random.normal(ks[10], (DT, N_STATE), jnp.float32) * 0.5 ** 0.5, 'C_im': jax.random.normal(ks[11], (DT, N_STATE), jnp.float32) * 0.5 ** 0.5, 'D_skip': jax.random.normal(ks[12], (DT,), jnp.float32), 'mod_gate': jnp.array(0.5, jnp.float32)}
        return inp
    _L0_xattn_all = _L0_xattn_setup()
    _L0_xattn_in = {k: v for k, v in _L0_xattn_all.items() if k in ('Wq', 'Wk', 'Wv', 'W_film_in', 'b_film_in', 'W_film_out', 'b_film_out', 'g_norm_in', 'b_norm_in', 'g_norm_out', 'b_norm_out', 'g_ffn', 'b_ffn', 'W1', 'b1', 'W2', 'b2', 'log_dt', 'A_re', 'A_im', 'C_re', 'C_im', 'D_skip', 'mod_gate')}
    del _L0_xattn_all

    def _L0_attn_setup():
        import jax, jax.numpy as jnp
        import numpy as np
        N_HEAD = 16
        PAGE_SIZE = 64
        ROPE_THETA = 10000.0

        def _rope_tables(T, D, dtype):
            inv = 1.0 / ROPE_THETA ** (np.arange(0, D, 2, dtype=np.float32) / D)
            ang = np.outer(np.arange(T, dtype=np.float32), inv)
            return (jnp.asarray(np.cos(ang), dtype), jnp.asarray(np.sin(ang), dtype))

        def _apply_rope(x, cos, sin):
            x1 = x[..., 0::2]
            x2 = x[..., 1::2]
            c = cos[None, :, None, :]
            s = sin[None, :, None, :]
            out = jnp.stack([x1 * c - x2 * s, x1 * s + x2 * c], axis=-1)
            return out.reshape(x.shape)
        key = jax.random.key(seed)
        ks = jax.random.split(key, 6)
        B, T, E = (2, 512, 256)
        L = E // 2
        sc = lambda fan: 1.0 / np.sqrt(fan)
        return {'x': jax.random.normal(ks[0], (B, T, E), jnp.float32), 'wq': jax.random.normal(ks[1], (E, E), jnp.float32) * sc(E), 'w_down': jax.random.normal(ks[2], (E, L), jnp.float32) * sc(E), 'wk_up': jax.random.normal(ks[3], (L, E), jnp.float32) * sc(L), 'wv_up': jax.random.normal(ks[4], (L, E), jnp.float32) * sc(L), 'wo': jax.random.normal(ks[5], (E, E), jnp.float32) * sc(E)}
    _L0_attn_all = _L0_attn_setup()
    _L0_attn_in = {k: v for k, v in _L0_attn_all.items() if k in ('wq', 'w_down', 'wk_up', 'wv_up', 'wo')}
    del _L0_attn_all

    def _L0_ffn_setup():
        import jax, jax.numpy as jnp
        import numpy as np
        B, S, H = (2, 1024, 256)
        I = 128
        E = 8
        TOPK = 2
        NGROUP = 2
        TOPK_GROUP = 1
        ROUTED_SCALE = 1.0

        def _silu(x):
            return x * jax.nn.sigmoid(x)
        key = jax.random.key(seed)
        ks = jax.random.split(key, 9)

        def w(k, shape, s=0.05):
            return jax.random.normal(k, shape, dtype=jnp.float32) * s
        return {'hidden_states': jax.random.normal(ks[0], (B, S, H), dtype=jnp.float32), 'router_weight': w(ks[1], (E, H)), 'correction_bias': w(ks[2], (E,)), 'w_gate': w(ks[3], (E, H, I)), 'w_up': w(ks[4], (E, H, I)), 'w_down': w(ks[5], (E, I, H)), 'sw_gate': w(ks[6], (H, I)), 'sw_up': w(ks[7], (H, I)), 'sw_down': w(ks[8], (I, H))}
    _L0_ffn_all = _L0_ffn_setup()
    _L0_ffn_in = {k: v for k, v in _L0_ffn_all.items() if k in ('router_weight', 'correction_bias', 'w_gate', 'w_up', 'w_down', 'sw_gate', 'sw_up', 'sw_down')}
    del _L0_ffn_all

    def _L1_xattn_setup():
        import jax, jax.numpy as jnp
        import numpy as np
        DIM = 256
        CTX_DIM = 192
        HEADS = 16
        key = jax.random.key(seed)
        ks = jax.random.split(key, 7)
        B, N, M = (4, 1024, 64)
        x = jax.random.normal(ks[0], (B, N, DIM), dtype=jnp.float32)
        context = jax.random.normal(ks[1], (B, M, CTX_DIM), dtype=jnp.float32)
        context_mask = jnp.ones((B, M), dtype=bool)
        s_d = 1.0 / np.sqrt(DIM)
        s_c = 1.0 / np.sqrt(CTX_DIM)
        Wq = jax.random.normal(ks[2], (DIM, DIM), dtype=jnp.float32) * s_d
        Wk = jax.random.normal(ks[3], (CTX_DIM, DIM), dtype=jnp.float32) * s_c
        Wv = jax.random.normal(ks[4], (CTX_DIM, DIM), dtype=jnp.float32) * s_c
        Wo = jax.random.normal(ks[5], (DIM, DIM), dtype=jnp.float32) * s_d
        return {'x': x, 'context': context, 'context_mask': context_mask, 'Wq': Wq, 'Wk': Wk, 'Wv': Wv, 'Wo': Wo}
    _L1_xattn_all = _L1_xattn_setup()
    _L1_xattn_in = {k: v for k, v in _L1_xattn_all.items() if k in ('Wq', 'Wk', 'Wv', 'Wo')}
    del _L1_xattn_all

    def _L1_attn_setup():
        import jax, jax.numpy as jnp
        import numpy as np
        B, N, DIM = (2, 512, 256)
        H, DH = (16, 64)
        NUM_MEM = 16
        SPARSE_TOPK = 64
        SCALE = DH ** (-0.5)
        NEG = -jnp.finfo(jnp.float32).max
        key = jax.random.key(seed)
        ks = jax.random.split(key, 10)
        inner = H * DH
        return {'x': jax.random.normal(ks[0], (B, N, DIM), jnp.float32), 'Wq': jax.random.normal(ks[1], (DIM, inner), jnp.float32) * 0.02, 'Wk': jax.random.normal(ks[2], (DIM, inner), jnp.float32) * 0.02, 'Wv': jax.random.normal(ks[3], (DIM, inner), jnp.float32) * 0.02, 'pre_proj': jax.random.normal(ks[4], (H, H), jnp.float32) * 0.25, 'post_proj': jax.random.normal(ks[5], (H, H), jnp.float32) * 0.25, 'mem_k': jax.random.normal(ks[6], (H, NUM_MEM, DH), jnp.float32), 'mem_v': jax.random.normal(ks[7], (H, NUM_MEM, DH), jnp.float32), 'Wo': jax.random.normal(ks[8], (inner, DIM), jnp.float32) * 0.02, 'bo': jnp.zeros((DIM,), jnp.float32)}
    _L1_attn_all = _L1_attn_setup()
    _L1_attn_in = {k: v for k, v in _L1_attn_all.items() if k in ('Wq', 'Wk', 'Wv', 'pre_proj', 'post_proj', 'mem_k', 'mem_v', 'Wo', 'bo')}
    del _L1_attn_all

    def _L1_ffn_setup():
        import jax, jax.numpy as jnp
        import numpy as np
        B, S, D, F, E = (2, 512, 256, 1024, 8)
        LN_EPS = 1e-05

        def _xavier(key, shape, fan_in, fan_out):
            a = np.sqrt(6.0 / (fan_in + fan_out))
            return jax.random.uniform(key, shape, jnp.float32, -a, a)
        key = jax.random.key(seed)
        ks = jax.random.split(key, 8)
        tgt = jax.random.normal(ks[0], (B, S, D), jnp.float32)
        router_w = _xavier(ks[1], (E, D), D, E)
        router_b = jnp.zeros((E,), jnp.float32)
        w1 = _xavier(ks[2], (E, D, F), D, F)
        b1 = jnp.zeros((E, F), jnp.float32)
        w2 = _xavier(ks[3], (E, F, D), F, D)
        b2 = jnp.zeros((E, D), jnp.float32)
        gamma = jnp.ones((D,), jnp.float32)
        beta = jnp.zeros((D,), jnp.float32)
        return {'tgt': tgt, 'router_w': router_w, 'router_b': router_b, 'w1': w1, 'b1': b1, 'w2': w2, 'b2': b2, 'gamma': gamma, 'beta': beta}
    _L1_ffn_all = _L1_ffn_setup()
    _L1_ffn_in = {k: v for k, v in _L1_ffn_all.items() if k in ('router_w', 'router_b', 'w1', 'b1', 'w2', 'b2', 'gamma', 'beta')}
    del _L1_ffn_all
    return {'x': x, 'ctx_768': ctx_768, 'mask_BxS_bf1': mask_BxS_bf1, 'mask_BxS2_bf1': mask_BxS2_bf1, 'L0_xattn_Wq': _L0_xattn_in['Wq'], 'L0_xattn_Wk': _L0_xattn_in['Wk'], 'L0_xattn_Wv': _L0_xattn_in['Wv'], 'L0_xattn_W_film_in': _L0_xattn_in['W_film_in'], 'L0_xattn_b_film_in': _L0_xattn_in['b_film_in'], 'L0_xattn_W_film_out': _L0_xattn_in['W_film_out'], 'L0_xattn_b_film_out': _L0_xattn_in['b_film_out'], 'L0_xattn_g_norm_in': _L0_xattn_in['g_norm_in'], 'L0_xattn_b_norm_in': _L0_xattn_in['b_norm_in'], 'L0_xattn_g_norm_out': _L0_xattn_in['g_norm_out'], 'L0_xattn_b_norm_out': _L0_xattn_in['b_norm_out'], 'L0_xattn_g_ffn': _L0_xattn_in['g_ffn'], 'L0_xattn_b_ffn': _L0_xattn_in['b_ffn'], 'L0_xattn_W1': _L0_xattn_in['W1'], 'L0_xattn_b1': _L0_xattn_in['b1'], 'L0_xattn_W2': _L0_xattn_in['W2'], 'L0_xattn_b2': _L0_xattn_in['b2'], 'L0_xattn_log_dt': _L0_xattn_in['log_dt'], 'L0_xattn_A_re': _L0_xattn_in['A_re'], 'L0_xattn_A_im': _L0_xattn_in['A_im'], 'L0_xattn_C_re': _L0_xattn_in['C_re'], 'L0_xattn_C_im': _L0_xattn_in['C_im'], 'L0_xattn_D_skip': _L0_xattn_in['D_skip'], 'L0_xattn_mod_gate': _L0_xattn_in['mod_gate'], 'L0_attn_wq': _L0_attn_in['wq'], 'L0_attn_w_down': _L0_attn_in['w_down'], 'L0_attn_wk_up': _L0_attn_in['wk_up'], 'L0_attn_wv_up': _L0_attn_in['wv_up'], 'L0_attn_wo': _L0_attn_in['wo'], 'L0_ffn_router_weight': _L0_ffn_in['router_weight'], 'L0_ffn_correction_bias': _L0_ffn_in['correction_bias'], 'L0_ffn_w_gate': _L0_ffn_in['w_gate'], 'L0_ffn_w_up': _L0_ffn_in['w_up'], 'L0_ffn_w_down': _L0_ffn_in['w_down'], 'L0_ffn_sw_gate': _L0_ffn_in['sw_gate'], 'L0_ffn_sw_up': _L0_ffn_in['sw_up'], 'L0_ffn_sw_down': _L0_ffn_in['sw_down'], 'L1_xattn_Wq': _L1_xattn_in['Wq'], 'L1_xattn_Wk': _L1_xattn_in['Wk'], 'L1_xattn_Wv': _L1_xattn_in['Wv'], 'L1_xattn_Wo': _L1_xattn_in['Wo'], 'L1_attn_Wq': _L1_attn_in['Wq'], 'L1_attn_Wk': _L1_attn_in['Wk'], 'L1_attn_Wv': _L1_attn_in['Wv'], 'L1_attn_pre_proj': _L1_attn_in['pre_proj'], 'L1_attn_post_proj': _L1_attn_in['post_proj'], 'L1_attn_mem_k': _L1_attn_in['mem_k'], 'L1_attn_mem_v': _L1_attn_in['mem_v'], 'L1_attn_Wo': _L1_attn_in['Wo'], 'L1_attn_bo': _L1_attn_in['bo'], 'L1_ffn_router_w': _L1_ffn_in['router_w'], 'L1_ffn_router_b': _L1_ffn_in['router_b'], 'L1_ffn_w1': _L1_ffn_in['w1'], 'L1_ffn_b1': _L1_ffn_in['b1'], 'L1_ffn_w2': _L1_ffn_in['w2'], 'L1_ffn_b2': _L1_ffn_in['b2'], 'L1_ffn_gamma': _L1_ffn_in['gamma'], 'L1_ffn_beta': _L1_ffn_in['beta']}

def reference(x, ctx_768, mask_BxS_bf1, mask_BxS2_bf1, L0_xattn_Wq, L0_xattn_Wk, L0_xattn_Wv, L0_xattn_W_film_in, L0_xattn_b_film_in, L0_xattn_W_film_out, L0_xattn_b_film_out, L0_xattn_g_norm_in, L0_xattn_b_norm_in, L0_xattn_g_norm_out, L0_xattn_b_norm_out, L0_xattn_g_ffn, L0_xattn_b_ffn, L0_xattn_W1, L0_xattn_b1, L0_xattn_W2, L0_xattn_b2, L0_xattn_log_dt, L0_xattn_A_re, L0_xattn_A_im, L0_xattn_C_re, L0_xattn_C_im, L0_xattn_D_skip, L0_xattn_mod_gate, L0_attn_wq, L0_attn_w_down, L0_attn_wk_up, L0_attn_wv_up, L0_attn_wo, L0_ffn_router_weight, L0_ffn_correction_bias, L0_ffn_w_gate, L0_ffn_w_up, L0_ffn_w_down, L0_ffn_sw_gate, L0_ffn_sw_up, L0_ffn_sw_down, L1_xattn_Wq, L1_xattn_Wk, L1_xattn_Wv, L1_xattn_Wo, L1_attn_Wq, L1_attn_Wk, L1_attn_Wv, L1_attn_pre_proj, L1_attn_post_proj, L1_attn_mem_k, L1_attn_mem_v, L1_attn_Wo, L1_attn_bo, L1_ffn_router_w, L1_ffn_router_b, L1_ffn_w1, L1_ffn_b1, L1_ffn_w2, L1_ffn_b2, L1_ffn_gamma, L1_ffn_beta):
    import jax
    import jax.numpy as jnp

    def _L0_xattn_ref(x_text, x_vision, text_mask, vision_mask, Wq, Wk, Wv, W_film_in, b_film_in, W_film_out, b_film_out, g_norm_in, b_norm_in, g_norm_out, b_norm_out, g_ffn, b_ffn, W1, b1, W2, b2, log_dt, A_re, A_im, C_re, C_im, D_skip, mod_gate):
        import jax, jax.numpy as jnp
        import numpy as np
        B, T, DT, G, DV = (16, 128, 256, 144, 192)
        H, DH = (4, 32)
        INNER = H * DH
        HID = 4 * DT
        N_STATE = 64
        K_TOP = 32

        def layernorm(x, g, b, eps=1e-05):
            m = x.mean(-1, keepdims=True)
            v = x.var(-1, keepdims=True)
            return (x - m) * jax.lax.rsqrt(v + eps) * g + b

        def s4d(x, log_dt, A_re, A_im, C_re, C_im, D_skip):
            Bb, L, D = x.shape
            dt = jnp.exp(log_dt)
            A = A_re + 1j * A_im
            C = C_re + 1j * C_im
            dtA = dt[:, None] * A
            dC = C * (jnp.exp(dtA) - 1.0) / A
            powers = jnp.exp(dtA[:, :, None] * jnp.arange(L))
            K = 2.0 * jnp.einsum('dn,dnl->dl', dC, powers).real
            n = 2 * L
            Kf = jnp.fft.rfft(K, n=n, axis=-1)
            xf = jnp.fft.rfft(x, n=n, axis=1)
            y = jnp.fft.irfft(xf * Kf.T[None], n=n, axis=1)[:, :L]
            return y + x * D_skip
        Bb, Tt, D = x_text.shape
        Gg = x_vision.shape[1]
        Q = (x_text @ Wq).reshape(Bb, Tt, H, DH)
        K = (x_vision @ Wk).reshape(Bb, Gg, H, DH)
        scores = jnp.einsum('bthd,bghd->bhtg', Q, K) / np.sqrt(DH).astype(np.float32)
        scores = jnp.where(vision_mask[:, None, None, :], scores, -jnp.inf)
        topv, topi = jax.lax.top_k(scores, K_TOP)
        probs = jax.nn.softmax(topv, axis=-1)
        bi = jnp.arange(Bb)[:, None, None, None]
        hi = jnp.arange(H)[None, :, None, None]
        ti = jnp.arange(Tt)[None, None, :, None]
        attn = jnp.zeros_like(scores).at[bi, hi, ti, topi].set(probs)
        attn_mean = attn.mean(axis=1)
        V = x_vision @ Wv
        c_t = jnp.einsum('btg,bgd->btd', attn_mean, V)
        c_t = c_t * text_mask[..., None]
        x = layernorm(x_text, g_norm_in, b_norm_in)
        scale_in, shift_in = jnp.split(c_t @ W_film_in + b_film_in, 2, axis=-1)
        x = x * (1.0 + mod_gate * scale_in) + mod_gate * shift_in
        y = s4d(x, log_dt, A_re, A_im, C_re, C_im, D_skip)
        scale_out, shift_out = jnp.split(c_t @ W_film_out + b_film_out, 2, axis=-1)
        y = y * (1.0 + mod_gate * scale_out) + mod_gate * shift_out
        xt = x_text + y
        h = layernorm(xt, g_ffn, b_ffn)
        h = jax.nn.gelu(h @ W1 + b1, approximate=False) @ W2 + b2
        xt = xt + h
        return layernorm(xt, g_norm_out, b_norm_out)

    def _L0_attn_ref(x, wq, w_down, wk_up, wv_up, wo):
        import jax, jax.numpy as jnp
        import numpy as np
        N_HEAD = 16
        PAGE_SIZE = 64
        ROPE_THETA = 10000.0

        def _rope_tables(T, D, dtype):
            inv = 1.0 / ROPE_THETA ** (np.arange(0, D, 2, dtype=np.float32) / D)
            ang = np.outer(np.arange(T, dtype=np.float32), inv)
            return (jnp.asarray(np.cos(ang), dtype), jnp.asarray(np.sin(ang), dtype))

        def _apply_rope(x, cos, sin):
            x1 = x[..., 0::2]
            x2 = x[..., 1::2]
            c = cos[None, :, None, :]
            s = sin[None, :, None, :]
            out = jnp.stack([x1 * c - x2 * s, x1 * s + x2 * c], axis=-1)
            return out.reshape(x.shape)
        B, T, E = x.shape
        H = N_HEAD
        D = E // H
        q = (x @ wq).reshape(B, T, H, D)
        lat = x @ w_down
        k = (lat @ wk_up).reshape(B, T, H, D)
        v = (lat @ wv_up).reshape(B, T, H, D)
        cos, sin = _rope_tables(T, D, x.dtype)
        q = _apply_rope(q, cos, sin)
        k = _apply_rope(k, cos, sin)
        scale = 1.0 / jnp.sqrt(jnp.asarray(D, x.dtype))
        scores = jnp.einsum('bqhd,bkhd->bhqk', q, k) * scale
        pages = jnp.arange(T) // PAGE_SIZE
        allowed = pages[None, :] <= pages[:, None]
        scores = jnp.where(allowed[None, None], scores, jnp.finfo(scores.dtype).min)
        attn = jax.nn.softmax(scores, axis=-1)
        out = jnp.einsum('bhqk,bkhd->bqhd', attn, v).reshape(B, T, E)
        return out @ wo

    def _L0_ffn_ref(hidden_states, router_weight, correction_bias, w_gate, w_up, w_down, sw_gate, sw_up, sw_down):
        import jax, jax.numpy as jnp
        import numpy as np
        B, S, H = (2, 1024, 256)
        I = 128
        E = 8
        TOPK = 2
        NGROUP = 2
        TOPK_GROUP = 1
        ROUTED_SCALE = 1.0

        def _silu(x):
            return x * jax.nn.sigmoid(x)
        b, s, h = hidden_states.shape
        x = hidden_states.reshape(-1, h)
        logits = x @ router_weight.T
        scores = jax.nn.sigmoid(logits)
        scores_for_choice = scores + correction_bias[None, :]
        e_per_g = E // NGROUP
        group_scores = jax.lax.top_k(scores_for_choice.reshape(-1, NGROUP, e_per_g), 2)[0].sum(-1)
        group_idx = jax.lax.top_k(group_scores, TOPK_GROUP)[1]
        group_mask = jax.nn.one_hot(group_idx, NGROUP, dtype=scores.dtype).sum(1)
        score_mask = jnp.repeat(group_mask, e_per_g, axis=1)
        masked = jnp.where(score_mask > 0, scores_for_choice, 0.0)
        topk_idx = jax.lax.top_k(masked, TOPK)[1]
        topk_w = jnp.take_along_axis(scores, topk_idx, axis=1)
        topk_w = topk_w / (topk_w.sum(-1, keepdims=True) + 1e-20)
        topk_w = topk_w * ROUTED_SCALE
        comb = (jax.nn.one_hot(topk_idx, E, dtype=x.dtype) * topk_w[..., None]).sum(1)
        g = jnp.einsum('th,ehi->tei', x, w_gate)
        u = jnp.einsum('th,ehi->tei', x, w_up)
        y = jnp.einsum('tei,eih->teh', _silu(g) * u, w_down)
        routed = jnp.einsum('teh,te->th', y, comb).reshape(b, s, h)
        shared = _silu(hidden_states @ sw_gate) * (hidden_states @ sw_up) @ sw_down
        return routed + shared

    def _L1_xattn_ref(x, context, context_mask, Wq, Wk, Wv, Wo):
        import jax, jax.numpy as jnp
        import numpy as np
        DIM = 256
        CTX_DIM = 192
        HEADS = 16
        B, N, _ = x.shape
        M = context.shape[1]
        hd = DIM // HEADS
        scale = hd ** (-0.5)
        q = (x @ Wq).reshape(B, N, HEADS, hd).transpose(0, 2, 1, 3)
        k = (context @ Wk).reshape(B, M, HEADS, hd).transpose(0, 2, 1, 3)
        v = (context @ Wv).reshape(B, M, HEADS, hd).transpose(0, 2, 1, 3)
        scores = jnp.einsum('bhid,bhjd->bhij', q, k) * scale
        max_neg = -jnp.finfo(scores.dtype).max
        scores = jnp.where(context_mask[:, None, None, :], scores, max_neg)
        attn = jax.nn.softmax(scores, axis=-1)
        out = jnp.einsum('bhij,bhjd->bhid', attn, v)
        out = out.transpose(0, 2, 1, 3).reshape(B, N, DIM)
        return out @ Wo

    def _L1_attn_ref(x, Wq, Wk, Wv, pre_proj, post_proj, mem_k, mem_v, Wo, bo):
        import jax, jax.numpy as jnp
        import numpy as np
        B, N, DIM = (2, 512, 256)
        H, DH = (16, 64)
        NUM_MEM = 16
        SPARSE_TOPK = 64
        SCALE = DH ** (-0.5)
        NEG = -jnp.finfo(jnp.float32).max
        b, n, _ = x.shape
        q = (x @ Wq).reshape(b, n, H, DH).transpose(0, 2, 1, 3)
        k = (x @ Wk).reshape(b, n, H, DH).transpose(0, 2, 1, 3)
        v = (x @ Wv).reshape(b, n, H, DH).transpose(0, 2, 1, 3)
        k = jnp.concatenate([jnp.broadcast_to(mem_k[None], (b, H, NUM_MEM, DH)), k], axis=2)
        v = jnp.concatenate([jnp.broadcast_to(mem_v[None], (b, H, NUM_MEM, DH)), v], axis=2)
        dots = jnp.einsum('bhid,bhjd->bhij', q, k) * SCALE
        dots = jnp.einsum('bhij,hk->bkij', dots, pre_proj)
        i, j = (dots.shape[-2], dots.shape[-1])
        causal = jnp.triu(jnp.ones((i, j), bool), k=j - i + 1)
        dots = jnp.where(causal[None, None], NEG, dots)
        top = jax.lax.top_k(dots, SPARSE_TOPK)[0]
        vk = top[..., -1:]
        dots = jnp.where(dots < vk, NEG, dots)
        attn = jax.nn.softmax(dots, axis=-1)
        attn = jnp.einsum('bhij,hk->bkij', attn, post_proj)
        out = jnp.einsum('bhij,bhjd->bhid', attn, v)
        out = out.transpose(0, 2, 1, 3).reshape(b, n, H * DH)
        return out @ Wo + bo

    def _L1_ffn_ref(tgt, router_w, router_b, w1, b1, w2, b2, gamma, beta):
        import jax, jax.numpy as jnp
        import numpy as np
        B, S, D, F, E = (2, 512, 256, 1024, 8)
        LN_EPS = 1e-05

        def _xavier(key, shape, fan_in, fan_out):
            a = np.sqrt(6.0 / (fan_in + fan_out))
            return jax.random.uniform(key, shape, jnp.float32, -a, a)
        logits = jnp.einsum('bsd,ed->bse', tgt, router_w) + router_b
        rw = jax.nn.softmax(logits, axis=-1)
        rw = jnp.zeros_like(rw).at[..., 0].set(1.0)
        h = jax.nn.relu(jnp.einsum('bsd,edf->besf', tgt, w1) + b1[None, :, None, :])
        eo = jnp.einsum('besf,efd->besd', h, w2) + b2[None, :, None, :]
        tgt2 = jnp.einsum('besd,bse->bsd', eo, rw)
        x = tgt + tgt2
        mean = jnp.mean(x, axis=-1, keepdims=True)
        var = jnp.mean(jnp.square(x - mean), axis=-1, keepdims=True)
        return (x - mean) * jax.lax.rsqrt(var + LN_EPS) * gamma + beta
    x = x + _L0_xattn_ref(_layernorm(x, axis=-1), ctx_768, mask_BxS_bf1, mask_BxS2_bf1, L0_xattn_Wq, L0_xattn_Wk, L0_xattn_Wv, L0_xattn_W_film_in, L0_xattn_b_film_in, L0_xattn_W_film_out, L0_xattn_b_film_out, L0_xattn_g_norm_in, L0_xattn_b_norm_in, L0_xattn_g_norm_out, L0_xattn_b_norm_out, L0_xattn_g_ffn, L0_xattn_b_ffn, L0_xattn_W1, L0_xattn_b1, L0_xattn_W2, L0_xattn_b2, L0_xattn_log_dt, L0_xattn_A_re, L0_xattn_A_im, L0_xattn_C_re, L0_xattn_C_im, L0_xattn_D_skip, L0_xattn_mod_gate)
    x = x + _L0_attn_ref(_layernorm(x, axis=-1), L0_attn_wq, L0_attn_w_down, L0_attn_wk_up, L0_attn_wv_up, L0_attn_wo)
    x = x + _L0_ffn_ref(_layernorm(x, axis=-1), L0_ffn_router_weight, L0_ffn_correction_bias, L0_ffn_w_gate, L0_ffn_w_up, L0_ffn_w_down, L0_ffn_sw_gate, L0_ffn_sw_up, L0_ffn_sw_down)
    x = x + _L1_xattn_ref(_layernorm(x, axis=-1), ctx_768, mask_BxS2_bf1, L1_xattn_Wq, L1_xattn_Wk, L1_xattn_Wv, L1_xattn_Wo)
    x = x + _L1_attn_ref(_layernorm(x, axis=-1), L1_attn_Wq, L1_attn_Wk, L1_attn_Wv, L1_attn_pre_proj, L1_attn_post_proj, L1_attn_mem_k, L1_attn_mem_v, L1_attn_Wo, L1_attn_bo)
    x = x + _L1_ffn_ref(_layernorm(x, axis=-1), L1_ffn_router_w, L1_ffn_router_b, L1_ffn_w1, L1_ffn_b1, L1_ffn_w2, L1_ffn_b2, L1_ffn_gamma, L1_ffn_beta)
    return x

_drawn_inputs = setup_inputs


def setup_inputs(seed=0):
    import zlib

    import numpy as np

    out = dict(_drawn_inputs(seed))
    spreads = {'L0_xattn_b_film_in': (0.0, 0.1),
     'L0_xattn_b_film_out': (0.0, 0.1),
     'L0_xattn_g_norm_in': (1.0, 0.2),
     'L0_xattn_b_norm_in': (0.0, 0.1),
     'L0_xattn_g_norm_out': (1.0, 0.2),
     'L0_xattn_b_norm_out': (0.0, 0.1),
     'L0_xattn_g_ffn': (1.0, 0.6),
     'L0_xattn_b_ffn': (0.0, 0.8),
     'L0_xattn_b1': (0.0, 0.532),
     'L0_xattn_b2': (0.0, 0.1),
     'L0_xattn_A_re': (-0.5, 0.6),
     'L1_attn_bo': (0.0, 0.1),
     'L1_ffn_router_b': (0.0, 0.1),
     'L1_ffn_b1': (0.0, 0.286),
     'L1_ffn_b2': (0.0, 0.1),
     'L1_ffn_gamma': (1.0, 0.2),
     'L1_ffn_beta': (0.0, 0.1)}
    factors = {'L0_xattn_Wq': 4.125,
     'L0_xattn_Wk': 4.422,
     'L0_xattn_W_film_in': 2.876,
     'L0_xattn_W_film_out': 3.563,
     'L1_attn_Wq': 4.596,
     'L1_attn_Wk': 8.0,
     'L1_attn_pre_proj': 4.728,
     'L1_attn_mem_k': 4.698}
    for name, (base, spread) in spreads.items():
        noise = np.random.default_rng([zlib.crc32(name.encode()), seed]).standard_normal(out[name].shape)
        drawn = base * np.exp(spread * noise) if base else spread * noise
        out[name] = jnp.asarray(drawn.astype(out[name].dtype))
    for name, factor in factors.items():
        out[name] = (out[name] * factor).astype(out[name].dtype)
    return out
```

```python
from contextlib import ExitStack

import numpy as np

import concourse.bass as bass
from concourse import mybir

F32 = mybir.dt.float32
BF16 = mybir.dt.bfloat16
I32 = mybir.dt.int32
U8 = mybir.dt.uint8
ALU = mybir.AluOpType
ACT = mybir.ActivationFunctionType
AXX = mybir.AxisListType.X

B, T, D = 16, 64, 256
J, CD = 1601, 192
P = 128
TILES = B * T // P
NJ = (J + P - 1) // P
JL = J - (NJ - 1) * P
EPS = 1e-5
BIG = 1.0e30
LOW = -3.0e38

XH, XD, KTOP = 4, 32, 32
NST = 64
HID = 1024
H16 = 16
NE, EI = 8, 128
AD, MEM, KEYS, KEEP = 64, 16, 80, 64


def constants():
    c = {}
    f = np.float32
    c["ident"] = np.eye(P, dtype=f)
    c["twice_eye"] = np.concatenate([np.eye(T), np.eye(T)]).astype(f)
    n = 2 * T
    t = np.arange(T)[:, None]
    k = np.arange(T)[None, :]
    cos, sin = np.cos(2 * np.pi * k * t / n), np.sin(2 * np.pi * k * t / n)
    nyq = np.cos(np.pi * t)
    fa = np.concatenate([cos, nyq, -sin[:, 1:]], 1)
    zero = np.zeros((T, 1))
    fb = np.concatenate([zero, -sin[:, 1:], zero, cos[:, 1:]], 1)
    kr = np.concatenate([cos, nyq, cos[:, 1:]], 1)
    ki = np.concatenate([zero, sin[:, 1:], zero, -sin[:, 1:]], 1)
    inv = np.concatenate([cos[:, :1], 2 * cos[:, 1:], nyq, -2 * sin[:, 1:]], 1).T / n
    dft = np.zeros((P, 2, 2, P))
    idft = np.zeros((P, 2, P))
    for b in range(2):
        dft[b * T:(b + 1) * T, b, 0] = fa
        dft[b * T:(b + 1) * T, b, 1] = fb
        idft[:, b, b * T:(b + 1) * T] = inv
    c["dft"] = dft.reshape(P, 4 * P).astype(f)
    c["idft"] = idft.reshape(P, 2 * P).astype(f)
    kd = np.zeros((P, 2, P))
    kd[:T, 0], kd[:T, 1] = kr, ki
    c["kdft"] = kd.reshape(P, 2 * P).astype(f)
    hd = D // H16
    inv_f = (1.0 / 10000.0 ** (np.arange(0, hd, 2, dtype=f) / f(hd))).astype(f)
    ang = np.outer(np.arange(T, dtype=f), inv_f).astype(f)
    co, si = np.cos(ang), np.sin(ang)
    cc = np.tile(np.repeat(co, 2, 1), (2, H16))
    ss = np.tile(np.stack([-si, si], -1).reshape(T, hd), (2, H16))
    q = 1.0 / np.sqrt(hd)
    c["rope"] = np.concatenate([cc * q, cc, ss * q, ss], 1).astype(f)
    c["head_of_row"] = (np.arange(P)[:, None] // hd == np.arange(8)[None, :]).astype(f)
    i8 = np.arange(P)[:, None, None] // H16
    ib = np.arange(8)[None, :, None]
    j = np.arange(KEYS)[None, None, :]
    c["causal"] = np.where((j < T) & (j > ib * 8 + i8), -BIG, 0.0).reshape(P, 8 * KEYS).astype(f)
    c["earlier"] = np.tile((np.arange(8)[None, :] < np.arange(8)[:, None]).reshape(1, 64), (P, 1)).astype(f)
    pick = np.zeros((P, NE, P))
    for e in range(NE):
        pick[e, e] = 1
    c["pick"] = pick.reshape(P, NE * P).astype(f)
    c["pair_diag"] = np.kron(np.eye(2), np.ones((T, hd))).astype(f)
    return c


WB = 16 * 25
WD = 16 * 12
WE = 16 * 7
WF = 16 * 29


class Events(dict):

    def __init__(self, nc, ctx):
        super().__init__()
        self.nc, self.ctx = nc, ctx
        self.sets, self.taken = ([], []), {}

    def __missing__(self, name):
        phase = name[0] if name[1:2] == "_" and not name.endswith("_done") else ""
        if phase and phase in "BCDEFG":
            slots, n = self.sets[ord(phase) % 2], self.taken.get(phase, 0)
            self.taken[phase] = n + 1
            if n == len(slots):
                slots.append(self.ctx.enter_context(self.nc.semaphore(f"phase_{ord(phase) % 2}_{n}")))
            self[name] = slots[n]
        else:
            self[name] = self.ctx.enter_context(self.nc.semaphore(name))
        return self[name]

    def of_phase_before(self, phase):
        return self.sets[(ord(phase) - 1) % 2]


class Arena:

    def __init__(self, whole, at=0):
        self.whole, self.at = whole, at

    def take(self, *shape):
        n = int(np.prod(shape))
        v = self.whole[:, self.at:self.at + n]
        self.at += n
        assert self.at <= self.whole.shape[1], (self.at, self.whole.shape)
        if len(shape) == 2:
            v = v.rearrange("p (a b) -> p a b", a=shape[0])
        if len(shape) == 3:
            v = v.rearrange("p (a b c) -> p a b c", a=shape[0], b=shape[1])
        if len(shape) == 4:
            v = v.rearrange("p (a b c d) -> p a b c d", a=shape[0], b=shape[1], c=shape[2])
        return v


def bank(v, n):
    return v.rearrange("p a b -> p (a b)")[:, 0:n]


class Own:

    def __init__(self, eng, sem):
        self.eng, self.sem, self.n = eng, sem, 0

    def mark(self, ins):
        self.n += 1
        ins.then_inc(self.sem, 1)
        return self.n

    def need(self, n):
        self.eng.wait_ge(self.sem, n)

    def step(self, ins):
        self.need(self.mark(ins))

    def end(self):
        self.need(self.n)
        self.eng.sem_clear(self.sem)


def perceiver(nc, ins, out, stages="ABCDEFG"):
    with ExitStack() as ctx:
        def sb(name, shape, dt=F32):
            return ctx.enter_context(nc.sbuf_tensor(name, shape, dt))

        S = Events(nc, ctx)
        U = 2

        X = sb("X", [P, TILES, D])
        CX = sb("CX", [P, 2, TILES * P])
        ident = sb("ident", [P, P])
        twice_eye = sb("twice_eye", [P, T])
        dft = sb("dft", [P, 2, 2, P])
        idft = sb("idft", [P, 2, P])
        kdft = sb("kdft", [P, 2, P])
        rope = sb("rope", [P, 2, 2 * D])
        head_of_row = sb("head_of_row", [P, 8])
        causal = sb("causal", [P, 8 * KEYS])
        earlier = sb("earlier", [P, 8, 8])
        pair_diag = sb("pair_diag", [P, 32])
        mhalf = sb("mhalf", [P, 1])
        mix = sb("mix", [P, 2, P])
        kfreq = sb("kfreq", [P, 2 * D])
        gains = sb("gains", [P, 8, D])
        gate = sb("gate", [P, 1])
        ones = sb("ones", [P, P])
        rows = sb("rows", [1, 2 * 512 + 3 * 256])
        cols = sb("cols", [P, 2, 8])
        cbias = sb("cbias", [P, 8])
        valid = sb("valid", [P, B])
        qmask = sb("qmask", [P, B])
        carrier = sb("carrier", [P, 88])
        carried = []

        def spare():
            carried.append(1)
            return carrier[:, len(carried) - 1:len(carried)]

        small = sb("small", [P, 256])
        R1 = Arena(sb("region1", [P, 7104]))
        R2 = Arena(sb("region2", [P, 8800]))
        arena = sb("arena", [P, 25060])
        PS = ctx.enter_context(nc.psum_tensor("PS", [P, 8, 512], F32))
        maskbias_dram = nc.dram_tensor("maskbias", (B, J), F32, kind="Internal").ap()

        wq0 = R1.take(2, P)
        wk0t = R1.take(CD)
        wv0 = R1.take(2, D)
        film = R1.take(2, 2, 512)
        w1_0 = R1.take(2, HID)
        w2_0 = R1.take(8, D)
        R1b = Arena(R1.whole)
        wq1 = R1b.take(2, D)
        wk1 = R1b.take(2, D)
        wv1 = R1b.take(2, D)
        wo1 = R1b.take(2, D)
        w1_1 = R1b.take(2, HID)
        w2_1 = R1b.take(8, D)
        aq = R2.take(2, D)
        adown = R2.take(2, P)
        akv = R2.take(2 * D)
        ao = R2.take(2, D)
        router = R2.take(2, NE)
        wgate = R2.take(2, NE + 1, EI)
        wup = R2.take(2, NE + 1, EI)
        wdown = R2.take(NE + 1, D)
        R2b = Arena(R2.whole)
        tq = R2b.take(2, 1024)
        tk = R2b.take(2, 1024)
        tv = R2b.take(2, 1024)
        to = R2b.take(8, D)

        ar = Arena(arena)
        ctxT = [ar.take(2, J) for _ in range(2)]
        ctxN = [ar.take(NJ, CD) for _ in range(2)]
        scores = [ar.take(J) for _ in range(2)]
        rest = [ar.take(J) for _ in range(2)]
        probs = [ar.take(J) for _ in range(2)]
        qsplit = ar.take(XH, P)
        qctx = ar.take(2, 2, XH, T)
        meanT = ar.take(NJ, T)
        xa = ar.take(D)
        xaT = ar.take(2, P)
        bnA = ar.take(16)
        lnA = ar.take(3, TILES)
        tops = ar.take(2, KTOP)
        topx = small[:, 128:192].rearrange("p (a b) -> p a b", a=2)
        rowst = ar.take(2, 8)
        rowdiag = [[ar.take(T) for _ in range(2)] for _ in range(2)]
        kern = ar.take(2, T)
        kernT = ar.take(D)
        maskrow = probs[0][0:B, :]
        masku8 = rest[0].bitcast(U8)[0:B, 0:J]
        textu8 = rest[1].bitcast(U8)[:, 0:B]
        kr = Arena(R2.whole)
        wpow = kr.take(2, 8, P)
        wbig = kr.take(2, 8, P)
        coef = kr.take(2, 8, P)
        ssm = kr.take(5, P)
        tm = [kr.take(P) for _ in range(10)]
        prod = kr.take(8, NST)
        prod2 = rope[:, 0, :].rearrange("p (a b) -> p a b", a=8)
        ldt = small[:, 0:2]

        def both(f):
            return [f() for _ in range(U)]

        ar = Arena(arena)
        xn = both(lambda: ar.take(D))
        xnT = both(lambda: ar.take(2, P))
        bn = both(lambda: ar.take(16))
        work = both(lambda: ar.take(D))
        top = ar.at
        ctT = both(lambda: ar.take(2, P))
        xf = both(lambda: ar.take(D))
        prd = both(lambda: ar.take(2, 2 * D))
        yfq = both(lambda: ar.take(2, D))
        hid = both(lambda: ar.take(8, P))
        ar = Arena(arena, top)
        latT = both(lambda: ar.take(P))
        lat2 = both(lambda: ar.take(2, 2, T))
        rot = both(lambda: ar.take(2 * D))
        rot2 = both(lambda: ar.take(2 * D))
        qz = both(lambda: ar.take(2, 8, P))
        kTs = both(lambda: ar.take(2, P))
        vz = both(lambda: ar.take(2, 8, 32))
        pr = both(lambda: ar.take(H16, T))
        prT = both(lambda: ar.take(8, P))
        st = both(lambda: ar.take(3, H16))
        oc = both(lambda: ar.take(H16, 16))
        ocT = both(lambda: ar.take(2, P))
        ar = Arena(arena, top)
        rt = both(lambda: ar.take(16, 8))
        cmp8 = both(lambda: ar.take(2, 8, 8))
        combT = both(lambda: ar.take(P))
        th = both(lambda: ar.take(4 * P))
        h9 = both(lambda: ar.take(NE + 1, P))
        pick = ar.take(NE, P)
        rbias = ar.take(8)

        ar = Arena(arena, top)
        fqz = both(lambda: ar.take(8, 2, T, 2))
        fk = both(lambda: ar.take(8, 2, KEYS))
        fv = both(lambda: ar.take(2, 16 * AD))
        foT = both(lambda: ar.take(8, P))
        fdT = [ar.take(T, H16) for _ in range(2 * U)]
        fd = [ar.take(8, KEYS) for _ in range(2 * U)]
        fm = [ar.take(8, KEYS) for _ in range(2 * U)]
        fst = [ar.take(32) for _ in range(2 * U)]
        f8 = [ar.take(2, 8) for _ in range(2 * U)]
        ar = Arena(arena, top)
        ghid = both(lambda: ar.take(8, P))
        ar = Arena(arena, top)
        ectx = [ar.take(2, J) for _ in range(2)]
        eK = ar.take(3, J)
        eV = ar.take(NJ, 8, 33)
        eP = [ar.take(2 * 512) for _ in range(2)]
        eqT = ar.take(3, P)
        eqz = ar.take(H16, T)
        emax = ar.take(8, 98)
        eo = ar.take(8, 32)
        eoT = ar.take(2, P)
        erz = ar.take(8)
        def flat(v):
            return v.rearrange("p a b -> p (a b)")

        def v_ln(dve, v, own, j, name, src, dst, ready=None):
            m = [0] * U
            for u in range(U):
                if ready is not None:
                    own.need(ready[u])
                m[u] = own.mark(v.bn_stats(bn[u][:, 0:6], src(u)))
            for u in range(U):
                own.need(m[u])
                m[u] = own.mark(v.bn_aggr(bn[u][:, 6:8], bn[u][:, 0:6]))
            for u in range(U):
                own.need(m[u])
                v.tensor_scalar(bn[u][:, 8:9], bn[u][:, 7:8], EPS, None, ALU.add).then_inc(S[name + "_var"], 1)
            for u in range(U):
                dve.wait_ge(S[name + "_rstd"], j * U + u + 1)
                m[u] = own.mark(v.tensor_scalar(dst(u), src(u), bn[u][:, 6:7], bn[u][:, 9:10], ALU.subtract, ALU.mult))
            return m

        def v_affine(v, own, m, x, i):
            for u in range(U):
                own.need(m[u])
                m[u] = own.mark(v.tensor_tensor(x(u), x(u), gains[:, i, :], ALU.mult))
            for u in range(U):
                own.need(m[u])
                m[u] = own.mark(v.tensor_tensor(x(u), x(u), gains[:, i + 1, :], ALU.add))
            return m

        def xtile(j, u):
            return X[:, bass.ds(j * U + u, 1), :].rearrange("p a b -> p (a b)")

        def cxtile(j, u, c):
            return CX[:, c, bass.ds(j * (U * P) + u * P, P)]

        def pe_turn(pe, u, bk, x):
            for c in range(2):
                i_ = pe.transpose(PS[:, 4 * u + bk, c * P:(c + 1) * P], x[:, c * P:(c + 1) * P], ident[:])
            return i_

        def pe_B(pe, mm, mm2):
            pe.wait_ge(S["kfreq"], 1)
            pe.wait_ge(S["A_done"], 4)
            with pe.Fori(0, TILES // U) as j:
                for u in range(U):
                    pe.wait_ge(S["B_end"], j * U)
                    for o in range(2):
                        os_ = slice(o * P, (o + 1) * P)
                        mm(PS[:, 4 * u, os_], wv0[:, 0, os_], cxtile(j, u, 0), start=True, stop=False)
                        i_ = mm(PS[:, 4 * u, os_], wv0[0:CD - P, 1, os_], cxtile(j, u, 1)[0:CD - P], start=False, stop=True)
                    i_.then_inc(S["B_ctT_psum"], 1)
                for u in range(U):
                    pe.wait_ge(S["B_ctT"], j * U + u + 1)
                    for f in range(2):
                        o = PS[:, 4 * u + 1 + f, :]
                        mm(o, ones[0:1, :], rows[:, f * 512:(f + 1) * 512], start=True, stop=False)
                        mm(o, ctT[u][:, 0, :], film[:, f, 0, :], start=False, stop=False)
                        i_ = mm(o, ctT[u][:, 1, :], film[:, f, 1, :], start=False, stop=True)
                    i_.then_inc(S["B_film_psum"], 1)
                for u in range(U):
                    pe.wait_ge(S["B_xf"], j * U + u + 1)
                    for b in range(2):
                        for f in range(2):
                            i_ = mm(PS[:, 4 * u + 3 * b, f * D:(f + 1) * D], dft[:, b, f, :], xf[u], start=True, stop=True)
                    i_.then_inc(S["B_dft_psum"], 1)
                for u in range(U):
                    pe.wait_ge(S["B_yf"], j * U + u + 1)
                    o = PS[:, 4 * u, 0:D]
                    mm(o, idft[:, 0, :], yfq[u][:, 0, :], start=True, stop=False)
                    mm(o, idft[:, 1, :], yfq[u][:, 1, :], start=False, stop=True).then_inc(S["B_y_psum"], 1)
                for u in range(U):
                    pe.wait_ge(S["B_h"], j * U + u + 1)
                    pe_turn(pe, u, 1, work[u]).then_inc(S["B_h_tp"], 1)
                for u in range(U):
                    pe.wait_ge(S["B_hT"], j * U + u + 1)
                    for c in range(8):
                        cs = slice(c * P, (c + 1) * P)
                        i_ = mm2(PS[:, 4 * u + 2 + c // 4, (c % 4) * P:(c % 4 + 1) * P],
                                 [w1_0[:, k, cs] for k in range(2)], [xnT[u][:, k, :] for k in range(2)])
                    i_.then_inc(S["B_hid_psum"], 1)
                for u in range(U):
                    pe.wait_ge(S["B_hid"], j * U + u + 1)
                    o = PS[:, 4 * u, 0:D]
                    mm(o, ones[0:1, :], rows[:, 1024:1024 + D], start=True, stop=False)
                    for c in range(8):
                        i_ = mm(o, hid[u][:, c, :], w2_0[:, c, :], start=False, stop=c == 7)
                    i_.then_inc(S["B_ffn_psum"], 1)

        def act_B(act, cp):
            act.wait_ge(S["A_done"], 4)
            with act.Fori(0, TILES // U) as j:
                for u in range(U):
                    act.wait_ge(S["B_ctT_psum"], j * U + u + 1)
                    cp(flat(ctT[u]), PS[:, 4 * u, 0:D]).then_inc(S["B_ctT"], 1)
                for u in range(U):
                    act.wait_ge(S["B_h_tp"], j * U + u + 1)
                    cp(flat(xnT[u]), PS[:, 4 * u + 1, 0:D]).then_inc(S["B_hT"], 1)
                for u in range(U):
                    act.wait_ge(S["B_hid_psum"], j * U + u + 1)
                    for c in range(8):
                        i_ = nc.scalar.activation(hid[u][:, c, :], PS[:, 4 * u + 2 + c // 4, (c % 4) * P:(c % 4 + 1) * P],
                                                  ACT.Gelu, bias=cols[:, 0, c:c + 1])
                    i_.then_inc(S["B_hid"], 1)

        def dve_B(dve, v):
            dve.wait_ge(S["A_done"], 4)
            with dve.Fori(0, TILES // U) as j:
                own = Own(dve, S["dve_turn"])
                m = v_ln(dve, v, own, j, "B0", lambda u: xtile(j, u), lambda u: xn[u])
                m = v_ln(dve, v, own, j, "B1", lambda u: xn[u], lambda u: xf[u], m)
                m = v_affine(v, own, m, lambda u: xf[u], 0)

                def filmed(f, x, m, wait):
                    for u in range(U):
                        if wait is not None:
                            dve.wait_ge(S[wait], j * U + u + 1)
                        own.step(v.tensor_scalar(prd[u][:, 0, 0:D], PS[:, 4 * u + 1 + f, 0:D], gate[:], 1.0, ALU.mult, ALU.add))
                        own.need(m[u])
                        own.step(v.tensor_tensor(x(u), x(u), prd[u][:, 0, 0:D], ALU.mult))
                        m[u] = own.mark(v.scalar_tensor_tensor(x(u), PS[:, 4 * u + 1 + f, D:2 * D], gate[:], x(u), ALU.mult, ALU.add))
                    return m

                m = filmed(0, lambda u: xf[u], m, "B_film_psum")
                for u in range(U):
                    own.need(m[u])
                    v.nop().then_inc(S["B_xf"], 1)
                for u in range(U):
                    dve.wait_ge(S["B_dft_psum"], j * U + u + 1)
                    for b in range(2):
                        m[u] = own.mark(v.tensor_tensor(prd[u][:, b, :], PS[:, 4 * u + 3 * b, :], kfreq[:], ALU.mult))
                    own.need(m[u])
                    v.tensor_tensor(yfq[u], prd[u][:, :, 0:D], prd[u][:, :, D:2 * D], ALU.add).then_inc(S["B_yf"], 1)
                for u in range(U):
                    dve.wait_ge(S["B_y_psum"], j * U + u + 1)
                    m[u] = own.mark(v.tensor_copy(xf[u], PS[:, 4 * u, 0:D]))
                m = filmed(1, lambda u: xf[u], m, None)
                for u in range(U):
                    own.need(m[u])
                    m[u] = own.mark(v.tensor_tensor(xn[u], xn[u], xf[u], ALU.add))
                m = v_ln(dve, v, own, j, "B2", lambda u: xn[u], lambda u: work[u], m)
                m = v_affine(v, own, m, lambda u: work[u], 2)
                for u in range(U):
                    own.need(m[u])
                    v.nop().then_inc(S["B_h"], 1)
                for u in range(U):
                    dve.wait_ge(S["B_ffn_psum"], j * U + u + 1)
                    m[u] = own.mark(v.tensor_tensor(xn[u], xn[u], PS[:, 4 * u, 0:D], ALU.add))
                for u in range(U):
                    own.need(m[u])
                    v.nop().then_inc(S["B_end"], 1)
                m = v_ln(dve, v, own, j, "B3", lambda u: xn[u], lambda u: work[u], m)
                m = v_affine(v, own, m, lambda u: work[u], 4)
                for u in range(U):
                    own.need(m[u])
                    m[u] = own.mark(v.tensor_tensor(xtile(j, u), xtile(j, u), work[u], ALU.add))
                for u in range(U):
                    own.need(m[u])
                own.end()

        def pe_C(pe, mm, mm2):
            pe.wait_ge(S["wC_in"], 16 * 7)
            with pe.Fori(0, TILES // U) as j:
                n = lambda u: j * U + u + 1
                for u in range(U):
                    pe.wait_ge(S["C_end"], j * U)
                    pe.wait_ge(S["C_xn"], n(u))
                    pe_turn(pe, u, 0, xn[u]).then_inc(S["C_tp"], 1)
                for u in range(U):
                    pe.wait_ge(S["C_xnT"], n(u))
                    xs = [xnT[u][:, c, :] for c in range(2)]
                    mm2(PS[:, 4 * u + 1, 0:P], [adown[:, c, :] for c in range(2)], xs).then_inc(S["C_lat_psum"], 1)
                    mm2(PS[:, 4 * u + 2, 0:D], xs, [aq[:, c, :] for c in range(2)])
                for u in range(U):
                    pe.wait_ge(S["C_latT"], n(u))
                    mm(PS[:, 4 * u + 2, D:2 * D], latT[u], akv[:, 0:D], start=True, stop=True)
                    for b in range(2):
                        i_ = mm(PS[:, 4 * u + 3, b * D:(b + 1) * D],
                                flat(lat2[u][:, b]), akv[:, D:2 * D],
                                start=True, stop=True)
                    i_.then_inc(S["C_qkv_psum"], 1)
                for u in range(U):
                    pe.wait_ge(S["C_rot"], n(u))
                    for i in range(4):
                        i_ = pe.transpose(PS[:, 4 * u + i // 2, (i % 2) * P:(i % 2 + 1) * P],
                                          rot[u][:, i * P:(i + 1) * P], ident[:])
                    i_.then_inc(S["C_rot_tp"], 1)
                for u in range(U):
                    pe.wait_ge(S["C_qz"], n(u))
                    pe.wait_ge(S["C_kT"], n(u))
                    pe.wait_ge(S["C_vz"], n(u))
                    for h in range(H16):
                        for b in range(2):
                            bs = slice(b * T, (b + 1) * T)
                            i_ = mm(PS[bs, 4 * u + 2 + h // 8, (h % 8) * T:(h % 8 + 1) * T],
                                    qz[u][:, h // 8, h % 8, bs], kTs[u][:, h // 8, bs], start=True, stop=True)
                    i_.then_inc(S["C_s_psum"], 1)
                for u in range(U):
                    pe.wait_ge(S["C_pr"], n(u))
                    for i in range(8):
                        i_ = pe.transpose(PS[:, 4 * u + i // 4, (i % 4) * P:(i % 4 + 1) * P],
                                          flat(pr[u])[:, i * P:(i + 1) * P], ident[:])
                    i_.then_inc(S["C_pr_tp"], 1)
                for u in range(U):
                    pe.wait_ge(S["C_prT"], n(u))
                    for i in range(8):
                        for b in range(2):
                            bs = slice(b * T, (b + 1) * T)
                            i_ = mm(PS[bs, 4 * u + 2, i * 32:(i + 1) * 32], prT[u][:, i, bs], vz[u][:, b, i, :],
                                    start=True, stop=True)
                    i_.then_inc(S["C_o_psum"], 1)
                for u in range(U):
                    pe.wait_ge(S["C_oc"], n(u))
                    pe_turn(pe, u, 3, flat(oc[u])).then_inc(S["C_oc_tp"], 1)
                for u in range(U):
                    pe.wait_ge(S["C_ocT"], n(u))
                    mm2(PS[:, 4 * u, 0:D], [ocT[u][:, c, :] for c in range(2)], [ao[:, c, :] for c in range(2)]
                        ).then_inc(S["C_y_psum"], 1)

        def act_C(act, cp):
            act.wait_ge(S["C_vz0"], 1)
            with act.Fori(0, TILES // U) as j:
                n = lambda u: j * U + u + 1
                for u in range(U):
                    act.wait_ge(S["C_tp"], n(u))
                    cp(flat(xnT[u]), PS[:, 4 * u, 0:D]).then_inc(S["C_xnT"], 1)
                for u in range(U):
                    act.wait_ge(S["C_lat_psum"], n(u))
                    cp(latT[u], PS[:, 4 * u + 1, 0:P])
                    cp(lat2[u], PS[:, 4 * u + 1, 0:P].rearrange("p (b i) -> p b i", b=2).unsqueeze(2).to_broadcast([P, 2, 2, T])
                       ).then_inc(S["C_latT"], 1)
                for u in range(U):
                    act.wait_ge(S["C_qkv_psum"], n(u))
                    for h in range(2):
                        hs = slice(h * T, (h + 1) * T)
                        i_ = cp(vz[u][hs, :, :, h * 16:h * 16 + 16].rearrange("p b i d -> p (b i) d"),
                                PS[hs, 4 * u + 3, :].rearrange("p (a d) -> p a d", d=32)[:, :, h * 16:h * 16 + 16])
                    i_.then_inc(S["C_vz"], 1)
                for u in range(U):
                    act.wait_ge(S["C_rot_tp"], n(u))
                    cp(flat(kTs[u]), PS[:, 4 * u + 1, 0:D]).then_inc(S["C_kT"], 1)
                for u in range(U):
                    act.wait_ge(S["C_sub"], n(u))
                    nc.scalar.activation(flat(pr[u]), flat(pr[u]), ACT.Exp).then_inc(S["C_pr"], 1)
                for u in range(U):
                    act.wait_ge(S["C_pr_tp"], n(u))
                    cp(flat(prT[u]), bank(PS[:, 4 * u:4 * u + 2, :], 8 * P)).then_inc(S["C_prT"], 1)
                for u in range(U):
                    act.wait_ge(S["C_oc_tp"], n(u))
                    cp(flat(ocT[u]), PS[:, 4 * u + 3, 0:D]).then_inc(S["C_ocT"], 1)

        def dve_C(dve, v):
            dve.wait_ge(S["wC_in"], 16 * 7)
            for u in range(U):
                v.memset(vz[u], 0.0)
            dve.drain().then_inc(S["C_vz0"], 1)
            with dve.Fori(0, TILES // U) as j:
                n = lambda u: j * U + u + 1
                own = Own(dve, S["dve_turn"])
                m = v_ln(dve, v, own, j, "C0", lambda u: xtile(j, u), lambda u: xn[u])
                for u in range(U):
                    own.need(m[u])
                    v.nop().then_inc(S["C_xn"], 1)
                for u in range(U):
                    dve.wait_ge(S["C_qkv_psum"], n(u))
                    qk = PS[:, 4 * u + 2, :]
                    own.mark(v.tensor_tensor(rot[u], qk, rope[:, 0, :], ALU.mult))
                    m[u] = own.mark(v.tensor_tensor(rot2[u].rearrange("p (a b) -> p a b", b=2),
                                                    qk.rearrange("p (a b) -> p a b", b=2)[:, :, ::-1],
                                                    rope[:, 1, :].rearrange("p (a b) -> p a b", b=2), ALU.mult))
                for u in range(U):
                    own.need(m[u])
                    v.tensor_tensor(rot[u], rot[u], rot2[u], ALU.add).then_inc(S["C_rot"], 1)
                for u in range(U):
                    dve.wait_ge(S["C_rot_tp"], n(u))
                    for c in range(2):
                        i_ = v.tensor_tensor(qz[u][:, c], PS[:, 4 * u, c * P:(c + 1) * P].unsqueeze(1).to_broadcast([P, 8, P]),
                                             head_of_row[:].unsqueeze(2).to_broadcast([P, 8, P]), ALU.mult)
                    i_.then_inc(S["C_qz"], 1)
                for u in range(U):
                    dve.wait_ge(S["C_s_psum"], n(u))
                    s_ = bank(PS[:, 4 * u + 2:4 * u + 4, :], H16 * T).rearrange("p (a b) -> p a b", a=H16)
                    own.step(v.tensor_reduce(st[u][:, 0, :], s_, AXX, ALU.max))
                    v.tensor_tensor(pr[u], s_, st[u][:, 0, :].unsqueeze(2).to_broadcast([P, H16, T]), ALU.subtract
                                    ).then_inc(S["C_sub"], 1)
                for u in range(U):
                    dve.wait_ge(S["C_pr"], n(u))
                    own.step(v.tensor_reduce(st[u][:, 1, :], pr[u], AXX, ALU.add))
                    m[u] = own.mark(v.reciprocal(st[u][:, 2, :], st[u][:, 1, :]))
                for u in range(U):
                    own.need(m[u])
                    dve.wait_ge(S["C_o_psum"], n(u))
                    v.tensor_tensor(oc[u], PS[:, 4 * u + 2, 0:D].rearrange("p (a b) -> p a b", a=H16),
                                    st[u][:, 2, :].unsqueeze(2).to_broadcast([P, H16, 16]), ALU.mult).then_inc(S["C_oc"], 1)
                for u in range(U):
                    dve.wait_ge(S["C_y_psum"], n(u))
                    nc.vector.memset(spare(), 0.0)
                    v.tensor_tensor(xtile(j, u), xtile(j, u), PS[:, 4 * u, 0:D], ALU.add).then_inc(S["C_end"], 1)
                own.end()
                dve.wait_ge(S["C_end"], n(U - 1))
                v.memset(spare(), 0.0)

        def pe_D(pe, mm, mm2):
            pe.wait_ge(S["wD_in"], WD)
            with pe.Fori(0, TILES // U) as j:
                n = lambda u: j * U + u + 1
                for u in range(U):
                    pe.wait_ge(S["D_end"], j * U)
                    pe.wait_ge(S["D_xn"], n(u))
                    pe_turn(pe, u, 0, xn[u]).then_inc(S["D_tp"], 1)
                for u in range(U):
                    pe.wait_ge(S["D_xnT"], n(u))
                    mm2(PS[:, 4 * u + 1, 0:NE], [xnT[u][:, c, :] for c in range(2)], [router[:, c, :] for c in range(2)]
                        ).then_inc(S["D_logit_psum"], 1)

                def experts(u, es, turn):
                    for i, e_ in enumerate(es):
                        for w, bk in ((wgate, 2), (wup, 3)):
                            i_ = mm2(PS[:, 4 * u + bk, i * P:(i + 1) * P], [w[:, c, e_, :] for c in range(2)],
                                     [xnT[u][:, c, :] for c in range(2)])
                    i_.then_inc(S["D_gu_psum"], 1)

                for u in range(U):
                    experts(u, range(0, 4), 0)
                for u in range(U):
                    pe.wait_ge(S["D_comb"], n(u))
                    pe.transpose(PS[0:NE, 4 * u + 1, 0:P], rt[u][:, 15, :], ident[:]).then_inc(S["D_comb_tp"], 1)
                for u in range(U):
                    pe.wait_ge(S["D_combT"], n(u))
                    for e_ in range(NE):
                        i_ = mm(PS[:, 4 * u + e_ // 4, (e_ % 4) * P:(e_ % 4 + 1) * P], pick[0:NE, e_, :], combT[u][0:NE, :],
                                start=True, stop=True)
                    i_.then_inc(S["D_pick_psum"], 1)
                for u in range(U):
                    pe.wait_ge(S["D_h"], j * (3 * U) + u + 1)
                    experts(u, range(4, 8), 1)
                for u in range(U):
                    pe.wait_ge(S["D_h"], j * (3 * U) + U + u + 1)
                    experts(u, [8], 2)
                for u in range(U):
                    pe.wait_ge(S["D_h"], j * (3 * U) + 2 * U + u + 1)
                    o = PS[:, 4 * u + 1, 0:D]
                    for e_ in range(NE + 1):
                        i_ = mm(o, h9[u][:, e_, :], wdown[:, e_, :], start=e_ == 0, stop=e_ == NE)
                    i_.then_inc(S["D_y_psum"], 1)

        def act_D(act, cp):
            with act.Fori(0, TILES // U) as j:
                n = lambda u: j * U + u + 1
                for u in range(U):
                    act.wait_ge(S["D_tp"], n(u))
                    cp(flat(xnT[u]), PS[:, 4 * u, 0:D]).then_inc(S["D_xnT"], 1)
                for u in range(U):
                    act.wait_ge(S["D_logit_psum"], n(u))
                    nc.scalar.activation(rt[u][:, 0, :], PS[:, 4 * u + 1, 0:NE], ACT.Exp, scale=-1.0).then_inc(S["D_e"], 1)

                def tanh(u, w, turn):
                    act.wait_ge(S["D_gu_psum"], j * (3 * U) + turn * U + u + 1)
                    act.wait_ge(S["D_h"], j * (3 * U) + turn * U + u + 1 - U) if turn else None
                    nc.scalar.activation(th[u][:, 0:w], PS[:, 4 * u + 2, 0:w], ACT.Tanh, scale=0.5).then_inc(S["D_th"], 1)

                for u in range(U):
                    tanh(u, 4 * P, 0)
                for u in range(U):
                    act.wait_ge(S["D_comb_tp"], n(u))
                    cp(combT[u][0:NE, :], PS[0:NE, 4 * u + 1, 0:P]).then_inc(S["D_combT"], 1)
                for u in range(U):
                    tanh(u, 4 * P, 1)
                for u in range(U):
                    tanh(u, P, 2)

        def dve_D(dve, v):
            dve.wait_ge(S["wD_in"], WD)
            with dve.Fori(0, TILES // U) as j:
                n = lambda u: j * U + u + 1
                own = Own(dve, S["dve_turn"])
                m = v_ln(dve, v, own, j, "D0", lambda u: xtile(j, u), lambda u: xn[u])
                for u in range(U):
                    own.need(m[u])
                    v.nop().then_inc(S["D_xn"], 1)

                def route(u):
                    r = lambda i, a=0, b=8: rt[u][:, i, a:b]
                    tt = v.tensor_tensor
                    dve.wait_ge(S["D_e"], n(u))
                    own.step(v.tensor_scalar(r(1), r(0), 1.0, None, ALU.add))
                    own.step(v.reciprocal(r(1), r(1)))
                    own.step(tt(r(2), r(1), rbias, ALU.add))
                    pairs = r(2).rearrange("p (a b) -> p a b", b=2)
                    own.mark(tt(r(3, 0, 4).unsqueeze(2), pairs[:, :, 0:1], pairs[:, :, 1:2], ALU.max))
                    own.step(tt(r(4, 0, 4).unsqueeze(2), pairs[:, :, 0:1], pairs[:, :, 1:2], ALU.min))
                    hi = r(3, 0, 4).rearrange("p (a b) -> p a b", b=2)
                    lo = r(4, 0, 4).rearrange("p (a b) -> p a b", b=2)
                    own.mark(tt(r(5, 0, 2).unsqueeze(2), hi[:, :, 0:1], hi[:, :, 1:2], ALU.max))
                    own.mark(tt(r(6, 0, 2).unsqueeze(2), hi[:, :, 0:1], hi[:, :, 1:2], ALU.min))
                    own.step(tt(r(7, 0, 2).unsqueeze(2), lo[:, :, 0:1], lo[:, :, 1:2], ALU.max))
                    own.step(tt(r(6, 0, 2), r(6, 0, 2), r(7, 0, 2), ALU.max))
                    own.step(tt(r(5, 0, 2), r(5, 0, 2), r(6, 0, 2), ALU.add))
                    own.mark(tt(r(8, 1, 2), r(5, 1, 2), r(5, 0, 1), ALU.is_gt))
                    own.step(tt(r(8, 0, 1), r(5, 1, 2), r(5, 0, 1), ALU.is_le))
                    own.step(tt(r(9).rearrange("p (a b) -> p a b", b=4), r(2).rearrange("p (a b) -> p a b", b=4),
                                r(8, 0, 2).unsqueeze(2).to_broadcast([P, 2, 4]), ALU.mult))
                    mine = r(9).unsqueeze(2).to_broadcast([P, 8, 8])
                    other = r(9).unsqueeze(1).to_broadcast([P, 8, 8])
                    own.mark(tt(cmp8[u][:, 0], other, mine, ALU.is_gt))
                    own.step(tt(cmp8[u][:, 1], other, mine, ALU.is_equal))
                    own.step(tt(cmp8[u][:, 1], cmp8[u][:, 1], earlier[:], ALU.mult))
                    own.step(tt(cmp8[u][:, 0], cmp8[u][:, 0], cmp8[u][:, 1], ALU.add))
                    own.step(v.tensor_reduce(r(10), cmp8[u][:, 0], AXX, ALU.add))
                    own.step(v.scalar_tensor_tensor(r(11), r(10), 1.5, r(1), ALU.is_lt, ALU.mult))
                    own.step(v.tensor_reduce(r(12, 0, 1), r(11), AXX, ALU.add))
                    own.step(v.tensor_scalar(r(12, 0, 1), r(12, 0, 1), 1e-20, None, ALU.add))
                    own.step(v.reciprocal(r(12, 1, 2), r(12, 0, 1)))
                    v.tensor_scalar(r(15), r(11), r(12, 1, 2), None, ALU.mult).then_inc(S["D_comb"], 1)

                def glu(u, w, turn, cb):
                    dve.wait_ge(S["D_th"], j * (3 * U) + turn * U + u + 1)
                    h_ = flat(h9[u])[:, turn * 4 * P:turn * 4 * P + w]
                    own.step(v.scalar_tensor_tensor(h_, th[u][:, 0:w], 1.0, PS[:, 4 * u + 2, 0:w], ALU.add, ALU.mult))
                    own.step(v.scalar_tensor_tensor(h_, h_, 0.5, PS[:, 4 * u + 3, 0:w], ALU.mult, ALU.mult))
                    if cb is None:
                        v.nop().then_inc(S["D_h"], 1)
                    else:
                        dve.wait_ge(S["D_pick_psum"], n(u))
                        v.tensor_tensor(h_, h_, PS[:, 4 * u + cb, :], ALU.mult).then_inc(S["D_h"], 1)

                for u in range(U):
                    route(u)
                for u in range(U):
                    glu(u, 4 * P, 0, 0)
                for u in range(U):
                    glu(u, 4 * P, 1, 1)
                for u in range(U):
                    glu(u, P, 2, None)
                for u in range(U):
                    dve.wait_ge(S["D_y_psum"], n(u))
                    nc.vector.memset(spare(), 0.0)
                    v.tensor_tensor(xtile(j, u), xtile(j, u), PS[:, 4 * u + 1, 0:D], ALU.add).then_inc(S["D_end"], 1)
                own.end()
                dve.wait_ge(S["D_end"], n(U - 1))
                v.memset(spare(), 0.0)

        SETS = ((0, 6), (6, 6), (12, 4))

        def kset(h):
            return h // 6

        def pe_E(pe, mm, mm2):
            pe.wait_ge(S["wE_in"], WE)
            pe.wait_ge(S["E_ready"], 1)
            pe.nop().then_inc(S["E_v_psum"], 8)
            pe.nop().then_inc(S["E_pv"], 1)
            with pe.Fori(0, TILES) as t:

                def keys(g, b, m):
                    h0, nh = SETS[m]
                    pe.wait_ge(S["E_k"], g * 3 + m + 1)
                    for i in range(4):
                        js = slice(i * 512, min(J, (i + 1) * 512))
                        o = PS[0:nh * 16, i, 0:js.stop - js.start]
                        mm(o, wk1[:, 0, h0 * 16:(h0 + nh) * 16], ectx[b][:, 0, js], start=True, stop=False)
                        i_ = mm(o, wk1[0:CD - P, 1, h0 * 16:(h0 + nh) * 16], ectx[b][0:CD - P, 1, js], start=False, stop=True)
                    i_.then_inc(S["E_k_psum"], 1)

                def values(g, b, i):
                    pe.wait_ge(S["E_v"], g * 7 + i)
                    for c in range(2 * i, min(NJ, 2 * i + 2)):
                        r = P if c < NJ - 1 else JL
                        o = PS[0:r, 4 + i % 2, (c % 2) * D:(c % 2 + 1) * D]
                        mm(o, ectx[b][:, 0, c * P:c * P + r], wv1[:, 0, :], start=True, stop=False)
                        i_ = mm(o, ectx[b][0:CD - P, 1, c * P:c * P + r], wv1[0:CD - P, 1, :], start=False, stop=True)
                    i_.then_inc(S["E_v_psum"], 1)

                def out_turn(g):
                    pe.wait_ge(S["E_o"], g + 1)
                    for c in range(2):
                        i_ = mm(PS[:, 7, c * T:(c + 1) * T], flat(eo[:, 4 * c:4 * c + 4, :]), twice_eye[:], start=True, stop=True)
                    i_.then_inc(S["E_oT_psum"], 1)

                for b in range(2):
                    g = t * 2 + b
                    pe.wait_ge(S[f"E_ctx{b}_in"], t * 32 + 32)
                    keys(g, b, 0)
                    if b == 0:
                        pe.wait_ge(S["E_xn"], t + 1)
                        for c in range(2):
                            i_ = pe.transpose(PS[:, 6, c * P:(c + 1) * P], xn[0][:, c * P:(c + 1) * P], ident[:])
                        i_.then_inc(S["E_tp"], 1)
                    else:
                        out_turn(g - 1)
                    for i in range(3):
                        values(g, b, i)
                    if b == 0:
                        pe.wait_ge(S["E_xnT"], t + 1)
                        for m, (h0, nh) in enumerate(SETS):
                            i_ = mm2(PS[0:nh * 16, 7, m * P:(m + 1) * P], [wq1[:, c, h0 * 16:(h0 + nh) * 16] for c in range(2)],
                                     [xnT[0][:, c, :] for c in range(2)])
                        i_.then_inc(S["E_q_psum"], 1)
                    keys(g, b, 1)
                    for i in range(3, 5):
                        values(g, b, i)
                    keys(g, b, 2)
                    pe.wait_ge(S["E_qz"], g + 1)
                    pe.wait_ge(S["E_v"], g * 7 + 6)
                    pe.wait_ge(S["E_oT"], g + 1)
                    pe.wait_ge(S["E_bias_in"], g * 48 + 48)
                    for p in range(8):
                        if p == 1:
                            pe.wait_ge(S["E_k"], g * 3 + 4)
                        if p >= 2:
                            pe.wait_ge(S["E_max"], g * 8 + p - 1)
                        m = kset(2 * p)
                        for i in range(4):
                            js = slice(i * 512, min(J, (i + 1) * 512))
                            i_ = mm(PS[:, 4 * ((p + 1) % 2) + i, 0:js.stop - js.start], flat(eqz[0:97, 2 * p:2 * p + 2, :]), eK[0:97, m, js],
                                    start=True, stop=True)
                        i_.then_inc(S["E_s_psum"], 1)
                    pe.wait_ge(S["E_max"], g * 8 + 7)
                    values(g, b, 5)
                    pe.wait_ge(S["E_max"], g * 8 + 8)
                    for p in range(8):
                        i_ = mm(PS[0:98, 6 + p // 4, (p % 4) * P:(p % 4 + 1) * P], emax[:, p, :], ident[:], start=True, stop=True)
                    i_.then_inc(S["E_mrow_psum"], 1)
                    values(g, b, 6)
                    pe.wait_ge(S["E_mrow"], g + 1)

                    def attend(c):
                        pe.wait_ge(S["E_p"], g * NJ + c + 1)
                        if c == 0:
                            pe.wait_ge(S["E_v"], g * 7 + 8)
                        r = P if c < NJ - 1 else JL
                        for p in range(8):
                            s_ = (0, 1, 2, 4, 5, 6, 3, 7)[p]
                            i_ = mm(PS[:, 6, p * 33:(p + 1) * 33], eP[c % 2][0:r, s_ * P:(s_ + 1) * P], eV[0:r, c, p, :],
                                    start=c == 0 and p == 0, stop=c == NJ - 1 and p == 7, skip_group_check=True)
                        i_.then_inc(S["E_pv"], 1)

                    for c in range(NJ):
                        r = P if c < NJ - 1 else JL
                        if c >= 2:
                            pe.wait_ge(S["E_p"], g * NJ + c - 1)
                        for m, (h0, nh) in enumerate(SETS):
                            k_ = eK[0:98, m, c * P:c * P + r]
                            if m < 2:
                                mm(PS[0:r, 2 * (c % 2) + m, 0:384], k_, flat(eqz[0:98, h0:h0 + 6, :]), start=True, stop=True)
                            else:
                                mm(PS[0:r, 2 * (c % 2), 384:512], k_, flat(eqz[0:98, 12:14, :]), start=True, stop=True)
                                i_ = mm(PS[0:r, 2 * (c % 2) + 1, 384:512], k_, flat(eqz[0:98, 14:16, :]), start=True, stop=True)
                        i_.then_inc(S["E_sT_psum"], 1)
                        if c >= 1:
                            attend(c - 1)
                    attend(NJ - 1)
                out_turn(t * 2 + 1)
                pe.wait_ge(S["E_oT"], t * 2 + 3)
                mm2(PS[:, 7, 0:D], [eoT[:, c, :] for c in range(2)], [wo1[:, c, :] for c in range(2)]).then_inc(S["E_y_psum"], 1)

        def act_E(act, cp):
            act.wait_ge(S["E_ready"], 1)
            for n in ("E_k", "E_oT"):
                act.nop().then_inc(S[n], 1)
            with act.Fori(0, TILES) as t:

                def out_turned(g, b):
                    act.wait_ge(S["E_oT_psum"], g + 1)
                    cp(eoT[:, :, b * T:(b + 1) * T], PS[:, 7, 0:P].rearrange("p (c i) -> p c i", c=2)).then_inc(S["E_oT"], 1)

                for b in range(2):
                    g = t * 2 + b
                    for m, (h0, nh) in enumerate(SETS):
                        act.wait_ge(S["E_k_psum"], g * 3 + m + 1)
                        cp(eK[0:nh * 16, m, :], bank(PS[0:nh * 16, 0:4, :], J)).then_inc(S["E_k"], 1)
                        if m == 0 and b == 0:
                            act.wait_ge(S["E_tp"], t + 1)
                            cp(flat(xnT[0]), PS[:, 6, 0:D]).then_inc(S["E_xnT"], 1)
                            act.wait_ge(S["E_q_psum"], t + 1)
                            for m_, (h0_, nh_) in enumerate(SETS):
                                i_ = cp(eqT[0:nh_ * 16, m_, :], PS[0:nh_ * 16, 7, m_ * P:(m_ + 1) * P], 0.25)
                            i_.then_inc(S["E_qT"], 1)
                        elif m == 0:
                            out_turned(g - 1, 0)
                    act.wait_ge(S["E_mrow_psum"], g + 1)
                    for i in range(2):
                        i_ = cp(flat(eqz[96:98, 8 * i:8 * i + 8, :]), PS[96:98, 6 + i, :])
                    i_.then_inc(S["E_mrow"], 1)
                    for c in range(NJ):
                        r = P if c < NJ - 1 else JL
                        act.wait_ge(S["E_sT_psum"], g * NJ + c + 1)
                        if c >= 2:
                            act.wait_ge(S["E_pv"], g * NJ + c)
                        nc.scalar.activation(eP[c % 2][0:r, :], bank(PS[0:r, 2 * (c % 2):2 * (c % 2) + 2, :], 1024), ACT.Exp
                                             ).then_inc(S["E_p"], 1)
                out_turned(t * 2 + 1, 1)

        def dve_E(dve, v):
            own = Own(dve, S["dve_E0"])
            dve.wait_ge(S["wE_in"], WE)
            own.step(v.memset(eK[64:P, :, :], 0.0))
            own.step(v.memset(eK[96:98, :, :], 1.0))
            own.step(v.memset(eqz[:, :, :], 1.0))
            own.step(v.memset(emax[:, :, 0:96], 0.0))
            own.step(v.memset(emax[:, :, 96:97], 1.0))
            own.step(v.memset(eV[:, :, :, 32:33], 1.0))
            own.step(v.memset(eqT[64:96, 2, :], 0.0))
            v.nop().then_inc(S["E_ready"], 1)
            v.nop().then_inc(S["E_v"], 1)
            with dve.Fori(0, TILES) as t:
                own = Own(dve, S["dve_turn"])
                b_ = bn[0]
                own.step(v.bn_stats(b_[:, 0:6], X[:, bass.ds(t, 1), :].rearrange("p a b -> p (a b)")))
                own.step(v.bn_aggr(b_[:, 6:8], b_[:, 0:6]))
                v.tensor_scalar(b_[:, 8:9], b_[:, 7:8], EPS, None, ALU.add).then_inc(S["E0_var"], 1)
                dve.wait_ge(S["E0_rstd"], t + 1)
                v.tensor_scalar(xn[0], X[:, bass.ds(t, 1), :].rearrange("p a b -> p (a b)"), b_[:, 6:7], b_[:, 9:10],
                                ALU.subtract, ALU.mult).then_inc(S["E_xn"], 1)

                def values_out(g, i):
                    dve.wait_ge(S["E_v_psum"], g * 7 + i + 9)
                    n_ = 2 if i < NJ // 2 else 1
                    r = P if n_ == 2 else JL
                    v.tensor_copy(eV[0:r, 2 * i:2 * i + n_, :, 0:32],
                                  PS[0:r, 4 + i % 2, 0:n_ * D].rearrange("p (c a d) -> p c a d", c=n_, d=32)).then_inc(S["E_v"], 1)

                for b in range(2):
                    g = t * 2 + b
                    for i in range(3):
                        values_out(g, i)
                    if b == 0:
                        dve.wait_ge(S["E_qT"], t + 1)
                    v.memset(spare(), 0.0)
                    for m, (h0, nh) in enumerate(SETS):
                        i_ = v.scalar_tensor_tensor(eqz[0:96, h0:h0 + nh, :], eqT[0:96, m, b * T:(b + 1) * T].unsqueeze(1).to_broadcast([96, nh, T]),
                                                    valid[0:96, bass.ds(t * 2 + b, 1)],
                                                    head_of_row[0:96, 0:nh].unsqueeze(2).to_broadcast([96, nh, T]), ALU.mult, ALU.mult)
                    i_.then_inc(S["E_qz"], 1)
                    for i in range(3, 5):
                        values_out(g, i)
                    for p in range(8):
                        dve.wait_ge(S["E_s_psum"], g * 8 + p + 1)
                        v.tensor_reduce(emax[:, p, 97:98], bank(PS[:, 4 * ((p + 1) % 2):4 * ((p + 1) % 2) + 4, :], J), AXX, ALU.max,
                                        negate=True).then_inc(S["E_max"], 1)
                    for i in range(5, 7):
                        values_out(g, i)
                    dve.wait_ge(S["E_pv"], g * NJ + NJ + 1)
                    o_ = PS[:, 6, 0:8 * 33].rearrange("p (a d) -> p a d", d=33)
                    own.step(v.reciprocal(erz.unsqueeze(2), o_[:, :, 32:33]))
                    own.step(v.tensor_tensor(eo, o_[:, :, 0:32], erz.unsqueeze(2).to_broadcast([P, 8, 32]), ALU.mult))
                    v.tensor_tensor(eo, eo, pair_diag[:].unsqueeze(1).to_broadcast([P, 8, 32]), ALU.mult).then_inc(S["E_o"], 1)
                dve.wait_ge(S["E_y_psum"], t + 1)
                v.memset(spare(), 0.0)
                x_ = X[:, bass.ds(t, 1), :].rearrange("p a b -> p (a b)")
                own.step(v.tensor_tensor(x_, x_, PS[:, 7, 0:D], ALU.add))
                own.end()

        LANES = 2 * U

        def pe_F(pe, mm, mm2):
            pe.wait_ge(S["wF_in"], WF)
            with pe.Fori(0, TILES // U) as j:
                n = lambda u: j * U + u + 1
                l = lambda w: j * LANES + w + 1
                for u in range(U):
                    pe.wait_ge(S["F_end"], j * U)
                    pe.wait_ge(S["F_xn"], n(u))
                    pe_turn(pe, u, 0, xn[u]).then_inc(S["F_tp"], 1)
                for u in range(U):
                    pe.wait_ge(S["F_xnT"], n(u))
                    xs = [xnT[u][:, c, :] for c in range(2)]
                    for w_, bk, name in ((tq, 0, "F_q_psum"), (tk, 2, "F_k_psum")):
                        for c in range(8):
                            cs = slice(c * P, (c + 1) * P)
                            i_ = mm2(PS[:, 4 * u + bk + c // 4, (c % 4) * P:(c % 4 + 1) * P],
                                     [w_[:, k, cs] for k in range(2)], xs)
                        i_.then_inc(S[name], 1)
                for u in range(U):
                    for b in range(2):
                        pe.wait_ge(S[("F_qz", "F_k")[b]], n(u))
                        for h in range(2):
                            i_ = mm2(PS[0:T, 4 * u + 2 * b + h, :], [xnT[u][:, k, b * T:(b + 1) * T] for k in range(2)],
                                     [tv[:, k, h * 512:(h + 1) * 512] for k in range(2)])
                        i_.then_inc(S["F_v_psum"], 1)
                for w in range(LANES):
                    u, b = divmod(w, 2)
                    pe.wait_ge(S["F_v"], l(w))
                    pe.wait_ge(S["F_qz"], n(u))
                    pe.wait_ge(S["F_k"], n(u))
                    for c in range(8):
                        i_ = mm(PS[0:KEYS, 2 * w + c // 4, (c % 4) * P:(c % 4 + 1) * P], fk[u][:, c, b, :],
                                fqz[u][:, c, b].rearrange("p i h -> p (i h)"), start=True, stop=True)
                    i_.then_inc(S["F_dT_psum"], 1)
                for w in range(LANES):
                    pe.wait_ge(S["F_dT"], l(w))
                    for i in range(8):
                        i_ = pe.transpose(PS[:, 2 * w + i // 4, (i % 4) * KEYS:(i % 4 + 1) * KEYS],
                                          fdT[w][0:KEYS, i * 8:(i + 1) * 8, :].rearrange("p i h -> p (i h)"),
                                          ident[0:KEYS, 0:KEYS])
                    i_.then_inc(S["F_d_psum"], 1)
                for w in range(LANES):
                    pe.wait_ge(S["F_d"], l(w))
                    for i in range(2):
                        i_ = mm(PS[:, 2 * w + i, 0:4 * KEYS], mix[:, 0, :], flat(fd[w][:, 4 * i:4 * i + 4, :]),
                                start=True, stop=True)
                    i_.then_inc(S["F_mix_psum"], 1)
                for w in range(LANES):
                    pe.wait_ge(S["F_p"], l(w))
                    for i in range(8):
                        i_ = mm(PS[0:KEYS, 2 * w + i // 4, (i % 4) * P:(i % 4 + 1) * P], fd[w][:, i, :], mix[:, 1, :],
                                start=True, stop=True)
                    i_.then_inc(S["F_pT_psum"], 1)
                for w in range(LANES):
                    u, b = divmod(w, 2)
                    pe.wait_ge(S["F_pT"], l(w))
                    for h in range(H16):
                        hs = slice((h % 2) * AD, (h % 2 + 1) * AD)
                        i_ = mm(PS[hs, 2 * w, (h // 2) * T:(h // 2 + 1) * T], fv[u][0:KEYS, b, h * AD:(h + 1) * AD],
                                fdT[w].rearrange("p a b -> p (a b)")[0:KEYS, h * T:(h + 1) * T], start=True, stop=True)
                    i_.then_inc(S["F_o_psum"], 1)
                for u in range(U):
                    pe.wait_ge(S["F_oT"], j * LANES + 2 * u + 2)
                    o = PS[:, 4 * u, 0:D]
                    mm(o, ones[0:1, :], rows[:, 1280:1280 + D], start=True, stop=False)
                    for c in range(8):
                        i_ = mm(o, foT[u][:, c, :], to[:, c, :], start=False, stop=c == 7)
                    i_.then_inc(S["F_y_psum"], 1)

        def act_F(act, cp):
            act.wait_ge(S["F_zero"], 1)
            with act.Fori(0, TILES // U) as j:
                n = lambda u: j * U + u + 1
                l = lambda w: j * LANES + w + 1
                for u in range(U):
                    act.wait_ge(S["F_tp"], n(u))
                    cp(flat(xnT[u]), PS[:, 4 * u, 0:D]).then_inc(S["F_xnT"], 1)
                for u in range(U):
                    act.wait_ge(S["F_q_psum"], n(u))
                    for bk in range(2):
                        for h in range(2):
                            hs = slice(h * AD, (h + 1) * AD)
                            i_ = cp(fqz[u][hs, 4 * bk:4 * bk + 4, :, :, h].rearrange("p c b i -> p c (b i)"),
                                    PS[hs, 4 * u + bk, :].rearrange("p (c t) -> p c t", c=4), AD ** -0.5)
                    i_.then_inc(S["F_qz"], 1)
                for w in range(LANES):
                    u, b = divmod(w, 2)
                    act.wait_ge(S["F_v_psum"], l(w))
                    cp(fv[u][0:T, b, :], bank(PS[0:T, 2 * w:2 * w + 2, :], 1024)).then_inc(S["F_v"], 1)
                for w in range(LANES):
                    act.wait_ge(S["F_dT_psum"], l(w))
                    for bk in range(2):
                        i_ = cp(fdT[w][0:KEYS, :, 8 * bk:8 * bk + 8].rearrange("p i (c h) -> p c i h", h=2),
                                PS[0:KEYS, 2 * w + bk, :].rearrange("p (c i h) -> p c i h", c=4, h=2))
                    i_.then_inc(S["F_dT"], 1)
                for w in range(LANES):
                    act.wait_ge(S["F_sub"], l(w))
                    nc.scalar.activation(flat(fd[w]), flat(fd[w]), ACT.Exp).then_inc(S["F_exp"], 1)
                for w in range(LANES):
                    act.wait_ge(S["F_pT_psum"], l(w))
                    for bk in range(2):
                        i_ = cp(fdT[w].rearrange("p a b -> p (a b)")[0:KEYS, :].rearrange("p (h i) -> p i h", h=H16)[:, 32 * bk:32 * bk + 32, :],
                                PS[0:KEYS, 2 * w + bk, :].rearrange("p (i h) -> p i h", h=H16))
                    i_.then_inc(S["F_pT"], 1)

        def dve_F(dve, v):
            for u in range(U):
                i_ = v.memset(fqz[u].rearrange("p a b c d -> p (a b c d)"), 0.0)
            i_.then_inc(S["F_zero"], 1)
            dve.wait_ge(S["wF_in"], WF)
            with dve.Fori(0, TILES // U) as j:
                n = lambda u: j * U + u + 1
                l = lambda w: j * LANES + w + 1
                own = Own(dve, S["dve_turn"])
                m = v_ln(dve, v, own, j, "F0", lambda u: xtile(j, u), lambda u: xn[u])
                for u in range(U):
                    own.need(m[u])
                    v.nop().then_inc(S["F_xn"], 1)
                for u in range(U):
                    dve.wait_ge(S["F_k_psum"], n(u))
                    for bk in range(2):
                        i_ = v.tensor_copy(fk[u][:, 4 * bk:4 * bk + 4, :, 0:T],
                                           PS[:, 4 * u + 2 + bk, :].rearrange("p (c b t) -> p c b t", c=4, b=2))
                    i_.then_inc(S["F_k"], 1)
                for w in range(LANES):
                    dve.wait_ge(S["F_d_psum"], l(w))
                    for i in range(2):
                        i_ = v.tensor_copy(flat(fd[w][:, 4 * i:4 * i + 4, :]), PS[:, 2 * w + i, 0:4 * KEYS])
                    i_.then_inc(S["F_d"], 1)
                LATE = slice(6, 8)
                mk = [0] * LANES
                for w in range(LANES):
                    dve.wait_ge(S["F_mix_psum"], l(w))
                    for i in range(2):
                        mk[w] = own.mark(v.tensor_tensor(flat(fm[w][:, 4 * i:4 * i + 4, :]), PS[:, 2 * w + i, 0:4 * KEYS],
                                                         causal[:, i * 4 * KEYS:(i + 1) * 4 * KEYS], ALU.add))
                for w in range(LANES):
                    own.need(mk[w])
                    own.mark(v.tensor_reduce(fst[w][:, 0:8], fm[w], AXX, ALU.max))
                    mk[w] = own.mark(v.tensor_scalar(fd[w][:, LATE, :], fm[w][:, LATE, :], -1.0, None, ALU.mult))
                for r in range(3):
                    for i in range(2):
                        for w in range(LANES):
                            src = fd[w][:, 6 + i, :]
                            own.need(mk[w])
                            k8 = own.mark(v.max(f8[w][:, i, :], src))
                            if r < 2:
                                own.need(k8)
                                nk = own.mark(v.match_replace(src, f8[w][:, i, :], src, LOW))
                            else:
                                nk = k8
                            if i == 1:
                                mk[w] = nk
                for w in range(LANES):
                    own.need(mk[w])
                    own.mark(v.tensor_scalar(fst[w][:, 8:10], f8[w][:, :, 0], -1.0, None, ALU.mult))
                    v.tensor_tensor(fd[w], fm[w], fst[w][:, 0:8].unsqueeze(2).to_broadcast([P, 8, KEYS]), ALU.subtract
                                    ).then_inc(S["F_sub"], 1)
                for w in range(LANES):
                    dve.wait_ge(S["F_exp"], l(w))
                    for i in range(2):
                        mk[w] = own.mark(v.scalar_tensor_tensor(fd[w][:, 6 + i, :], fm[w][:, 6 + i, :], fst[w][:, 8 + i:9 + i],
                                                                fd[w][:, 6 + i, :], ALU.is_ge, ALU.mult))
                for w in range(LANES):
                    own.need(mk[w])
                    mk[w] = own.mark(v.tensor_reduce(fst[w][:, 16:24], fd[w], AXX, ALU.add))
                for w in range(LANES):
                    own.need(mk[w])
                    mk[w] = own.mark(v.reciprocal(fst[w][:, 24:32], fst[w][:, 16:24]))
                for w in range(LANES):
                    own.need(mk[w])
                    v.tensor_tensor(fd[w], fd[w], fst[w][:, 24:32].unsqueeze(2).to_broadcast([P, 8, KEYS]), ALU.mult
                                    ).then_inc(S["F_p"], 1)
                for w in range(LANES):
                    u, b = divmod(w, 2)
                    dve.wait_ge(S["F_o_psum"], l(w))
                    v.tensor_copy(foT[u][:, :, b * T:(b + 1) * T], PS[:, 2 * w, :].rearrange("p (c i) -> p c i", c=8)
                                  ).then_inc(S["F_oT"], 1)
                for u in range(U):
                    dve.wait_ge(S["F_y_psum"], n(u))
                    v.memset(spare(), 0.0)
                    v.tensor_tensor(xtile(j, u), xtile(j, u), PS[:, 4 * u, 0:D], ALU.add).then_inc(S["F_end"], 1)
                own.end()
                dve.wait_ge(S["F_end"], n(U - 1))
                v.memset(spare(), 0.0)

        def pe_G(pe, mm, mm2):
            pe.wait_ge(S["wG_in"], 32)
            with pe.Fori(0, TILES // U) as j:
                n = lambda u: j * U + u + 1
                for u in range(U):
                    pe.wait_ge(S["G_end"], j * U)
                    pe.wait_ge(S["G_xn"], n(u))
                    pe_turn(pe, u, 0, xn[u]).then_inc(S["G_tp"], 1)
                for u in range(U):
                    pe.wait_ge(S["G_xnT"], n(u))
                    for c in range(8):
                        cs = slice(c * P, (c + 1) * P)
                        i_ = mm2(PS[:, 4 * u + 2 + c // 4, (c % 4) * P:(c % 4 + 1) * P],
                                 [w1_1[:, k, cs] for k in range(2)], [xnT[u][:, k, :] for k in range(2)])
                    i_.then_inc(S["G_hid_psum"], 1)
                for u in range(U):
                    pe.wait_ge(S["G_hid"], n(u))
                    o = PS[:, 4 * u, 0:D]
                    mm(o, ones[0:1, :], rows[:, 1536:1536 + D], start=True, stop=False)
                    for c in range(8):
                        i_ = mm(o, ghid[u][:, c, :], w2_1[:, c, :], start=False, stop=c == 7)
                    i_.then_inc(S["G_ffn_psum"], 1)

        def act_G(act, cp):
            with act.Fori(0, TILES // U) as j:
                n = lambda u: j * U + u + 1
                for u in range(U):
                    act.wait_ge(S["G_tp"], n(u))
                    cp(flat(xnT[u]), PS[:, 4 * u, 0:D]).then_inc(S["G_xnT"], 1)
                for u in range(U):
                    act.wait_ge(S["G_hid_psum"], n(u))
                    for c in range(8):
                        i_ = nc.scalar.activation(ghid[u][:, c, :], PS[:, 4 * u + 2 + c // 4, (c % 4) * P:(c % 4 + 1) * P],
                                                  ACT.Relu, bias=cols[:, 1, c:c + 1])
                    i_.then_inc(S["G_hid"], 1)

        def dve_G(dve, v):
            with dve.Fori(0, TILES // U) as j:
                n = lambda u: j * U + u + 1
                own = Own(dve, S["dve_turn"])
                m = v_ln(dve, v, own, j, "G0", lambda u: xtile(j, u), lambda u: xn[u])
                for u in range(U):
                    own.need(m[u])
                    v.nop().then_inc(S["G_xn"], 1)
                for u in range(U):
                    dve.wait_ge(S["G_ffn_psum"], n(u))
                    m[u] = own.mark(v.tensor_tensor(xn[u], xn[u], PS[:, 4 * u, 0:D], ALU.add))
                for u in range(U):
                    own.need(m[u])
                    v.nop().then_inc(S["G_end"], 1)
                m = v_ln(dve, v, own, j, "G1", lambda u: xn[u], lambda u: work[u], m)
                m = v_affine(v, own, m, lambda u: work[u], 6)
                for u in range(U):
                    own.need(m[u])
                    m[u] = own.mark(v.tensor_tensor(xtile(j, u), xtile(j, u), work[u], ALU.add))
                own.end()


        def pe_rest(pe, mm, mm2):
            pe.wait_ge(S["A_done"], 4)
            for ph, f in (("B", pe_B), ("C", pe_C), ("D", pe_D), ("E", pe_E), ("F", pe_F), ("G", pe_G)):
                if ph in stages:
                    f(pe, mm, mm2)
                    pe.drain().then_inc(S[ph + "_done"], 1)
                    pe.wait_ge(S[ph + "_done"], 4)
            pe.drain().then_inc(S["all_done"], 1)

        def act_rest(act, cp):
            act.wait_ge(S["A_done"], 4)
            for ph, f in (("B", act_B), ("C", act_C), ("D", act_D), ("E", act_E), ("F", act_F), ("G", act_G)):
                if ph in stages:
                    f(act, cp)
                    act.drain().then_inc(S[ph + "_done"], 1)
                    act.wait_ge(S[ph + "_done"], 4)
            act.drain().then_inc(S["all_done"], 1)

        def dve_rest(dve, v):
            dve.wait_ge(S["A_done"], 4)
            for ph, f in (("B", dve_B), ("C", dve_C), ("D", dve_D), ("E", dve_E), ("F", dve_F), ("G", dve_G)):
                if ph in stages:
                    f(dve, v)
                    dve.drain().then_inc(S[ph + "_done"], 1)
                    dve.wait_ge(S[ph + "_done"], 4)
            dve.drain().then_inc(S["all_done"], 1)

        def tail_loads(sp, load):
            if "C" in stages:
                load(rope[:], ins["rope"].rearrange("p (a b) -> p a b", a=2), "wC_in")
                load(head_of_row[:], ins["head_of_row"], "wC_in")
            sp.wait_ge(S["B_done"], 4)
            if "D" in stages:
                for c in range(2):
                    load(wgate[:, c, 0:NE, :], ins["L0_ffn_w_gate"][:, c * P:(c + 1) * P, :].rearrange("e p i -> p e i"), "wD_in")
                for c in range(2):
                    load(wup[:, c, 0:NE, :], ins["L0_ffn_w_up"][:, c * P:(c + 1) * P, :].rearrange("e p i -> p e i"), "wD_in")
                load(wgate[:, :, NE, :], ins["L0_ffn_sw_gate"].rearrange("(c p) i -> p c i", p=P), "wD_in")
                load(wup[:, :, NE, :], ins["L0_ffn_sw_up"].rearrange("(c p) i -> p c i", p=P), "wD_in")
                load(wdown[:, 0:NE, :], ins["L0_ffn_w_down"].rearrange("e i h -> i e h"), "wD_in")
                load(wdown[:, NE, :], ins["L0_ffn_sw_down"], "wD_in")
                load(router, ins["router_T"].rearrange("(c p) e -> p c e", p=P), "wD_in")
                load(earlier[:], ins["earlier"].rearrange("p (a b) -> p a b", a=8), "wD_in")
                sp.wait_ge(S["C_done"], 4)
                load(pick, ins["pick"].rearrange("p (a b) -> p a b", a=NE), "wD_in")
                load(rbias, ins["L0_ffn_correction_bias"].partition_broadcast(P), "wD_in")
            if "E" in stages:
                load(wq1, ins["L1_xattn_Wq"].rearrange("(c p) n -> p c n", p=P), "wE_in")
                for w_, n in ((wk1, "L1_xattn_Wk"), (wv1, "L1_xattn_Wv")):
                    load(w_[:, 0, :], ins[n][0:P, :], "wE_in")
                    load(w_[0:CD - P, 1, :], ins[n][P:CD, :], "wE_in")
                load(wo1, ins["L1_xattn_Wo"].rearrange("(c p) n -> p c n", p=P), "wE_in")
                load(pair_diag[:], ins["pair_diag"], "wE_in")
            if "G" in stages:
                load(w1_1, ins["L1_ffn_w1"].rearrange("(c p) n -> p c n", p=P), "wG_in")
                load(w2_1, ins["L1_ffn_w2"].rearrange("(c p) n -> p c n", p=P), "wG_in")
            sp.wait_ge(S["D_done"], 4)
            if "F" in stages:
                load(tq, ins["L1_attn_Wq"].rearrange("(c p) n -> p c n", p=P), "wF_in")
                load(tk, ins["L1_attn_Wk"].rearrange("(c p) n -> p c n", p=P), "wF_in")
                load(tv, ins["L1_attn_Wv"].rearrange("(c p) n -> p c n", p=P), "wF_in")
                load(to, ins["L1_attn_Wo"].rearrange("(c p) n -> p c n", p=P), "wF_in")
                load(causal[:], ins["causal"], "wF_in")
                sp.wait_ge(S["mix_zero"], 1)
                for f, n in enumerate(("L1_attn_pre_proj", "L1_attn_post_proj")):
                    for i in range(8):
                        load(mix[i * H16:(i + 1) * H16, f, i * H16:(i + 1) * H16], ins[n], "wF_in")
            if "E" in stages:
                sp.wait_ge(S["E_ready"], 1)
                with sp.Fori(0, TILES) as t:
                    for b in range(2):
                        one = bass.ds(t * 2 + b, 1)
                        sp.wait_ge(S["E_v_psum"], t * 14 + b * 7 + 1)
                        load(ectx[b][:, 0, :], ins["ctxT"][one, 0:P, :].rearrange("a p j -> p (a j)"), f"E_ctx{b}_in")
                        load(ectx[b][0:CD - P, 1, :], ins["ctxT"][one, P:CD, :].rearrange("a p j -> p (a j)"), f"E_ctx{b}_in")
                        sp.wait_ge(S["E_pv"], t * 26 + b * 13 + 1)
                        for m in range(3):
                            load(eK[96:97, m, :], maskbias_dram[one, :], "E_bias_in")
            if "F" in stages:
                sp.wait_ge(S["E_done"], 4)
                for u in range(U):
                    for b in range(2):
                        load(fk[u][:, :, b, T:KEYS], ins["mem_kT"], "wF_in")
                        load(fv[u][T:KEYS, b, :], ins["L1_attn_mem_v"], "wF_in")


        block = ctx.enter_context(nc.Block())

        @block.sync
        def _(sp):
            def load(dst, src, name):
                sp.dma_start(dst, src).then_inc(S[name], 16)

            sp.nop().then_inc(S["started"], 1)
            load(masku8, ins["ctx_mask"], "mask_in")
            load(textu8[0:T, :], ins["text_maskT"], "mask_in")
            load(textu8[T:P, :], ins["text_maskT"], "mask_in")
            load(X[:], ins["x"].rearrange("(t p) d -> p t d", p=P), "x_in")
            load(ident[:], ins["ident"], "wA_in")
            load(twice_eye[:], ins["twice_eye"], "wA_in")
            load(wq0, ins["L0_xattn_Wq"].rearrange("(c p) n -> p c n", p=P), "wA_in")
            load(wk0t, ins["L0_xattn_WkT"], "wA_in")
            sp.wait_ge(S["maskbias"], 1)
            sp.dma_start(maskbias_dram, maskrow).then_inc(S["maskbias_out"], 16)
            sp.wait_ge(S["maskbias_out"], 16)

            def context(t, first):
                for b in range(2):
                    one = bass.ds(t * 2 + b, 1)
                    if not first:
                        sp.wait_ge(S["scores_psum"], t * 4 + 2 * b - 2)
                    load(ctxT[b][:, 0, :], ins["ctxT"][one, 0:P, :].rearrange("a p j -> p (a j)"), f"ctxT{b}_in")
                    load(ctxT[b][0:CD - P, 1, :], ins["ctxT"][one, P:CD, :].rearrange("a p j -> p (a j)"), f"ctxT{b}_in")
                    load(ctxT[b][CD - P:CD - P + 1, 1, :], maskbias_dram[one, :], f"ctxT{b}_in")
                for b in range(2):
                    one = bass.ds(t * 2 + b, 1)
                    if not first:
                        sp.wait_ge(S["cx_psum"], t * 2 + b - 1)
                    load(ctxN[b][:, 0:NJ - 1, :],
                         ins["ctx"][one, 0:(NJ - 1) * P, :].rearrange("a (c p) d -> p (a c) d", p=P), f"ctxN{b}_in")
                    load(ctxN[b][0:JL, NJ - 1, :],
                         ins["ctx"][one, (NJ - 1) * P:J, :].rearrange("a p d -> p (a d)"), f"ctxN{b}_in")

            context(0, True)
            with sp.Fori(1, TILES) as t:
                context(t, False)
            sp.wait_ge(S["A_done"], 4)
            if "C" in stages:
                load(aq, ins["L0_attn_wq"].rearrange("(c p) n -> p c n", p=P), "wC_in")
                load(adown, ins["L0_attn_w_down"].rearrange("(c p) n -> p c n", p=P), "wC_in")
                load(akv[:, 0:D], ins["L0_attn_wk_up"], "wC_in")
                load(akv[:, D:2 * D], ins["L0_attn_wv_up"], "wC_in")
                load(ao, ins["L0_attn_wo"].rearrange("(c p) n -> p c n", p=P), "wC_in")
            tail_loads(sp, load)
            sp.wait_ge(S["all_done"], 4)
            sp.dma_start(out.rearrange("(t p) d -> p t d", p=P), X[:]).then_inc(S["out"], 16)
            sp.wait_ge(S["out"], 16)

        @block.tensor
        def _(pe):
            mm = pe.matmul

            def mm2(out_, lhs, rhs):
                mm(out_, lhs[0], rhs[0], start=True, stop=False)
                return mm(out_, lhs[1], rhs[1], start=False, stop=True)

            pe.nop().then_inc(S["meanT_psum"], 2)
            pe.wait_ge(S["valid_diag"], 1)
            pe.wait_ge(S["ones"], 1)
            mm(PS[:, 0, 0:B], ones[0:B, :], small[0:B, 16:16 + B], start=True, stop=True).then_inc(S["valid_psum"], 1)
            pe.wait_ge(S["wA_in"], 16 * 4)

            def q_transposes(t):
                pe.wait_ge(S["xa"], t + 1)
                for c in range(2):
                    i_ = pe.transpose(PS[:, 6, c * P:(c + 1) * P], xa[:, c * P:(c + 1) * P], ident[:])
                i_.then_inc(S["xa_tp"], 1)

            def q_product(t):
                pe.wait_ge(S["xaT"], t + 1)
                mm2(PS[:, 7, 0:P], [wq0[:, c, :] for c in range(2)], [xaT[:, c, :] for c in range(2)]
                    ).then_inc(S["q_psum"], 1)

            def q_context(t):
                pe.wait_ge(S["qsplit"], t + 1)
                mm(PS[:, 6, :], wk0t[:, 0:P], qsplit.rearrange("p a b -> p (a b)"), start=True, stop=True)
                mm(PS[0:CD - P, 7, :], wk0t[:, P:CD], qsplit.rearrange("p a b -> p (a b)"), start=True, stop=True
                   ).then_inc(S["qctx_psum"], 1)

            def score(t, r):
                b, hp = r // 2, r % 2
                if r == 0:
                    pe.wait_ge(S["qctx"], t + 1)
                if hp == 0:
                    pe.wait_ge(S[f"ctxT{b}_in"], t * 48 + 48)
                pe.wait_ge(S["scores_sb"], t * 4 + r + 1)
                q0 = qctx[:, 0, b, 2 * hp:2 * hp + 2, :].rearrange("p a b -> p (a b)")
                q1 = qctx[0:CD - P + 1, 1, b, 2 * hp:2 * hp + 2, :].rearrange("p a b -> p (a b)")
                for n in range(4):
                    js = slice(n * 512, min(J, (n + 1) * 512))
                    o = PS[:, n, 0:js.stop - js.start]
                    mm(o, q0, ctxT[b][:, 0, js], start=True, stop=False)
                    i_ = mm(o, q1, ctxT[b][0:CD - P + 1, 1, js],
                            start=False, stop=True)
                i_.then_inc(S["scores_psum"], 1)

            def mean(t, b, between=None):
                pe.wait_ge(S["probs"], t * 4 + 2 * b + 4)
                pe.wait_ge(S["rowdiag"], t * 4 + 2 * b + 2)
                pe.wait_ge(S["meanT"], t * 2 + b + 1)
                pe.wait_ge(S["cx_out"], t * 2 + b + 1)
                for c in range(NJ):
                    if c == 8 and between is not None:
                        between()
                    r = P if c < NJ - 1 else JL
                    o = PS[0:r, 4 + c // 8, (c % 8) * T:(c % 8) * T + T]
                    for hp in range(2):
                        i_ = mm(o, probs[hp][:, c * P:c * P + r], rowdiag[b][hp], start=hp == 0, stop=hp == 1)
                i_.then_inc(S["meanT_psum"], 1)

            def gather(t, b):
                pe.wait_ge(S["meanT"], t * 2 + b + 2)
                pe.wait_ge(S[f"ctxN{b}_in"], t * 32 + 32)
                for o, ds in ((PS[:, 5, 320:320 + T], slice(0, P)), (PS[0:CD - P, 5, 384:384 + T], slice(P, CD))):
                    for c in range(NJ):
                        r = P if c < NJ - 1 else JL
                        i_ = mm(o, ctxN[b][0:r, c, ds], meanT[0:r, c, :], start=c == 0, stop=c == NJ - 1)
                i_.then_inc(S["cx_psum"], 1)

            def tile(t, first=False, last=False):
                if not last:
                    q_transposes(t + 1)
                score(t, 2)
                if not first:
                    gather(t - 1, 1)
                if not last:
                    q_product(t + 1)
                score(t, 3)
                mean(t, 0, None if last else lambda: q_context(t + 1))
                if not last:
                    score(t + 1, 0)
                gather(t, 0)
                if not last:
                    score(t + 1, 1)
                mean(t, 1)

            q_transposes(0)
            q_product(0)
            q_context(0)
            score(0, 0)
            score(0, 1)
            tile(0, first=True)
            with pe.Fori(1, TILES - 1) as t:
                tile(t)
            tile(TILES - 1, last=True)
            gather(TILES - 1, 1)
            pe.wait_ge(S["kern"], 1)
            pe.wait_ge(S["cx_out"], 2 * TILES + 1)
            for c in range(2):
                i_ = pe.transpose(PS[0:T, 0, c * P:(c + 1) * P], kern[:, c, :], ident[:])
            i_.then_inc(S["kern_tp"], 1)
            pe.wait_ge(S["kernT"], 1)
            pe.wait_ge(S["wB_in"], WB)
            for f in range(2):
                i_ = mm(PS[:, 1, f * D:(f + 1) * D], kdft[0:T, f, :], kernT[0:T, :], start=True, stop=True)
            i_.then_inc(S["kfreq_psum"], 1)
            pe.drain().then_inc(S["A_done"], 1)
            pe_rest(pe, mm, mm2)

        @block.scalar
        def _(act):
            def cp(o, i, scale=1.0):
                return nc.scalar.activation(o, i, ACT.Copy, scale=scale)

            act.dma_start(ssm[:, 0, :], ins["L0_xattn_A_re"].rearrange("(c p) n -> p c n", p=P)).then_inc(S["ssm_in"], 16)
            act.dma_start(ssm[:, 1, :], ins["L0_xattn_A_im"].rearrange("(c p) n -> p c n", p=P)).then_inc(S["ssm_in"], 16)
            act.dma_start(ssm[:, 2, :], ins["L0_xattn_C_re"].rearrange("(c p) n -> p c n", p=P)).then_inc(S["ssm_in"], 16)
            act.dma_start(ssm[:, 3, :], ins["L0_xattn_C_im"].rearrange("(c p) n -> p c n", p=P)).then_inc(S["ssm_in"], 16)
            act.dma_start(ldt, ins["L0_xattn_log_dt"]).then_inc(S["ssm_in"], 16)
            act.dma_start(small[:, 2:4], ins["L0_xattn_D_skip"]).then_inc(S["ssm_in"], 16)
            nb = [0]

            def loadB(dst, src):
                nb[0] += 16
                act.dma_start(dst, src).then_inc(S["wB_in"], 16)
            loadB(wv0[:, 0, :], ins["L0_xattn_Wv"][0:P, :])
            loadB(wv0[0:CD - P, 1, :], ins["L0_xattn_Wv"][P:CD, :])
            loadB(film[:, 0], ins["L0_xattn_W_film_in"].rearrange("(c p) n -> p c n", p=P))
            loadB(film[:, 1], ins["L0_xattn_W_film_out"].rearrange("(c p) n -> p c n", p=P))
            loadB(w1_0, ins["L0_xattn_W1"].rearrange("(c p) n -> p c n", p=P))
            loadB(w2_0, ins["L0_xattn_W2"].rearrange("(c p) n -> p c n", p=P))
            loadB(dft[:], ins["dft"].rearrange("p (a b c) -> p a b c", a=2, b=2))
            loadB(idft[:], ins["idft"].rearrange("p (a b) -> p a b", a=2))
            loadB(kdft[:], ins["kdft"].rearrange("p (a b) -> p a b", a=2))
            for i, n in enumerate(["L0_xattn_g_norm_in", "L0_xattn_b_norm_in", "L0_xattn_g_ffn", "L0_xattn_b_ffn",
                                   "L0_xattn_g_norm_out", "L0_xattn_b_norm_out", "L1_ffn_gamma", "L1_ffn_beta"]):
                loadB(gains[:, i, :], ins[n].partition_broadcast(P))
            loadB(gate[:], ins["L0_xattn_mod_gate"].partition_broadcast(P))
            loadB(cols[:, 0, :], ins["L0_xattn_b1"])
            loadB(cols[:, 1, :], ins["L1_ffn_b1"])
            for a, n in ((0, "L0_xattn_b_film_in"), (512, "L0_xattn_b_film_out"), (1024, "L0_xattn_b2"),
                         (1280, "L1_attn_bo"), (1536, "L1_ffn_b2")):
                w = 512 if a < 1024 else D
                loadB(rows[:, a:a + w], ins[n].rearrange("(a n) -> a n", a=1))
            assert nb[0] == WB, nb[0]
            act.wait_ge(S["angles"], 1)
            nc.scalar.activation(tm[4], tm[2], ACT.Sin, scale=0.5)
            nc.scalar.activation(tm[5], tm[3], ACT.Sin).then_inc(S["sines"], 1)
            for n in ("scores_sb", "meanT", "cx_out"):
                act.nop().then_inc(S[n], 1)

            def xaT_out(t):
                act.wait_ge(S["xa_tp"], t + 1)
                cp(xaT.rearrange("p a b -> p (a b)"), PS[:, 6, 0:D]).then_inc(S["xaT"], 1)

            def q_out(t):
                act.wait_ge(S["q_psum"], t + 1)
                for h in range(XH):
                    rs = slice(h * XD, (h + 1) * XD)
                    i_ = cp(qsplit[rs, h, :], PS[rs, 7, 0:P], 1.0 / float(np.sqrt(XD)))
                i_.then_inc(S["qsplit"], 1)

            def qctx_out(t, first=False):
                act.wait_ge(S["qctx_psum"], t + 1)
                if not first:
                    act.wait_ge(S["scores_psum"], t * 4)
                cp(qctx[:, 0].rearrange("p b h i -> p h b i"), PS[:, 6, :].rearrange("p (h b i) -> p h b i", h=XH, b=2))
                cp(qctx[0:CD - P, 1].rearrange("p b h i -> p h b i"),
                   PS[0:CD - P, 7, :].rearrange("p (h b i) -> p h b i", h=XH, b=2)).then_inc(S["qctx"], 1)

            def copy(t, r):
                act.wait_ge(S["probs"], t * 4 + r + 1)
                act.wait_ge(S["scores_psum"], t * 4 + r + 1)
                cp(scores[r % 2], bank(PS[:, 0:4, :], J)).then_inc(S["scores_sb"], 1)

            def exps(t, r):
                q = r % 2
                act.wait_ge(S["topk"], t * 4 + r + 1)
                nc.scalar.activation(topx[:, q, :], tops[:, q, :], ACT.Exp, bias=rowst[:, q, 0:1],
                                     accum_out=rowst[:, q, 1:2]).then_inc(S["zsum"], 1)
                nc.scalar.activation(scores[q], scores[q], ACT.Exp, bias=rowst[:, q, 0:1])
                nc.scalar.activation(rest[q], rest[q], ACT.Exp, bias=rowst[:, q, 0:1]).then_inc(S["exps"], 1)

            def mean_out(t, b):
                act.wait_ge(S["meanT_psum"], t * 2 + b + 3)
                cp(meanT[:, 0:8, :].rearrange("p a b -> p (a b)"), PS[:, 4, :])
                cp(meanT[:, 8:12, :].rearrange("p a b -> p (a b)"), PS[:, 5, 0:4 * T])
                cp(meanT[0:JL, 12, :], PS[0:JL, 5, 4 * T:5 * T]).then_inc(S["meanT"], 1)

            def cx_out(t, b):
                act.wait_ge(S["cx_psum"], t * 2 + b + 1)
                nc.scalar.activation(spare(), ones[:, 0:1], ACT.Copy)
                cp(CX[:, 0, bass.ds(t * P + b * T, T)], PS[:, 5, 320:320 + T])
                cp(CX[0:CD - P, 1, bass.ds(t * P + b * T, T)], PS[0:CD - P, 5, 384:384 + T]).then_inc(S["cx_out"], 1)

            def tile(t, first=False, last=False):
                exps(t, 0)
                if not first:
                    mean_out(t - 1, 1)
                if not last:
                    xaT_out(t + 1)
                copy(t, 2)
                exps(t, 1)
                if not first:
                    cx_out(t - 1, 1)
                if not last:
                    q_out(t + 1)
                copy(t, 3)
                if not last:
                    qctx_out(t + 1)
                exps(t, 2)
                mean_out(t, 0)
                if not last:
                    copy(t + 1, 0)
                exps(t, 3)
                cx_out(t, 0)
                if not last:
                    copy(t + 1, 1)

            xaT_out(0)
            q_out(0)
            qctx_out(0, first=True)
            copy(0, 0)
            copy(0, 1)
            tile(0, first=True)
            with act.Fori(1, TILES - 1) as t:
                tile(t)
            tile(TILES - 1, last=True)
            mean_out(TILES - 1, 1)
            cx_out(TILES - 1, 1)
            act.drain().then_inc(S["A_done"], 1)
            act_rest(act, cp)

        @block.vector
        def _(dve):
            v = nc.vector

            own = Own(dve, S["dve_setup"])
            dve.wait_ge(S["mask_in"], 48)
            own.step(v.tensor_scalar(maskrow, masku8, -1.0, BIG, ALU.add, ALU.mult))
            v.nop().then_inc(S["maskbias"], 1)
            own.step(v.tensor_reduce(small[0:B, 8:9], maskrow, AXX, ALU.max))
            own.step(v.tensor_scalar(small[0:B, 9:10], small[0:B, 8:9], -1.0, None, ALU.is_ge))
            dve.wait_ge(S["wA_in"], 64)
            own.step(v.tensor_scalar(small[0:B, 16:16 + B], ident[0:B, 0:B], small[0:B, 9:10], None, ALU.mult))
            v.nop().then_inc(S["valid_diag"], 1)
            dve.wait_ge(S["valid_psum"], 1)
            own.step(v.tensor_copy(valid[:], PS[:, 0, 0:B]))
            own.step(v.reciprocal(small[:, 32:32 + B], valid[:]))
            own.step(v.scalar_tensor_tensor(small[:, 48:48 + B], valid[:], 1.0 / XH, small[:, 32:32 + B], ALU.mult, ALU.mult))
            own.step(v.tensor_tensor(qmask[:], textu8, small[:, 48:48 + B], ALU.mult))

            own.step(v.memset(mix[:], 0.0))
            v.nop().then_inc(S["mix_zero"], 1)
            dve.wait_ge(S["x_in"], 16)
            for i in range(TILES):
                own.step(v.bn_stats(bnA[:, 0:6], X[:, i, :]))
                own.step(v.bn_aggr(bnA[:, 6:8], bnA[:, 0:6]))
                own.step(v.tensor_copy(lnA[:, 0:2, i], bnA[:, 6:8]))
            v.tensor_scalar(lnA[:, 1, :], lnA[:, 1, :], EPS, None, ALU.add).then_inc(S["A_var"], 1)

            dve.wait_ge(S["ssm_in"], 96)
            MAGIC = 12582912.0

            def expm1(o, x, k, q, s, si):
                own.step(v.tensor_scalar(k, x, 1.4426950408889634, MAGIC, ALU.mult, ALU.add))
                own.step(v.tensor_scalar(k, k, -MAGIC, None, ALU.add))
                own.step(v.scalar_tensor_tensor(o, k, -0.693359375, x, ALU.mult, ALU.add))
                own.step(v.scalar_tensor_tensor(o, k, 2.12194440e-4, o, ALU.mult, ALU.add))
                own.step(v.tensor_scalar(q, o, 1.0 / 5040, None, ALU.mult))
                for c in (720, 120, 24, 6, 2, 1):
                    own.step(v.scalar_tensor_tensor(q, q, 1.0 / c, o, ALU.add, ALU.mult))
                own.step(v.tensor_scalar(si, k, 127.0, 8388608.0, ALU.add, ALU.mult))
                own.step(v.tensor_tensor(q, q, s, ALU.mult))
                own.step(v.scalar_tensor_tensor(o, s, -1.0, q, ALU.add, ALU.add))

            e = small
            expm1(e[:, 64:66], ldt, e[:, 66:68], e[:, 68:70], e[:, 70:72], e[:, 70:72].bitcast(I32))
            own.step(v.tensor_scalar(e[:, 64:66], e[:, 64:66], 1.0, None, ALU.add))
            for c in range(2):
                cs = slice(c * NST, (c + 1) * NST)
                own.step(v.tensor_scalar(tm[0][:, cs], ssm[:, 0, cs], e[:, 64 + c:65 + c], None, ALU.mult))
                own.step(v.tensor_scalar(tm[1][:, cs], ssm[:, 1, cs], e[:, 64 + c:65 + c], None, ALU.mult))
            twopi = 2 * np.pi
            c1 = 6.28125
            c2 = float(np.float32(np.round((twopi - c1) * 2 ** 22) / 2 ** 22))
            c3 = float(twopi - c1 - c2)
            own.step(v.tensor_scalar(tm[3], tm[1], 1 / twopi, MAGIC, ALU.mult, ALU.add))
            own.step(v.tensor_scalar(tm[3], tm[3], -MAGIC, None, ALU.add))
            own.step(v.scalar_tensor_tensor(tm[2], tm[3], -c1, tm[1], ALU.mult, ALU.add))
            own.step(v.scalar_tensor_tensor(tm[2], tm[3], -c2, tm[2], ALU.mult, ALU.add))
            own.step(v.scalar_tensor_tensor(tm[2], tm[3], -c3, tm[2], ALU.mult, ALU.add))
            own.step(v.scalar_tensor_tensor(tm[3], tm[2], -1.0, tm[2], ALU.mult, ALU.max))
            own.step(v.tensor_scalar(tm[3], tm[3], -0.5, float(np.pi / 2), ALU.mult, ALU.add))
            v.nop().then_inc(S["angles"], 1)
            expm1(tm[1], tm[0], tm[6], tm[7], tm[8], tm[8].bitcast(I32))
            dve.wait_ge(S["sines"], 1)
            own.step(v.scalar_tensor_tensor(tm[6], tm[4], 2.0, tm[5], ALU.mult, ALU.mult))
            own.step(v.scalar_tensor_tensor(tm[7], tm[4], -2.0, tm[4], ALU.mult, ALU.mult))
            own.step(v.scalar_tensor_tensor(wpow[:, 0, 1, :], tm[7], 1.0, tm[1], ALU.add, ALU.mult))
            own.step(v.tensor_tensor(tm[0], wpow[:, 0, 1, :], tm[7], ALU.add))
            own.step(v.scalar_tensor_tensor(wpow[:, 1, 1, :], tm[1], 1.0, tm[6], ALU.add, ALU.mult))
            own.step(v.tensor_scalar(wpow[:, 0, 1, :], tm[0], 1.0, None, ALU.add))
            own.step(v.memset(wpow[:, 0, 0, :], 1.0))
            own.step(v.memset(wpow[:, 1, 0, :], 0.0))
            own.step(v.memset(wbig[:, 0, 0, :], 1.0))
            own.step(v.memset(wbig[:, 1, 0, :], 0.0))
            are, aim, cre, cim = (ssm[:, i, :] for i in range(4))
            wi = wpow[:, 1, 1, :]
            own.step(v.tensor_tensor(tm[1], are, are, ALU.mult))
            own.step(v.tensor_tensor(tm[2], aim, aim, ALU.mult))
            own.step(v.tensor_tensor(tm[1], tm[1], tm[2], ALU.add))
            own.step(v.reciprocal(tm[2], tm[1]))
            own.step(v.tensor_tensor(tm[3], tm[0], are, ALU.mult))
            own.step(v.tensor_tensor(tm[4], wi, aim, ALU.mult))
            own.step(v.tensor_tensor(tm[3], tm[3], tm[4], ALU.add))
            own.step(v.scalar_tensor_tensor(tm[3], tm[3], 2.0, tm[2], ALU.mult, ALU.mult))
            own.step(v.tensor_tensor(tm[4], wi, are, ALU.mult))
            own.step(v.tensor_tensor(tm[5], tm[0], aim, ALU.mult))
            own.step(v.tensor_tensor(tm[4], tm[4], tm[5], ALU.subtract))
            own.step(v.scalar_tensor_tensor(tm[4], tm[4], 2.0, tm[2], ALU.mult, ALU.mult))
            own.step(v.tensor_tensor(tm[5], cre, tm[3], ALU.mult))
            own.step(v.tensor_tensor(tm[6], cim, tm[4], ALU.mult))
            own.step(v.tensor_tensor(tm[0], tm[5], tm[6], ALU.subtract))
            own.step(v.tensor_tensor(tm[5], cre, tm[4], ALU.mult))
            own.step(v.tensor_tensor(tm[6], cim, tm[3], ALU.mult))
            own.step(v.tensor_tensor(tm[1], tm[5], tm[6], ALU.add))
            v.nop().then_inc(S["ssm_base"], 1)

            dve.wait_ge(S["A_rstd"], 1)

            def normed(t):
                v.tensor_scalar(xa, X[:, bass.ds(t, 1), :].rearrange("p a b -> p (a b)"), lnA[:, 0, bass.ds(t, 1)],
                                lnA[:, 2, bass.ds(t, 1)], ALU.subtract, ALU.mult).then_inc(S["xa"], 1)

            def row_scale(own, t, r):
                q, b, hp = r % 2, r // 2, r % 2
                dve.wait_ge(S["zsum"], t * 4 + r + 1)
                own.step(v.reciprocal(rowst[:, q, 2:3], rowst[:, q, 1:2]))
                dve.wait_ge(S["meanT_psum"], t * 2 + b + 1)
                v.tensor_scalar(rowdiag[b][hp], twice_eye[:], rowst[:, q, 2:3], qmask[:, bass.ds(t * 2 + b, 1)],
                                ALU.mult, ALU.mult).then_inc(S["rowdiag"], 1)

            def topk(own, t, r, before=None):
                q = r % 2
                dve.wait_ge(S["probs"], t * 4 + r + 1)
                dve.wait_ge(S["scores_sb"], t * 4 + r + 2)
                nc.vector.memset(spare(), 0.0)
                src = scores[q]
                for i in range(KTOP // 8):
                    t8 = tops[:, q, i * 8:i * 8 + 8]
                    own.need(own.mark(v.max(t8, src)))
                    if i == 0:
                        v.tensor_scalar(rowst[:, q, 0:1], t8[:, 0:1], -1.0, None, ALU.mult)
                    last = v.match_replace(rest[q], t8, src, LOW)
                    if i < KTOP // 8 - 1:
                        own.need(own.mark(last))
                    src = rest[q]
                    if i == 1 and before is not None:
                        row_scale(own, *before)
                last.then_inc(S["topk"], 1)

            def lags(t, c):
                dve.wait_ge(S["kprod"], t * 2 + c + 1)
                nc.vector.memset(spare(), 0.0)
                v.tensor_reduce(kern[:, c, bass.ds(t * 8, 8)], prod, AXX, ALU.add).then_inc(S["kpart"], 1)

            def tile(t, first=False, last=False):
                own = Own(dve, S["dve_turn"])
                topk(own, t, 0, None if first else (t - 1, 3))
                if not last:
                    dve.wait_ge(S["xa_tp"], t + 1)
                    normed(t + 1)
                topk(own, t, 1, (t, 0))
                topk(own, t, 2, (t, 1))
                lags(t, 0)
                topk(own, t, 3, (t, 2))
                lags(t, 1)
                own.end()

            normed(0)
            tile(0, first=True)
            with dve.Fori(1, TILES - 1) as t:
                tile(t)
            tile(TILES - 1, last=True)
            own = Own(dve, S["dve_turn"])
            row_scale(own, TILES - 1, 3)
            own.end()
            own = Own(dve, S["dve_setup2"])
            dve.wait_ge(S["kpart"], 2 * TILES + 1)
            for c in range(2):
                own.step(v.tensor_tensor(kern[:, c, 0:1], kern[:, c, 0:1], small[:, 2 + c:3 + c], ALU.add))
            v.nop().then_inc(S["kern"], 1)
            dve.wait_ge(S["kern_tp"], 1)
            v.tensor_copy(kernT[0:T, :], PS[0:T, 0, 0:D]).then_inc(S["kernT"], 1)
            dve.wait_ge(S["kfreq_psum"], 1)
            v.tensor_copy(kfreq[:], PS[:, 1, :]).then_inc(S["kfreq"], 1)
            dve.drain().then_inc(S["A_done"], 1)
            dve_rest(dve, v)

        @block.gpsimd
        def _(pool):
            g = nc.gpsimd
            own = Own(pool, S["pool_setup"])
            own.step(g.memset(ones[:], 1.0))
            own.step(g.memset(mhalf[:], -0.5))
            own.step(g.memset(qsplit, 0.0))
            own.step(g.memset(qctx[CD - P:CD - P + 1, 1], 1.0))
            g.nop().then_inc(S["ones"], 1)
            g.nop().then_inc(S["probs"], 2)
            g.nop().then_inc(S["kpart"], 1)

            def cmul(o, x, y, tmp):
                own.step(g.tensor_tensor(tmp[0], x[0], y[0], ALU.mult))
                own.step(g.tensor_tensor(tmp[1], x[1], y[1], ALU.mult))
                own.step(g.tensor_tensor(tmp[2], x[0], y[1], ALU.mult))
                own.step(g.tensor_tensor(tmp[3], x[1], y[0], ALU.mult))
                own.step(g.tensor_tensor(o[0], tmp[0], tmp[1], ALU.subtract))
                own.step(g.tensor_tensor(o[1], tmp[2], tmp[3], ALU.add))

            def wide(pw, a, n):
                return pw[:, 0, a:a + n, :], pw[:, 1, a:a + n, :]

            def powers():
                pool.wait_ge(S["ssm_base"], 1)
                tmp = [coef[:, i // 4, (i % 4) * 2:(i % 4) * 2 + 2, :] for i in range(8)]
                for pw in (wpow, wbig):
                    if pw is wbig:
                        cmul(wide(wbig, 1, 1), wide(wpow, 4, 1), wide(wpow, 4, 1), [x[:, 0:1] for x in tmp])
                    cmul(wide(pw, 2, 1), wide(pw, 1, 1), wide(pw, 1, 1), [x[:, 0:1] for x in tmp])
                    cmul(wide(pw, 3, 1), wide(pw, 2, 1), wide(pw, 1, 1), [x[:, 0:1] for x in tmp])
                    cmul(wide(pw, 4, 1), wide(pw, 2, 1), wide(pw, 2, 1), [x[:, 0:1] for x in tmp])
                    f4 = [pw[:, i, 4:5, :].to_broadcast([P, 2, P]) for i in range(2)]
                    cmul(wide(pw, 5, 2), wide(pw, 1, 2), f4, tmp)
                    cmul(wide(pw, 7, 1), wide(pw, 3, 1), wide(pw, 4, 1), [x[:, 0:1] for x in tmp])
                for b in range(8):
                    x = [wpow[:, i, b, :] for i in range(2)]
                    cmul([coef[:, i, b, :] for i in range(2)], x, [tm[0], tm[1]], [tm[3], tm[4], tm[5], tm[6]])

            pool.wait_ge(S["A_var"], 1)
            g.tensor_tensor(lnA[:, 2, :], lnA[:, 1, :], mhalf[:].to_broadcast([P, TILES]), ALU.pow).then_inc(S["A_rstd"], 1)
            powers()
            with pool.Fori(0, TILES) as t:
                own = Own(pool, S["pool_A"])

                def prob(r):
                    pool.wait_ge(S["meanT_psum"], t * 2 + r // 2 + 2)
                    pool.wait_ge(S["exps"], t * 4 + r + 1)
                    g.tensor_tensor(probs[r % 2], scores[r % 2], rest[r % 2], ALU.subtract).then_inc(S["probs"], 1)

                def lag_terms(c):
                    cs = slice(c * NST, (c + 1) * NST)
                    pool.wait_ge(S["kpart"], t * 2 + c + 1)
                    nc.gpsimd.tensor_tensor(spare(), mhalf[:], mhalf[:], ALU.add)
                    x = [wbig[:, i, bass.ds(t, 1), cs].to_broadcast([P, 8, NST]) for i in range(2)]
                    g.tensor_tensor(prod, coef[:, 0, :, cs], x[0], ALU.mult)
                    own.step(g.tensor_tensor(prod2, coef[:, 1, :, cs], x[1], ALU.mult))
                    g.tensor_tensor(prod, prod, prod2, ALU.subtract).then_inc(S["kprod"], 1)

                prob(0)
                prob(1)
                lag_terms(0)
                prob(2)
                lag_terms(1)
                prob(3)
                own.end()
            pool.drain().then_inc(S["A_done"], 1)
            for phase, lns in (("B", 4), ("C", 1), ("D", 1), ("E", 1), ("F", 1), ("G", 2)):
                if phase not in stages:
                    continue
                pool.wait_ge(S[chr(ord(phase) - 1) + "_done"], 4)
                if phase > "B":
                    for s_ in S.of_phase_before(phase):
                        pool.sem_clear(s_)
                with pool.Fori(0, TILES // U) as j:
                    for i in range(lns):
                        for u in range(U):
                            pool.wait_ge(S[f"{phase}{i}_var"], j * U + u + 1)
                            b_ = bn[0 if phase == "E" else u]
                            g.tensor_tensor(b_[:, 9:10], b_[:, 8:9], mhalf[:], ALU.pow
                                            ).then_inc(S[f"{phase}{i}_rstd"], 1)
                pool.drain().then_inc(S[phase + "_done"], 1)
            g.drain().then_inc(S["all_done"], 1)


_PLAIN = ["x", "ctx", "L0_xattn_Wq", "L0_xattn_Wv", "L0_xattn_W_film_in", "L0_xattn_b_film_in", "L0_xattn_W_film_out",
          "L0_xattn_b_film_out", "L0_xattn_g_norm_in", "L0_xattn_b_norm_in", "L0_xattn_g_norm_out",
          "L0_xattn_b_norm_out", "L0_xattn_g_ffn", "L0_xattn_b_ffn", "L0_xattn_W1", "L0_xattn_b1", "L0_xattn_W2",
          "L0_xattn_b2", "L0_xattn_log_dt", "L0_xattn_A_re", "L0_xattn_A_im", "L0_xattn_C_re", "L0_xattn_C_im",
          "L0_xattn_D_skip", "L0_attn_wq", "L0_attn_w_down", "L0_attn_wk_up", "L0_attn_wv_up", "L0_attn_wo",
          "L0_ffn_correction_bias", "L0_ffn_w_gate", "L0_ffn_w_up", "L0_ffn_w_down", "L0_ffn_sw_gate",
          "L0_ffn_sw_up", "L0_ffn_sw_down", "L1_xattn_Wq", "L1_xattn_Wk", "L1_xattn_Wv", "L1_xattn_Wo",
          "L1_attn_Wq", "L1_attn_Wk", "L1_attn_Wv", "L1_attn_pre_proj", "L1_attn_post_proj", "L1_attn_mem_v",
          "L1_attn_Wo", "L1_attn_bo", "L1_ffn_w1", "L1_ffn_b1", "L1_ffn_w2", "L1_ffn_b2", "L1_ffn_gamma",
          "L1_ffn_beta"]
STAGES = "ABCDEFG"


def kernel(**inputs):
    import numpy as _np
    import concourse.bacc as _bacc
    from concourse import mybir as _mybir
    from concourse.bass_utils import run_bass_kernel_spmd as _run

    a = {n: _np.asarray(v) for n, v in inputs.items()}
    a["x"] = a["x"].reshape(B * T, D)
    a["ctx"] = a["ctx_768"]
    a["ctxT"] = a["ctx_768"].transpose(0, 2, 1)
    a["ctx_mask"] = a["mask_BxS2_bf1"]
    a["text_maskT"] = a["mask_BxS_bf1"].T
    a["L0_xattn_WkT"] = a["L0_xattn_Wk"].T
    a["L0_xattn_mod_gate"] = a["L0_xattn_mod_gate"].reshape(1)
    a["router_T"] = a["L0_ffn_router_weight"].T
    for n in ("L1_ffn_w1", "L1_ffn_b1", "L1_ffn_w2", "L1_ffn_b2"):
        a[n] = a[n][0]
    for n in ("L0_xattn_log_dt", "L0_xattn_D_skip", "L0_xattn_b1", "L1_ffn_b1"):
        a[n] = a[n].reshape(-1, P).T
    mk = a["L1_attn_mem_k"].reshape(8, 2, MEM, AD)
    a["mem_kT"] = mk.transpose(1, 3, 0, 2).reshape(P, 8, MEM)
    a["L1_attn_mem_v"] = a["L1_attn_mem_v"].transpose(1, 0, 2).reshape(MEM, 16 * AD)
    names = _PLAIN + ["ctxT", "ctx_mask", "text_maskT", "L0_xattn_WkT", "L0_xattn_mod_gate", "router_T", "mem_kT"]
    table = constants()
    a.update(table)
    nc = _bacc.Bacc("TRN2", target_bir_lowering=False, num_devices=1)
    arrays, ins = {}, {}
    for n in names + list(table):
        v = _np.ascontiguousarray(a[n])
        arrays[f"in_{n}"] = v
        ins[n] = nc.dram_tensor(f"in_{n}", v.shape, _mybir.dt.from_np(v.dtype), kind="ExternalInput").ap()
    out = nc.dram_tensor("out", (B * T, D), _mybir.dt.float32, kind="ExternalOutput").ap()
    perceiver(nc, ins, out, STAGES)
    r = _run(nc, [arrays], core_ids=[0])
    return r.results[0]["out"].reshape(B, T, D)
```

```python
from contextlib import ExitStack

import numpy as np

import concourse.bass as bass
from concourse import mybir

F32 = mybir.dt.float32
BF16 = mybir.dt.bfloat16
I32 = mybir.dt.int32
U8 = mybir.dt.uint8
ALU = mybir.AluOpType
ACT = mybir.ActivationFunctionType
AXX = mybir.AxisListType.X

B, T, D = 16, 64, 256
J, CD = 1601, 192
P = 128
TILES = B * T // P
NJ = (J + P - 1) // P
JL = J - (NJ - 1) * P
EPS = 1e-5
BIG = 1.0e30
LOW = -3.0e38

XH, XD, KTOP = 4, 32, 32
NST = 64
HID = 1024
H16 = 16
NE, EI = 8, 128
AD, MEM, KEYS, KEEP = 64, 16, 80, 64


def constants():
    c = {}
    f = np.float32
    c["ident"] = np.eye(P, dtype=f)
    c["twice_eye"] = np.concatenate([np.eye(T), np.eye(T)]).astype(f)
    n = 2 * T
    t = np.arange(T)[:, None]
    k = np.arange(T)[None, :]
    cos, sin = np.cos(2 * np.pi * k * t / n), np.sin(2 * np.pi * k * t / n)
    nyq = np.cos(np.pi * t)
    fa = np.concatenate([cos, nyq, -sin[:, 1:]], 1)
    zero = np.zeros((T, 1))
    fb = np.concatenate([zero, -sin[:, 1:], zero, cos[:, 1:]], 1)
    kr = np.concatenate([cos, nyq, cos[:, 1:]], 1)
    ki = np.concatenate([zero, sin[:, 1:], zero, -sin[:, 1:]], 1)
    inv = np.concatenate([cos[:, :1], 2 * cos[:, 1:], nyq, -2 * sin[:, 1:]], 1).T / n
    dft = np.zeros((P, 2, 2, P))
    idft = np.zeros((P, 2, P))
    for b in range(2):
        dft[b * T:(b + 1) * T, b, 0] = fa
        dft[b * T:(b + 1) * T, b, 1] = fb
        idft[:, b, b * T:(b + 1) * T] = inv
    c["dft"] = dft.reshape(P, 4 * P).astype(f)
    c["idft"] = idft.reshape(P, 2 * P).astype(f)
    kd = np.zeros((P, 2, P))
    kd[:T, 0], kd[:T, 1] = kr, ki
    c["kdft"] = kd.reshape(P, 2 * P).astype(f)
    hd = D // H16
    inv_f = (1.0 / 10000.0 ** (np.arange(0, hd, 2, dtype=f) / f(hd))).astype(f)
    ang = np.outer(np.arange(T, dtype=f), inv_f).astype(f)
    co, si = np.cos(ang), np.sin(ang)
    cc = np.tile(np.repeat(co, 2, 1), (2, H16))
    ss = np.tile(np.stack([-si, si], -1).reshape(T, hd), (2, H16))
    q = 1.0 / np.sqrt(hd)
    c["rope"] = np.concatenate([cc * q, cc, ss * q, ss], 1).astype(f)
    c["head_of_row"] = (np.arange(P)[:, None] // hd == np.arange(8)[None, :]).astype(f)
    i8 = np.arange(P)[:, None, None] // H16
    ib = np.arange(8)[None, :, None]
    j = np.arange(KEYS)[None, None, :]
    c["causal"] = np.where((j < T) & (j > ib * 8 + i8), -BIG, 0.0).reshape(P, 8 * KEYS).astype(f)
    c["earlier"] = np.tile((np.arange(8)[None, :] < np.arange(8)[:, None]).reshape(1, 64), (P, 1)).astype(f)
    pick = np.zeros((P, NE, P))
    for e in range(NE):
        pick[e, e] = 1
    c["pick"] = pick.reshape(P, NE * P).astype(f)
    c["fold"] = np.concatenate([np.eye(33), np.eye(33)]).astype(f)
    c["pair_diag"] = np.kron(np.eye(2), np.ones((T, hd))).astype(f)
    return c


WB = 16 * 25
WD = 16 * 12
WE = 16 * 8
WF = 16 * 29


class Events(dict):

    def __init__(self, nc, ctx):
        super().__init__()
        self.nc, self.ctx = nc, ctx
        self.sets, self.taken = ([], []), {}

    def __missing__(self, name):
        phase = name[0] if name[1:2] == "_" and not name.endswith("_done") else ""
        if phase and phase in "BCDEFG":
            slots, n = self.sets[ord(phase) % 2], self.taken.get(phase, 0)
            self.taken[phase] = n + 1
            if n == len(slots):
                slots.append(self.ctx.enter_context(self.nc.semaphore(f"phase_{ord(phase) % 2}_{n}")))
            self[name] = slots[n]
        else:
            self[name] = self.ctx.enter_context(self.nc.semaphore(name))
        return self[name]

    def of_phase_before(self, phase):
        return self.sets[(ord(phase) - 1) % 2]


class Arena:

    def __init__(self, whole, at=0):
        self.whole, self.at = whole, at

    def take(self, *shape):
        n = int(np.prod(shape))
        v = self.whole[:, self.at:self.at + n]
        self.at += n
        assert self.at <= self.whole.shape[1], (self.at, self.whole.shape)
        if len(shape) == 2:
            v = v.rearrange("p (a b) -> p a b", a=shape[0])
        if len(shape) == 3:
            v = v.rearrange("p (a b c) -> p a b c", a=shape[0], b=shape[1])
        if len(shape) == 4:
            v = v.rearrange("p (a b c d) -> p a b c d", a=shape[0], b=shape[1], c=shape[2])
        return v


def bank(v, n):
    return v.rearrange("p a b -> p (a b)")[:, 0:n]


class Own:

    def __init__(self, eng, sem):
        self.eng, self.sem, self.n = eng, sem, 0

    def mark(self, ins):
        self.n += 1
        ins.then_inc(self.sem, 1)
        return self.n

    def need(self, n):
        self.eng.wait_ge(self.sem, n)

    def step(self, ins):
        self.need(self.mark(ins))

    def end(self):
        self.need(self.n)
        self.eng.sem_clear(self.sem)


def perceiver(nc, ins, out, stages="ABCDEFG"):
    with ExitStack() as ctx:
        def sb(name, shape, dt=F32):
            return ctx.enter_context(nc.sbuf_tensor(name, shape, dt))

        S = Events(nc, ctx)
        U = 2

        X = sb("X", [P, TILES, D])
        CX = sb("CX", [P, 2, TILES * P])
        ident = sb("ident", [P, P])
        twice_eye = sb("twice_eye", [P, T])
        dft = sb("dft", [P, 2, 2, P])
        idft = sb("idft", [P, 2, P])
        kdft = sb("kdft", [P, 2, P])
        rope = sb("rope", [P, 2, 2 * D])
        head_of_row = sb("head_of_row", [P, 8])
        causal = sb("causal", [P, 8 * KEYS])
        earlier = sb("earlier", [P, 8, 8])
        pair_diag = sb("pair_diag", [P, 32])
        mhalf = sb("mhalf", [P, 1])
        mix = sb("mix", [P, 2, P])
        kfreq = sb("kfreq", [P, 2 * D])
        gains = sb("gains", [P, 8, D])
        gate = sb("gate", [P, 1])
        ones = sb("ones", [P, P])
        rows = sb("rows", [1, 2 * 512 + 3 * 256])
        cols = sb("cols", [P, 2, 8])
        valid = sb("valid", [P, B])
        qmask = sb("qmask", [P, B])
        carrier = sb("carrier", [P, 88])
        carried = []

        def spare():
            carried.append(1)
            return carrier[:, len(carried) - 1:len(carried)]

        small = sb("small", [P, 256])
        R1 = Arena(sb("region1", [P, 7104]))
        R2 = Arena(sb("region2", [P, 8800]))
        arena = sb("arena", [P, 25060])
        PS = ctx.enter_context(nc.psum_tensor("PS", [P, 8, 512], F32))
        maskbias_dram = nc.dram_tensor("maskbias", (B, J), F32, kind="Internal").ap()
        maskbias16_dram = nc.dram_tensor("maskbias16", (B, 8 * J), BF16, kind="Internal").ap()

        wq0 = R1.take(2, P)
        wk0t = R1.take(CD)
        wv0 = R1.take(2, D)
        film = R1.take(2, 2, 512)
        w1_0 = R1.take(2, HID)
        w2_0 = R1.take(8, D)
        R1b = Arena(R1.whole)
        wq1 = R1b.take(2, D)
        wk1 = R1b.take(2, D)
        wv1 = R1b.take(2, D)
        wo1 = R1b.take(2, D)
        w1_1 = R1b.take(2, HID)
        w2_1 = R1b.take(8, D)
        aq = R2.take(2, D)
        adown = R2.take(2, P)
        akv = R2.take(2 * D)
        ao = R2.take(2, D)
        router = R2.take(2, NE)
        wgate = R2.take(2, NE + 1, EI)
        wup = R2.take(2, NE + 1, EI)
        wdown = R2.take(NE + 1, D)
        R2b = Arena(R2.whole)
        tq = R2b.take(2, 1024)
        tk = R2b.take(2, 1024)
        tv = R2b.take(2, 1024)
        to = R2b.take(8, D)

        ar = Arena(arena)
        ctxT = [ar.take(2, J) for _ in range(2)]
        ctxN = [ar.take(NJ, CD) for _ in range(2)]
        scores = [ar.take(J) for _ in range(2)]
        rest = [ar.take(J) for _ in range(2)]
        probs = [ar.take(J) for _ in range(2)]
        qsplit = ar.take(XH, P)
        qctx = ar.take(2, 2, XH, T)
        meanT = ar.take(NJ, T)
        xa = ar.take(D)
        xaT = ar.take(2, P)
        bnA = ar.take(16)
        lnA = ar.take(3, TILES)
        tops = ar.take(2, KTOP)
        topx = small[:, 128:192].rearrange("p (a b) -> p a b", a=2)
        rowst = ar.take(2, 8)
        rowdiag = [[ar.take(T) for _ in range(2)] for _ in range(2)]
        kern = ar.take(2, T)
        kernT = ar.take(D)
        maskrow = probs[0][0:B, :]
        maskrow16 = scores[0].bitcast(BF16)[0:B, 0:J]
        masku8 = rest[0].bitcast(U8)[0:B, 0:J]
        textu8 = rest[1].bitcast(U8)[:, 0:B]
        kr = Arena(R2.whole)
        wpow = kr.take(2, 8, P)
        wbig = kr.take(2, 8, P)
        coef = kr.take(2, 8, P)
        ssm = kr.take(4, P)
        tm = [kr.take(P) for _ in range(10)]
        prod = kr.take(8, NST)
        prod2 = rope[:, 0, :].rearrange("p (a b) -> p a b", a=8)
        ldt = small[:, 0:2]

        def both(f):
            return [f() for _ in range(U)]

        ar = Arena(arena)
        xn = both(lambda: ar.take(D))
        xnT = both(lambda: ar.take(2, P))
        bn = both(lambda: ar.take(16))
        work = both(lambda: ar.take(D))
        top = ar.at
        ctT = both(lambda: ar.take(2, P))
        xf = both(lambda: ar.take(D))
        prd = both(lambda: ar.take(2, 2 * D))
        yfq = both(lambda: ar.take(2, D))
        hid = both(lambda: ar.take(8, P))
        ar = Arena(arena, top)
        latT = both(lambda: ar.take(P))
        lat2 = both(lambda: ar.take(2, 2, T))
        rot = both(lambda: ar.take(2 * D))
        rot2 = both(lambda: ar.take(2 * D))
        qz = both(lambda: ar.take(2, 8, P))
        kTs = both(lambda: ar.take(2, P))
        vz = both(lambda: ar.take(2, 8, 32))
        pr = both(lambda: ar.take(H16, T))
        prT = both(lambda: ar.take(8, P))
        st = both(lambda: ar.take(3, H16))
        oc = both(lambda: ar.take(H16, 16))
        ocT = both(lambda: ar.take(2, P))
        ar = Arena(arena, top)
        rt = both(lambda: ar.take(16, 8))
        cmp8 = both(lambda: ar.take(2, 8, 8))
        combT = both(lambda: ar.take(P))
        th = both(lambda: ar.take(4 * P))
        h9 = both(lambda: ar.take(NE + 1, P))
        pick = ar.take(NE, P)
        rbias = ar.take(8)

        ar = Arena(arena, top)
        fqz = both(lambda: ar.take(8, 2, T, 2))
        fk = both(lambda: ar.take(8, 2, KEYS))
        fv = both(lambda: ar.take(2, 16 * AD))
        foT = both(lambda: ar.take(8, P))
        fdT = [ar.take(T, H16) for _ in range(2 * U)]
        fd = [ar.take(8, KEYS) for _ in range(2 * U)]
        fm = [ar.take(8, KEYS) for _ in range(2 * U)]
        fst = [ar.take(32) for _ in range(2 * U)]
        f8 = [ar.take(2, 8) for _ in range(2 * U)]
        ar = Arena(arena, top)
        ghid = both(lambda: ar.take(8, P))
        ar = Arena(arena, top)
        ectx = [ar.take(2, J) for _ in range(2)]
        ehi = ar.take((3 * J + 1) // 2).bitcast(BF16)[:, 0:3 * J].rearrange("p (a b) -> p a b", a=3)
        cx16 = CX[:].rearrange("p a b -> p (a b)").bitcast(BF16)
        elo = [cx16[:, 0:J], cx16[:, J + 1:2 * J + 1],
               rope[:].rearrange("p a b -> p (a b)").bitcast(BF16)[:, 0:J]]
        KR = 100
        ekst = ar.take(8 * J // 2 + 1).bitcast(BF16)[:, 0:8 * J].rearrange("p (a b) -> p a b", a=8)
        eV = ar.take(NJ * 8 * 33).bitcast(BF16).rearrange("p (a b c) -> p a b c", a=NJ, b=8)
        eP = [ar.take(2 * 512) for _ in range(2)]
        l0_gains = gains[:, 0:6, :].rearrange("p a b -> p (a b)")
        ePh = [l0_gains[:, i * 512:(i + 1) * 512].bitcast(BF16) for i in range(2)]
        fold = R1b.take(33)[0:66, :]
        ePl = [v_.bitcast(BF16) for v_ in (l0_gains[:, 1024:1536], R1b.take(512))]
        eqhl = ar.take(2, 3 * P // 2)
        eqhi, eqlo = (eqhl[:, i, :].bitcast(BF16).rearrange("p (a b) -> p a b", a=3) for i in range(2))
        eqst = dft[:].rearrange("p a b c -> p (a b c)").bitcast(BF16).rearrange("p (a b) -> p a b", a=8)
        eqz = ar.take(H16 * T // 2).bitcast(BF16).rearrange("p (a b) -> p a b", a=H16)
        emax = ar.take(8 * KR // 2).bitcast(BF16).rearrange("p (a b) -> p a b", a=8)
        enm = ar.take(3, 8)
        ehalf = ar.take(8, 2)
        ehalf_of_row = ar.take(2)
        ident16 = ar.take(P // 2).bitcast(BF16)
        eo = ar.take(8, 32)
        eoT = ar.take(2, P)
        erz = ar.take(8)
        def flat(v):
            return v.rearrange("p a b -> p (a b)")

        def v_ln(dve, v, own, j, name, src, dst, ready=None):
            m = [0] * U
            for u in range(U):
                if ready is not None:
                    own.need(ready[u])
                m[u] = own.mark(v.bn_stats(bn[u][:, 0:6], src(u)))
            for u in range(U):
                own.need(m[u])
                m[u] = own.mark(v.bn_aggr(bn[u][:, 6:8], bn[u][:, 0:6]))
            for u in range(U):
                own.need(m[u])
                v.tensor_scalar(bn[u][:, 8:9], bn[u][:, 7:8], EPS, None, ALU.add).then_inc(S[name + "_var"], 1)
            for u in range(U):
                dve.wait_ge(S[name + "_rstd"], j * U + u + 1)
                m[u] = own.mark(v.tensor_scalar(dst(u), src(u), bn[u][:, 6:7], bn[u][:, 9:10], ALU.subtract, ALU.mult))
            return m

        def v_affine(v, own, m, x, i):
            for u in range(U):
                own.need(m[u])
                m[u] = own.mark(v.tensor_tensor(x(u), x(u), gains[:, i, :], ALU.mult))
            for u in range(U):
                own.need(m[u])
                m[u] = own.mark(v.tensor_tensor(x(u), x(u), gains[:, i + 1, :], ALU.add))
            return m

        def xtile(j, u):
            return X[:, bass.ds(j * U + u, 1), :].rearrange("p a b -> p (a b)")

        def cxtile(j, u, c):
            return CX[:, c, bass.ds(j * (U * P) + u * P, P)]

        def pe_turn(pe, u, bk, x):
            for c in range(2):
                i_ = pe.transpose(PS[:, 4 * u + bk, c * P:(c + 1) * P], x[:, c * P:(c + 1) * P], ident[:])
            return i_

        def pe_B(pe, mm, mm2):
            pe.wait_ge(S["kfreq"], 1)
            pe.wait_ge(S["A_done"], 4)
            pe.nop().then_inc(S["B_end"], 1)
            with pe.Fori(0, TILES // U) as j:
                for u in range(U):
                    pe.wait_ge(S["B_end"], j * U + 1)
                    for o in range(2):
                        os_ = slice(o * P, (o + 1) * P)
                        mm(PS[:, 4 * u, os_], wv0[:, 0, os_], cxtile(j, u, 0), start=True, stop=False)
                        i_ = mm(PS[:, 4 * u, os_], wv0[0:CD - P, 1, os_], cxtile(j, u, 1)[0:CD - P], start=False, stop=True)
                    i_.then_inc(S["B_ctT_psum"], 1)
                for u in range(U):
                    pe.wait_ge(S["B_ctT"], j * U + u + 1)
                    for f in range(2):
                        o = PS[:, 4 * u + 1 + f, :]
                        mm(o, ones[0:1, :], rows[:, f * 512:(f + 1) * 512], start=True, stop=False)
                        mm(o, ctT[u][:, 0, :], film[:, f, 0, :], start=False, stop=False)
                        i_ = mm(o, ctT[u][:, 1, :], film[:, f, 1, :], start=False, stop=True)
                    i_.then_inc(S["B_film_psum"], 1)
                for u in range(U):
                    pe.wait_ge(S["B_xf"], j * U + u + 1)
                    for b in range(2):
                        for f in range(2):
                            i_ = mm(PS[:, 4 * u + 3 * b, f * D:(f + 1) * D], dft[:, b, f, :], xf[u], start=True, stop=True)
                    i_.then_inc(S["B_dft_psum"], 1)
                for u in range(U):
                    pe.wait_ge(S["B_yf"], j * U + u + 1)
                    o = PS[:, 4 * u, 0:D]
                    mm(o, idft[:, 0, :], yfq[u][:, 0, :], start=True, stop=False)
                    mm(o, idft[:, 1, :], yfq[u][:, 1, :], start=False, stop=True).then_inc(S["B_y_psum"], 1)
                for u in range(U):
                    pe.wait_ge(S["B_h"], j * U + u + 1)
                    pe_turn(pe, u, 1, work[u]).then_inc(S["B_h_tp"], 1)
                for u in range(U):
                    pe.wait_ge(S["B_hT"], j * U + u + 1)
                    for c in range(8):
                        cs = slice(c * P, (c + 1) * P)
                        i_ = mm2(PS[:, 4 * u + 2 + c // 4, (c % 4) * P:(c % 4 + 1) * P],
                                 [w1_0[:, k, cs] for k in range(2)], [xnT[u][:, k, :] for k in range(2)])
                        if c % 4 == 3:
                            i_.then_inc(S["B_hid_psum"], 1)
                for u in range(U):
                    o = PS[:, 4 * u, 0:D]
                    mm(o, ones[0:1, :], rows[:, 1024:1024 + D], start=True, stop=False)
                    for c in range(8):
                        if c % 4 == 0:
                            pe.wait_ge(S["B_hid"], (j * U + u) * 2 + c // 4 + 1)
                        i_ = mm(o, hid[u][:, c, :], w2_0[:, c, :], start=False, stop=c == 7)
                    i_.then_inc(S["B_ffn_psum"], 1)

        def act_B(act, cp):
            act.wait_ge(S["A_done"], 4)
            with act.Fori(0, TILES // U) as j:
                for u in range(U):
                    act.wait_ge(S["B_ctT_psum"], j * U + u + 1)
                    cp(flat(ctT[u]), PS[:, 4 * u, 0:D]).then_inc(S["B_ctT"], 1)
                for u in range(U):
                    act.wait_ge(S["B_h_tp"], j * U + u + 1)
                    cp(flat(xnT[u]), PS[:, 4 * u + 1, 0:D]).then_inc(S["B_hT"], 1)
                for u in range(U):
                    for c in range(8):
                        if c % 4 == 0:
                            act.wait_ge(S["B_hid_psum"], (j * U + u) * 2 + c // 4 + 1)
                        i_ = nc.scalar.activation(hid[u][:, c, :], PS[:, 4 * u + 2 + c // 4, (c % 4) * P:(c % 4 + 1) * P],
                                                  ACT.Gelu, bias=cols[:, 0, c:c + 1])
                        if c % 4 == 3:
                            i_.then_inc(S["B_hid"], 1)

        def dve_B(dve, v):
            dve.wait_ge(S["A_done"], 4)
            with dve.Fori(0, TILES // U) as j:
                own = Own(dve, S["dve_turn"])
                m = v_ln(dve, v, own, j, "B0", lambda u: xtile(j, u), lambda u: xn[u])
                m = v_ln(dve, v, own, j, "B1", lambda u: xn[u], lambda u: xf[u], m)
                m = v_affine(v, own, m, lambda u: xf[u], 0)

                def filmed(f, x, m, wait):
                    for u in range(U):
                        if wait is not None:
                            dve.wait_ge(S[wait], j * U + u + 1)
                        own.step(v.tensor_scalar(prd[u][:, 0, 0:D], PS[:, 4 * u + 1 + f, 0:D], gate[:], 1.0, ALU.mult, ALU.add))
                        own.need(m[u])
                        own.step(v.tensor_tensor(x(u), x(u), prd[u][:, 0, 0:D], ALU.mult))
                        m[u] = own.mark(v.scalar_tensor_tensor(x(u), PS[:, 4 * u + 1 + f, D:2 * D], gate[:], x(u), ALU.mult, ALU.add))
                    return m

                m = filmed(0, lambda u: xf[u], m, "B_film_psum")
                for u in range(U):
                    own.need(m[u])
                    v.nop().then_inc(S["B_xf"], 1)
                for u in range(U):
                    dve.wait_ge(S["B_dft_psum"], j * U + u + 1)
                    for b in range(2):
                        m[u] = own.mark(v.tensor_tensor(prd[u][:, b, :], PS[:, 4 * u + 3 * b, :], kfreq[:], ALU.mult))
                    own.need(m[u])
                    v.tensor_tensor(yfq[u], prd[u][:, :, 0:D], prd[u][:, :, D:2 * D], ALU.add).then_inc(S["B_yf"], 1)
                for u in range(U):
                    dve.wait_ge(S["B_y_psum"], j * U + u + 1)
                    m[u] = own.mark(v.tensor_copy(xf[u], PS[:, 4 * u, 0:D]))
                m = filmed(1, lambda u: xf[u], m, None)
                for u in range(U):
                    own.need(m[u])
                    m[u] = own.mark(v.tensor_tensor(xn[u], xn[u], xf[u], ALU.add))
                m = v_ln(dve, v, own, j, "B2", lambda u: xn[u], lambda u: work[u], m)
                m = v_affine(v, own, m, lambda u: work[u], 2)
                for u in range(U):
                    own.need(m[u])
                    v.nop().then_inc(S["B_h"], 1)
                for u in range(U):
                    dve.wait_ge(S["B_ffn_psum"], j * U + u + 1)
                    m[u] = own.mark(v.tensor_tensor(xn[u], xn[u], PS[:, 4 * u, 0:D], ALU.add))
                for u in range(U):
                    own.need(m[u])
                    v.nop().then_inc(S["B_end"], 1)
                m = v_ln(dve, v, own, j, "B3", lambda u: xn[u], lambda u: work[u], m)
                m = v_affine(v, own, m, lambda u: work[u], 4)
                for u in range(U):
                    own.need(m[u])
                    m[u] = own.mark(v.tensor_tensor(xtile(j, u), xtile(j, u), work[u], ALU.add))
                for u in range(U):
                    own.need(m[u])
                own.end()

        def pe_C(pe, mm, mm2):
            pe.wait_ge(S["wC_in"], 16 * 7)
            pe.nop().then_inc(S["C_end"], 1)
            with pe.Fori(0, TILES // U) as j:
                n = lambda u: j * U + u + 1
                for u in range(U):
                    pe.wait_ge(S["C_end"], j * U + 1)
                    pe.wait_ge(S["C_xn"], n(u))
                    pe_turn(pe, u, 0, xn[u]).then_inc(S["C_tp"], 1)
                for u in range(U):
                    pe.wait_ge(S["C_xnT"], n(u))
                    xs = [xnT[u][:, c, :] for c in range(2)]
                    mm2(PS[:, 4 * u + 1, 0:P], [adown[:, c, :] for c in range(2)], xs).then_inc(S["C_lat_psum"], 1)
                    mm2(PS[:, 4 * u + 2, 0:D], xs, [aq[:, c, :] for c in range(2)])
                for u in range(U):
                    pe.wait_ge(S["C_latT"], n(u))
                    mm(PS[:, 4 * u + 2, D:2 * D], latT[u], akv[:, 0:D], start=True, stop=True)
                    for b in range(2):
                        i_ = mm(PS[:, 4 * u + 3, b * D:(b + 1) * D],
                                flat(lat2[u][:, b]), akv[:, D:2 * D],
                                start=True, stop=True)
                    i_.then_inc(S["C_qkv_psum"], 1)
                for u in range(U):
                    pe.wait_ge(S["C_rot"], n(u))
                    for i in range(4):
                        i_ = pe.transpose(PS[:, 4 * u + i // 2, (i % 2) * P:(i % 2 + 1) * P],
                                          rot[u][:, i * P:(i + 1) * P], ident[:])
                    i_.then_inc(S["C_rot_tp"], 1)
                for u in range(U):
                    pe.wait_ge(S["C_qz"], n(u))
                    pe.wait_ge(S["C_kT"], n(u))
                    pe.wait_ge(S["C_vz"], n(u))
                    for h in range(H16):
                        for b in range(2):
                            bs = slice(b * T, (b + 1) * T)
                            i_ = mm(PS[bs, 4 * u + 2 + h // 8, (h % 8) * T:(h % 8 + 1) * T],
                                    qz[u][:, h // 8, h % 8, bs], kTs[u][:, h // 8, bs], start=True, stop=True)
                    i_.then_inc(S["C_s_psum"], 1)
                for u in range(U):
                    pe.wait_ge(S["C_pr"], n(u))
                    for i in range(8):
                        i_ = pe.transpose(PS[:, 4 * u + i // 4, (i % 4) * P:(i % 4 + 1) * P],
                                          flat(pr[u])[:, i * P:(i + 1) * P], ident[:])
                    i_.then_inc(S["C_pr_tp"], 1)
                for u in range(U):
                    pe.wait_ge(S["C_prT"], n(u))
                    for i in range(8):
                        for b in range(2):
                            bs = slice(b * T, (b + 1) * T)
                            i_ = mm(PS[bs, 4 * u + 2, i * 32:(i + 1) * 32], prT[u][:, i, bs], vz[u][:, b, i, :],
                                    start=True, stop=True)
                    i_.then_inc(S["C_o_psum"], 1)
                for u in range(U):
                    pe.wait_ge(S["C_oc"], n(u))
                    pe_turn(pe, u, 3, flat(oc[u])).then_inc(S["C_oc_tp"], 1)
                for u in range(U):
                    pe.wait_ge(S["C_ocT"], n(u))
                    mm2(PS[:, 4 * u, 0:D], [ocT[u][:, c, :] for c in range(2)], [ao[:, c, :] for c in range(2)]
                        ).then_inc(S["C_y_psum"], 1)

        def act_C(act, cp):
            act.wait_ge(S["C_vz0"], 1)
            with act.Fori(0, TILES // U) as j:
                n = lambda u: j * U + u + 1
                for u in range(U):
                    act.wait_ge(S["C_tp"], n(u))
                    cp(flat(xnT[u]), PS[:, 4 * u, 0:D]).then_inc(S["C_xnT"], 1)
                for u in range(U):
                    act.wait_ge(S["C_lat_psum"], n(u))
                    cp(latT[u], PS[:, 4 * u + 1, 0:P])
                    cp(lat2[u], PS[:, 4 * u + 1, 0:P].rearrange("p (b i) -> p b i", b=2).unsqueeze(2).to_broadcast([P, 2, 2, T])
                       ).then_inc(S["C_latT"], 1)
                for u in range(U):
                    act.wait_ge(S["C_qkv_psum"], n(u))
                    for h in range(2):
                        hs = slice(h * T, (h + 1) * T)
                        i_ = cp(vz[u][hs, :, :, h * 16:h * 16 + 16].rearrange("p b i d -> p (b i) d"),
                                PS[hs, 4 * u + 3, :].rearrange("p (a d) -> p a d", d=32)[:, :, h * 16:h * 16 + 16])
                    i_.then_inc(S["C_vz"], 1)
                for u in range(U):
                    act.wait_ge(S["C_rot_tp"], n(u))
                    cp(flat(kTs[u]), PS[:, 4 * u + 1, 0:D]).then_inc(S["C_kT"], 1)
                for u in range(U):
                    act.wait_ge(S["C_sub"], n(u))
                    nc.scalar.activation(flat(pr[u]), flat(pr[u]), ACT.Exp).then_inc(S["C_pr"], 1)
                for u in range(U):
                    act.wait_ge(S["C_pr_tp"], n(u))
                    cp(flat(prT[u]), bank(PS[:, 4 * u:4 * u + 2, :], 8 * P)).then_inc(S["C_prT"], 1)
                for u in range(U):
                    act.wait_ge(S["C_oc_tp"], n(u))
                    cp(flat(ocT[u]), PS[:, 4 * u + 3, 0:D]).then_inc(S["C_ocT"], 1)

        def dve_C(dve, v):
            dve.wait_ge(S["wC_in"], 16 * 7)
            for u in range(U):
                v.memset(vz[u], 0.0)
            dve.drain().then_inc(S["C_vz0"], 1)
            with dve.Fori(0, TILES // U) as j:
                n = lambda u: j * U + u + 1
                own = Own(dve, S["dve_turn"])
                m = v_ln(dve, v, own, j, "C0", lambda u: xtile(j, u), lambda u: xn[u])
                for u in range(U):
                    own.need(m[u])
                    v.nop().then_inc(S["C_xn"], 1)
                for u in range(U):
                    dve.wait_ge(S["C_qkv_psum"], n(u))
                    qk = PS[:, 4 * u + 2, :]
                    own.mark(v.tensor_tensor(rot[u], qk, rope[:, 0, :], ALU.mult))
                    m[u] = own.mark(v.tensor_tensor(rot2[u].rearrange("p (a b) -> p a b", b=2),
                                                    qk.rearrange("p (a b) -> p a b", b=2)[:, :, ::-1],
                                                    rope[:, 1, :].rearrange("p (a b) -> p a b", b=2), ALU.mult))
                for u in range(U):
                    own.need(m[u])
                    v.tensor_tensor(rot[u], rot[u], rot2[u], ALU.add).then_inc(S["C_rot"], 1)
                for u in range(U):
                    dve.wait_ge(S["C_rot_tp"], n(u))
                    for c in range(2):
                        i_ = v.tensor_tensor(qz[u][:, c], PS[:, 4 * u, c * P:(c + 1) * P].unsqueeze(1).to_broadcast([P, 8, P]),
                                             head_of_row[:].unsqueeze(2).to_broadcast([P, 8, P]), ALU.mult)
                    i_.then_inc(S["C_qz"], 1)
                for u in range(U):
                    dve.wait_ge(S["C_s_psum"], n(u))
                    s_ = bank(PS[:, 4 * u + 2:4 * u + 4, :], H16 * T).rearrange("p (a b) -> p a b", a=H16)
                    own.step(v.tensor_reduce(st[u][:, 0, :], s_, AXX, ALU.max))
                    v.tensor_tensor(pr[u], s_, st[u][:, 0, :].unsqueeze(2).to_broadcast([P, H16, T]), ALU.subtract
                                    ).then_inc(S["C_sub"], 1)
                for u in range(U):
                    dve.wait_ge(S["C_pr"], n(u))
                    own.step(v.tensor_reduce(st[u][:, 1, :], pr[u], AXX, ALU.add))
                    m[u] = own.mark(v.reciprocal(st[u][:, 2, :], st[u][:, 1, :]))
                for u in range(U):
                    own.need(m[u])
                    dve.wait_ge(S["C_o_psum"], n(u))
                    v.tensor_tensor(oc[u], PS[:, 4 * u + 2, 0:D].rearrange("p (a b) -> p a b", a=H16),
                                    st[u][:, 2, :].unsqueeze(2).to_broadcast([P, H16, 16]), ALU.mult).then_inc(S["C_oc"], 1)
                for u in range(U):
                    dve.wait_ge(S["C_y_psum"], n(u))
                    nc.vector.memset(spare(), 0.0)
                    v.tensor_tensor(xtile(j, u), xtile(j, u), PS[:, 4 * u, 0:D], ALU.add).then_inc(S["C_end"], 1)
                own.end()
                dve.wait_ge(S["C_end"], n(U - 1) + 1)
                v.memset(spare(), 0.0)

        def pe_D(pe, mm, mm2):
            pe.wait_ge(S["wD_in"], WD)
            pe.nop().then_inc(S["D_end"], 1)
            with pe.Fori(0, TILES // U) as j:
                n = lambda u: j * U + u + 1
                for u in range(U):
                    pe.wait_ge(S["D_end"], j * U + 1)
                    pe.wait_ge(S["D_xn"], n(u))
                    pe_turn(pe, u, 0, xn[u]).then_inc(S["D_tp"], 1)
                for u in range(U):
                    pe.wait_ge(S["D_xnT"], n(u))
                    mm2(PS[:, 4 * u + 1, 0:NE], [xnT[u][:, c, :] for c in range(2)], [router[:, c, :] for c in range(2)]
                        ).then_inc(S["D_logit_psum"], 1)

                def experts(u, es, turn):
                    for i, e_ in enumerate(es):
                        for w, bk in ((wgate, 2), (wup, 3)):
                            i_ = mm2(PS[:, 4 * u + bk, i * P:(i + 1) * P], [w[:, c, e_, :] for c in range(2)],
                                     [xnT[u][:, c, :] for c in range(2)])
                    i_.then_inc(S["D_gu_psum"], 1)

                for u in range(U):
                    experts(u, range(0, 4), 0)
                for u in range(U):
                    pe.wait_ge(S["D_comb"], n(u))
                    pe.transpose(PS[0:NE, 4 * u + 1, 0:P], rt[u][:, 15, :], ident[:]).then_inc(S["D_comb_tp"], 1)
                for u in range(U):
                    pe.wait_ge(S["D_combT"], n(u))
                    for e_ in range(NE):
                        i_ = mm(PS[:, 4 * u + e_ // 4, (e_ % 4) * P:(e_ % 4 + 1) * P], pick[0:NE, e_, :], combT[u][0:NE, :],
                                start=True, stop=True)
                    i_.then_inc(S["D_pick_psum"], 1)
                for u in range(U):
                    pe.wait_ge(S["D_h"], j * (3 * U) + u + 1)
                    experts(u, range(4, 8), 1)
                for u in range(U):
                    pe.wait_ge(S["D_h"], j * (3 * U) + U + u + 1)
                    experts(u, [8], 2)
                for u in range(U):
                    pe.wait_ge(S["D_h"], j * (3 * U) + 2 * U + u + 1)
                    o = PS[:, 4 * u + 1, 0:D]
                    for e_ in range(NE + 1):
                        i_ = mm(o, h9[u][:, e_, :], wdown[:, e_, :], start=e_ == 0, stop=e_ == NE)
                    i_.then_inc(S["D_y_psum"], 1)

        def act_D(act, cp):
            with act.Fori(0, TILES // U) as j:
                n = lambda u: j * U + u + 1
                for u in range(U):
                    act.wait_ge(S["D_tp"], n(u))
                    cp(flat(xnT[u]), PS[:, 4 * u, 0:D]).then_inc(S["D_xnT"], 1)
                for u in range(U):
                    act.wait_ge(S["D_logit_psum"], n(u))
                    nc.scalar.activation(rt[u][:, 0, :], PS[:, 4 * u + 1, 0:NE], ACT.Exp, scale=-1.0).then_inc(S["D_e"], 1)

                def tanh(u, w, turn):
                    act.wait_ge(S["D_gu_psum"], j * (3 * U) + turn * U + u + 1)
                    if turn:
                        act.wait_ge(S["D_h"], j * (3 * U) + turn * U + u + 1 - U)
                    nc.scalar.activation(th[u][:, 0:w], PS[:, 4 * u + 2, 0:w], ACT.Tanh, scale=0.5).then_inc(S["D_th"], 1)

                for u in range(U):
                    tanh(u, 4 * P, 0)
                for u in range(U):
                    act.wait_ge(S["D_comb_tp"], n(u))
                    cp(combT[u][0:NE, :], PS[0:NE, 4 * u + 1, 0:P]).then_inc(S["D_combT"], 1)
                for u in range(U):
                    tanh(u, 4 * P, 1)
                for u in range(U):
                    tanh(u, P, 2)

        def dve_D(dve, v):
            dve.wait_ge(S["wD_in"], WD)
            with dve.Fori(0, TILES // U) as j:
                n = lambda u: j * U + u + 1
                own = Own(dve, S["dve_turn"])
                m = v_ln(dve, v, own, j, "D0", lambda u: xtile(j, u), lambda u: xn[u])
                for u in range(U):
                    own.need(m[u])
                    v.nop().then_inc(S["D_xn"], 1)

                def route(u):
                    r = lambda i, a=0, b=8: rt[u][:, i, a:b]
                    tt = v.tensor_tensor
                    dve.wait_ge(S["D_e"], n(u))
                    own.step(v.tensor_scalar(r(1), r(0), 1.0, None, ALU.add))
                    own.step(v.reciprocal(r(1), r(1)))
                    own.step(tt(r(2), r(1), rbias, ALU.add))
                    pairs = r(2).rearrange("p (a b) -> p a b", b=2)
                    own.mark(tt(r(3, 0, 4).unsqueeze(2), pairs[:, :, 0:1], pairs[:, :, 1:2], ALU.max))
                    own.step(tt(r(4, 0, 4).unsqueeze(2), pairs[:, :, 0:1], pairs[:, :, 1:2], ALU.min))
                    hi = r(3, 0, 4).rearrange("p (a b) -> p a b", b=2)
                    lo = r(4, 0, 4).rearrange("p (a b) -> p a b", b=2)
                    own.mark(tt(r(5, 0, 2).unsqueeze(2), hi[:, :, 0:1], hi[:, :, 1:2], ALU.max))
                    own.mark(tt(r(6, 0, 2).unsqueeze(2), hi[:, :, 0:1], hi[:, :, 1:2], ALU.min))
                    own.step(tt(r(7, 0, 2).unsqueeze(2), lo[:, :, 0:1], lo[:, :, 1:2], ALU.max))
                    own.step(tt(r(6, 0, 2), r(6, 0, 2), r(7, 0, 2), ALU.max))
                    own.step(tt(r(5, 0, 2), r(5, 0, 2), r(6, 0, 2), ALU.add))
                    own.mark(tt(r(8, 1, 2), r(5, 1, 2), r(5, 0, 1), ALU.is_gt))
                    own.step(tt(r(8, 0, 1), r(5, 1, 2), r(5, 0, 1), ALU.is_le))
                    own.step(tt(r(9).rearrange("p (a b) -> p a b", b=4), r(2).rearrange("p (a b) -> p a b", b=4),
                                r(8, 0, 2).unsqueeze(2).to_broadcast([P, 2, 4]), ALU.mult))
                    mine = r(9).unsqueeze(2).to_broadcast([P, 8, 8])
                    other = r(9).unsqueeze(1).to_broadcast([P, 8, 8])
                    own.mark(tt(cmp8[u][:, 0], other, mine, ALU.is_gt))
                    own.step(tt(cmp8[u][:, 1], other, mine, ALU.is_equal))
                    own.step(tt(cmp8[u][:, 1], cmp8[u][:, 1], earlier[:], ALU.mult))
                    own.step(tt(cmp8[u][:, 0], cmp8[u][:, 0], cmp8[u][:, 1], ALU.add))
                    own.step(v.tensor_reduce(r(10), cmp8[u][:, 0], AXX, ALU.add))
                    own.step(v.scalar_tensor_tensor(r(11), r(10), 1.5, r(1), ALU.is_lt, ALU.mult))
                    own.step(v.tensor_reduce(r(12, 0, 1), r(11), AXX, ALU.add))
                    own.step(v.tensor_scalar(r(12, 0, 1), r(12, 0, 1), 1e-20, None, ALU.add))
                    own.step(v.reciprocal(r(12, 1, 2), r(12, 0, 1)))
                    v.tensor_scalar(r(15), r(11), r(12, 1, 2), None, ALU.mult).then_inc(S["D_comb"], 1)

                def glu(u, w, turn, cb):
                    dve.wait_ge(S["D_th"], j * (3 * U) + turn * U + u + 1)
                    h_ = flat(h9[u])[:, turn * 4 * P:turn * 4 * P + w]
                    own.step(v.scalar_tensor_tensor(h_, th[u][:, 0:w], 1.0, PS[:, 4 * u + 2, 0:w], ALU.add, ALU.mult))
                    own.step(v.scalar_tensor_tensor(h_, h_, 0.5, PS[:, 4 * u + 3, 0:w], ALU.mult, ALU.mult))
                    if cb is None:
                        v.nop().then_inc(S["D_h"], 1)
                    else:
                        dve.wait_ge(S["D_pick_psum"], n(u))
                        v.tensor_tensor(h_, h_, PS[:, 4 * u + cb, :], ALU.mult).then_inc(S["D_h"], 1)

                for u in range(U):
                    route(u)
                for u in range(U):
                    glu(u, 4 * P, 0, 0)
                for u in range(U):
                    glu(u, 4 * P, 1, 1)
                for u in range(U):
                    glu(u, P, 2, None)
                for u in range(U):
                    dve.wait_ge(S["D_y_psum"], n(u))
                    nc.vector.memset(spare(), 0.0)
                    v.tensor_tensor(xtile(j, u), xtile(j, u), PS[:, 4 * u + 1, 0:D], ALU.add).then_inc(S["D_end"], 1)
                own.end()
                dve.wait_ge(S["D_end"], n(U - 1) + 1)
                v.memset(spare(), 0.0)

        SETS = ((0, 6), (6, 6), (12, 4))
        NPAIR = [n // 2 for _, n in SETS]
        HALF = (slice(0, 1024), slice(1024, J))
        VALUES_AT = (1, 4, 7, 10)

        def kset(h):
            return h // 6

        def pe_E(pe, mm, mm2):
            pe.wait_ge(S["wE_in"], WE)
            pe.wait_ge(S["E_ready"], 1)
            pe.nop().then_inc(S["E_v_psum"], 8)
            pe.nop().then_inc(S["E_pv"], 1)
            pe.nop().then_inc(S["E_sT_psum"], 1)

            def keys(g, b, n):
                (h0, nh), slot = SETS[n // 2], 2 * (n % 3)
                if n >= 3:
                    pe.wait_ge(S["E_klo"], g * 6 + n - 1)
                for i in range(2):
                    js = slice((n % 2 * 2 + i) * 512, min(J, (n % 2 * 2 + i + 1) * 512))
                    o = PS[0:nh * 16, slot + i, 0:js.stop - js.start]
                    mm(o, wk1[:, 0, h0 * 16:(h0 + nh) * 16], ectx[b][:, 0, js], start=True, stop=False)
                    i_ = mm(o, wk1[0:CD - P, 1, h0 * 16:(h0 + nh) * 16], ectx[b][0:CD - P, 1, js], start=False, stop=True)
                i_.then_inc(S["E_k_psum"], 1)

            def values(g, b, i):
                pe.wait_ge(S["E_v"], g * 7 + i + 1)
                for c in range(2 * i, min(NJ, 2 * i + 2)):
                    r = P if c < NJ - 1 else JL
                    o = PS[0:r, 4 + i % 2, (c % 2) * D:(c % 2 + 1) * D]
                    mm(o, ectx[b][:, 0, c * P:c * P + r], wv1[:, 0, :], start=True, stop=False)
                    i_ = mm(o, ectx[b][0:CD - P, 1, c * P:c * P + r], wv1[0:CD - P, 1, :], start=False, stop=True)
                i_.then_inc(S["E_v_psum"], 1)

            def token_turn(g):
                pe.wait_ge(S["E_acc"], g + 1)
                for p in range(8):
                    i_ = mm(PS[:, 6, p * 33:(p + 1) * 33], eP[1][0:66, p * P:(p + 1) * P], fold, start=True, stop=True)
                i_.then_inc(S["E_sums_psum"], 1)

            def out_turn(g):
                pe.wait_ge(S["E_o"], g + 1)
                for c in range(2):
                    i_ = mm(PS[:, 7, c * T:(c + 1) * T], flat(eo[:, 4 * c:4 * c + 4, :]), twice_eye[:], start=True, stop=True)
                i_.then_inc(S["E_oT_psum"], 1)


            def product(t):
                pe.wait_ge(S["E_oT"], t * 2 + 3)
                mm2(PS[:, 6, 0:D], [eoT[:, c, :] for c in range(2)], [wo1[:, c, :] for c in range(2)]).then_inc(S["E_y_psum"], 1)

            def first_keys(t, b):
                pe.wait_ge(S[f"E_ctx{b}_in"], t * 32 + 32)
                keys(t * 2 + b, b, 0)

            def tile(t, first=False, last=False):
                for b in range(2):
                    g = t * 2 + b
                    keys(g, b, 1)
                    before = b == 1 or not first
                    if before:
                        token_turn(g - 1)
                    if b == 0:
                        pe.wait_ge(S["E_xn"], t + 1)
                        for c in range(2):
                            i_ = pe.transpose(PS[:, 7, (2 + c) * P:(3 + c) * P], xn[0][:, c * P:(c + 1) * P], ident[:])
                        i_.then_inc(S["E_tp"], 1)
                    keys(g, b, 2)
                    pe.wait_ge(S["E_xnT"], t + 1)
                    if before:
                        out_turn(g - 1)
                    keys(g, b, 3)
                    if b == 0:
                        pe.wait_ge(S["E_oT"], g + 1)
                        for m, (h0, nh) in enumerate(SETS):
                            i_ = mm2(PS[0:nh * 16, 7, m * P:(m + 1) * P], [wq1[:, c, h0 * 16:(h0 + nh) * 16] for c in range(2)],
                                     [xnT[0][:, c, :] for c in range(2)])
                        i_.then_inc(S["E_q_psum"], 1)
                        if not first:
                            product(t - 1)
                    keys(g, b, 4)
                    keys(g, b, 5)
                    if b == 0:
                        pe.wait_ge(S["E_klo"], g * 6 + 7)
                        values(g, b, 0)
                    pe.wait_ge(S["E_qz"], g + 1)
                    pe.wait_ge(S["E_oT"], g + 1)
                    if b == 0 and not first:
                        pe.wait_ge(S["E_x"], t)
                    pe.wait_ge(S["E_bias_in"], g * 16 + 16)
                    for n in range(16):
                        p, slot = n // 2, (6, 0, 2)[n % 3]
                        m = kset(2 * p)
                        if n % 2 == 0 and (p == 0 or kset(2 * p - 2) != m):
                            pe.wait_ge(S[f"E_kst{m}"], (g + 1) * 48 * NPAIR[m])
                        if n in (1, 2):
                            pe.wait_ge(S["E_klo"], g * 6 + n + 4)
                        if n >= 3:
                            pe.wait_ge(S["E_max"], g * 16 + n - 2)
                        for i in range(2):
                            js = slice((n % 2 * 2 + i) * 512, min(J, (n % 2 * 2 + i + 1) * 512))
                            i_ = mm(PS[:, slot + i, 0:js.stop - js.start], flat(eqz[0:97, 2 * p:2 * p + 2, :]), ekst[0:97, p, js],
                                    start=True, stop=True)
                        i_.then_inc(S["E_s_psum"], 1)
                        if n == 1:
                            pe.wait_ge(S["E_klo"], g * 6 + 7)
                        if n in VALUES_AT and (b == 1 or n > 1):
                            values(g, b, VALUES_AT.index(n))
                    values(g, b, 4)
                    values(g, b, 5)
                    pe.wait_ge(S["E_maxes"], g + 1)
                    for p in range(8):
                        i_ = mm(PS[0:KR, 6 + p // 4, (p % 4) * P:(p % 4 + 1) * P], emax[:, p, :], ident16, start=True, stop=True)
                    i_.then_inc(S["E_mrow_psum"], 1)
                    values(g, b, 6)
                    pe.wait_ge(S["E_mrow"], g + 1)
                    pe.wait_ge(S["E_mrow_v"], g + 1)

                    def attend(c):
                        pe.wait_ge(S["E_plo"], g * NJ + c + 1)
                        if c == 0:
                            pe.wait_ge(S["E_v"], g * 7 + 9)
                        r = P if c < NJ - 1 else JL
                        for p in range(8):
                            for part in (ePh, ePl):
                                i_ = mm(PS[0:66, 6 + p // 4, (p % 4) * P:(p % 4 + 1) * P], eV[0:r, c, p, :],
                                        part[c % 2][0:r, p * P:(p + 1) * P], start=c == 0 and p % 4 == 0 and part is ePh,
                                        stop=c == NJ - 1 and p % 4 == 3 and part is ePl, skip_group_check=True)
                        i_.then_inc(S["E_pv"], 1)

                    for c in range(NJ):
                        r = P if c < NJ - 1 else JL
                        if c >= 2:
                            pe.wait_ge(S["E_p"], g * NJ + c - 1)
                        for p in range(8):
                            i_ = mm(PS[0:r, 2 * (c % 2) + p // 4, (p % 4) * P:(p % 4 + 1) * P], ekst[0:KR, p, c * P:c * P + r],
                                    flat(eqz[0:KR, 2 * p:2 * p + 2, :]), start=True, stop=True)
                        i_.then_inc(S["E_sT_psum"], 1)
                        if c >= 2:
                            attend(c - 2)
                    if b == 0 or not last:
                        pe.wait_ge(S["E_p"], g * NJ + NJ)
                        first_keys(t + b, 1 - b)
                    attend(NJ - 2)
                    attend(NJ - 1)

            first_keys(0, 0)
            tile(0, first=True)
            with pe.Fori(1, TILES - 1) as t:
                tile(t)
            tile(TILES - 1, last=True)
            token_turn(B - 1)
            out_turn(B - 1)
            product(TILES - 1)

        def act_E(act, cp):
            act.wait_ge(S["E_ready"], 1)
            act.nop().then_inc(S["E_oT"], 1)

            def out_turned(g, b):
                act.wait_ge(S["E_oT_psum"], g + 1)
                cp(eoT[:, :, b * T:(b + 1) * T], PS[:, 7, 0:P].rearrange("p (c i) -> p c i", c=2)).then_inc(S["E_oT"], 1)

            def high(g, n):
                rs, slot, js = slice(0, SETS[n // 2][1] * 16), 2 * (n % 3), HALF[n % 2]
                act.wait_ge(S["E_k_psum"], g * 6 + n + 1)
                cp(ehi[rs, n // 2, js], bank(PS[rs, slot:slot + 2, :], js.stop - js.start)).then_inc(S["E_khi"], 1)

            def values_out(g, i):
                act.wait_ge(S["E_v_psum"], g * 7 + i + 9)
                n_ = 2 if i < NJ // 2 else 1
                r = P if n_ == 2 else JL
                cp(eV[0:r, 2 * i:2 * i + n_, :, 0:32],
                   PS[0:r, 4 + i % 2, 0:n_ * D].rearrange("p (c a d) -> p c a d", c=n_, d=32)).then_inc(S["E_vhi"], 1)

            def tile(t, first=False):
                for b in range(2):
                    g = t * 2 + b
                    high(g, 0)
                    if b == 0:
                        act.wait_ge(S["E_tp"], t + 1)
                        cp(flat(xnT[0]), PS[:, 7, D:2 * D]).then_inc(S["E_xnT"], 1)
                    high(g, 1)
                    high(g, 2)
                    if b == 1 or not first:
                        out_turned(g - 1, 1 - b)
                    high(g, 3)
                    if b == 0:
                        act.wait_ge(S["E_q_psum"], t + 1)
                        for m, (h0, nh) in enumerate(SETS):
                            i_ = cp(eqhi[0:nh * 16, m, :], PS[0:nh * 16, 7, m * P:(m + 1) * P], 0.25)
                        i_.then_inc(S["E_qhi"], 1)
                    high(g, 4)
                    high(g, 5)
                    for i in range(6):
                        values_out(g, i)
                    act.wait_ge(S["E_mrow_psum"], g + 1)
                    cp(flat(eqz[96:KR, 0:8, :]), PS[96:KR, 6, :]).then_inc(S["E_mrow"], 1)
                    values_out(g, 6)
                    for c in range(NJ):
                        r = P if c < NJ - 1 else JL
                        act.wait_ge(S["E_sT_psum"], g * NJ + c + 2)
                        if c >= 2:
                            act.wait_ge(S["E_plo"], g * NJ + c - 1)
                        nc.scalar.activation(eP[c % 2][0:r, :], bank(PS[0:r, 2 * (c % 2):2 * (c % 2) + 2, :], 1024), ACT.Exp
                                             ).then_inc(S["E_p"], 1)
                        if c % 2 == 0:
                            if c >= 2:
                                act.wait_ge(S["E_pv"], g * NJ + c)
                            act.wait_ge(S["E_p"], g * NJ + c + 1)
                            cp(ePh[c % 2][0:r, :], eP[c % 2][0:r, :]).then_inc(S["E_phi"], 1)
                    act.wait_ge(S["E_pv"], g * NJ + NJ + 1)
                    cp(eP[1][0:66, :], bank(PS[0:66, 6:8, :], 1024)).then_inc(S["E_acc"], 1)

            tile(0, first=True)
            with act.Fori(1, TILES) as t:
                tile(t)
            out_turned(B - 1, 1)

        def dve_E(dve, v):
            own = Own(dve, S["dve_E0"])
            dve.wait_ge(S["wE_in"], WE)
            own.step(v.memset(ekst[96:KR, :, :], 1.0))
            own.step(v.memset(eqz[:, :, :], 1.0))
            own.step(v.memset(emax[:, :, 0:96], 0.0))
            own.step(v.memset(emax[:, :, 96:97], 1.0))
            own.step(v.tensor_copy(ident16, ident[:]))
            own.step(v.tensor_reduce(ehalf_of_row, head_of_row[:].rearrange("p (a b) -> p b a", b=2), AXX, ALU.add))
            own.step(v.memset(eV[:, :, :, 32:33], 1.0))
            own.step(v.memset(eV[:, :, :, 65:66], 0.0))
            v.nop().then_inc(S["E_ready"], 1)
            for n in ("E_klo", "E_v", "E_v"):
                v.nop().then_inc(S[n], 1)
            def low(g, n):
                rs, slot, js = slice(0, SETS[n // 2][1] * 16), 2 * (n % 3), HALF[n % 2]
                dve.wait_ge(S["E_khi"], g * 6 + n + 1)
                v.tensor_tensor(elo[n // 2][rs, js], bank(PS[rs, slot:slot + 2, :], js.stop - js.start), ehi[rs, n // 2, js],
                                ALU.subtract).then_inc(S["E_klo"], 1)

            def values_low(g, i):
                dve.wait_ge(S["E_vhi"], g * 7 + i + 1)
                n_ = 2 if i < NJ // 2 else 1
                r = P if n_ == 2 else JL
                for k in range(n_):
                    i_ = v.tensor_tensor(eV[0:r, 2 * i + k, :, 33:65],
                                         PS[0:r, 4 + i % 2, k * D:(k + 1) * D].rearrange("p (a d) -> p a d", d=32),
                                         eV[0:r, 2 * i + k, :, 0:32], ALU.subtract)
                i_.then_inc(S["E_v"], 1)

            def split_q(t, b):
                v.memset(spare(), 0.0)
                q_ = eqst[0:96, :, b * T:(b + 1) * T]
                z_ = eqz[0:96, :, :].rearrange("p (a h) i -> p a h i", h=2)
                for h in range(2):
                    i_ = v.scalar_tensor_tensor(z_[:, :, h, :], q_, valid[0:96, bass.ds(t * 2 + b, 1)],
                                                ehalf_of_row[0:96, h:h + 1].unsqueeze(2).to_broadcast([96, 8, T]),
                                                ALU.mult, ALU.mult)
                i_.then_inc(S["E_qz"], 1)

            def sums_out(own, g):
                dve.wait_ge(S["E_sums_psum"], g + 1)
                o_ = PS[:, 6, 0:8 * 33].rearrange("p (a d) -> p a d", d=33)
                own.step(v.reciprocal(erz.unsqueeze(2), o_[:, :, 32:33]))
                own.step(v.tensor_tensor(eo, o_[:, :, 0:32], erz.unsqueeze(2).to_broadcast([P, 8, 32]), ALU.mult))
                v.tensor_tensor(eo, eo, pair_diag[:].unsqueeze(1).to_broadcast([P, 8, 32]), ALU.mult).then_inc(S["E_o"], 1)

            def x_out(t):
                dve.wait_ge(S["E_y_psum"], t + 1)
                v.memset(spare(), 0.0)
                x_ = X[:, bass.ds(t, 1), :].rearrange("p a b -> p (a b)")
                v.tensor_tensor(x_, x_, PS[:, 6, 0:D], ALU.add).then_inc(S["E_x"], 1)

            def tile(t, first=False):
                own = Own(dve, S["dve_turn"])
                b_ = bn[0]
                own.step(v.bn_stats(b_[:, 0:6], X[:, bass.ds(t, 1), :].rearrange("p a b -> p (a b)")))
                own.step(v.bn_aggr(b_[:, 6:8], b_[:, 0:6]))
                v.tensor_scalar(b_[:, 8:9], b_[:, 7:8], EPS, None, ALU.add).then_inc(S["E0_var"], 1)
                dve.wait_ge(S["E0_rstd"], t + 1)
                v.tensor_scalar(xn[0], X[:, bass.ds(t, 1), :].rearrange("p a b -> p (a b)"), b_[:, 6:7], b_[:, 9:10],
                                ALU.subtract, ALU.mult).then_inc(S["E_xn"], 1)

                for b in range(2):
                    g = t * 2 + b
                    low(g, 0)
                    if b == 1 or not first:
                        sums_out(own, g - 1)
                    low(g, 1)
                    low(g, 2)
                    if b == 1:
                        split_q(t, b)
                    low(g, 3)
                    if b == 0:
                        dve.wait_ge(S["E_qhi"], t + 1)
                        for m, (h0, nh) in enumerate(SETS):
                            rs = slice(0, nh * 16)
                            i_ = v.scalar_tensor_tensor(eqlo[rs, m, :], PS[rs, 7, m * P:(m + 1) * P], 0.25, eqhi[rs, m, :],
                                                        ALU.mult, ALU.subtract)
                        i_.then_inc(S["E_qlo"], 1)
                        if not first:
                            x_out(t - 1)
                    low(g, 4)
                    low(g, 5)
                    if b == 0:
                        dve.wait_ge(S["E_qst"], t * 144 + 144)
                        split_q(t, b)
                    for n in range(16):
                        slot = (6, 0, 2)[n % 3]
                        dve.wait_ge(S["E_s_psum"], g * 16 + n + 1)
                        v.tensor_reduce(ehalf[:, n // 2, n % 2:n % 2 + 1], bank(PS[:, slot:slot + 2, :], (1024, J - 1024)[n % 2]),
                                        AXX, ALU.max, negate=True).then_inc(S["E_max"], 1)
                        if n - 2 in VALUES_AT:
                            values_low(g, VALUES_AT.index(n - 2))
                    dve.wait_ge(S["E_max"], g * 16 + 16)
                    v.memset(spare(), 0.0)
                    own.step(v.tensor_tensor(enm[:, 0, :].unsqueeze(2), ehalf[:, :, 0:1], ehalf[:, :, 1:2], ALU.min))
                    for i in range(3):
                        own.step(v.tensor_copy(emax[:, :, 97 + i:98 + i], enm[:, i, :].unsqueeze(2)))
                        if i < 2:
                            own.step(v.tensor_tensor(enm[:, i + 1, :].unsqueeze(2), enm[:, i, :].unsqueeze(2),
                                                     emax[:, :, 97 + i:98 + i], ALU.subtract))
                    v.nop().then_inc(S["E_maxes"], 1)
                    dve.wait_ge(S["E_mrow_psum"], g + 1)
                    v.tensor_copy(flat(eqz[96:KR, 8:16, :]), PS[96:KR, 7, :]).then_inc(S["E_mrow_v"], 1)
                    for i in range(4, 7):
                        values_low(g, i)
                    for c in range(NJ):
                        r = P if c < NJ - 1 else JL
                        if c % 2 == 0:
                            dve.wait_ge(S["E_phi"], g * 7 + c // 2 + 1)
                        else:
                            dve.wait_ge(S["E_p"], g * NJ + c + 1)
                            if c >= 2:
                                dve.wait_ge(S["E_pv"], g * NJ + c)
                            own.step(v.tensor_copy(ePh[1][0:r, :], eP[1][0:r, :]))
                        if c % 2 == 0 and c >= 2:
                            dve.wait_ge(S["E_pv"], g * NJ + c)
                        v.tensor_tensor(ePl[c % 2][0:r, :], eP[c % 2][0:r, :], ePh[c % 2][0:r, :], ALU.subtract
                                        ).then_inc(S["E_plo"], 1)
                own.end()

            tile(0, first=True)
            with dve.Fori(1, TILES) as t:
                tile(t)
            own = Own(dve, S["dve_turn"])
            sums_out(own, B - 1)
            own.end()
            x_out(TILES - 1)

        LANES = 2 * U

        def pe_F(pe, mm, mm2):
            pe.wait_ge(S["wF_in"], WF)
            pe.nop().then_inc(S["F_end"], 1)
            with pe.Fori(0, TILES // U) as j:
                n = lambda u: j * U + u + 1
                l = lambda w: j * LANES + w + 1
                for u in range(U):
                    pe.wait_ge(S["F_end"], j * U + 1)
                    pe.wait_ge(S["F_xn"], n(u))
                    pe_turn(pe, u, 0, xn[u]).then_inc(S["F_tp"], 1)
                for u in range(U):
                    pe.wait_ge(S["F_xnT"], n(u))
                    xs = [xnT[u][:, c, :] for c in range(2)]
                    for w_, bk, name in ((tq, 0, "F_q_psum"), (tk, 2, "F_k_psum")):
                        for c in range(8):
                            cs = slice(c * P, (c + 1) * P)
                            i_ = mm2(PS[:, 4 * u + bk + c // 4, (c % 4) * P:(c % 4 + 1) * P],
                                     [w_[:, k, cs] for k in range(2)], xs)
                        i_.then_inc(S[name], 1)
                for u in range(U):
                    pe.wait_ge(S["F_qz"], n(u))
                    for h in range(2):
                        i_ = mm2(PS[:, 4 * u + h, :], [xnT[u][:, k, :] for k in range(2)],
                                 [tv[:, k, h * 512:(h + 1) * 512] for k in range(2)])
                    i_.then_inc(S["F_v_psum"], 1)
                for w in range(LANES):
                    u, b = divmod(w, 2)
                    pe.wait_ge(S["F_v"], l(2 * u + 1))
                    pe.wait_ge(S["F_qz"], n(u))
                    pe.wait_ge(S["F_k"], n(u))
                    for c in range(8):
                        i_ = mm(PS[0:KEYS, 2 * w + c // 4, (c % 4) * P:(c % 4 + 1) * P], fk[u][:, c, b, :],
                                fqz[u][:, c, b].rearrange("p i h -> p (i h)"), start=True, stop=True)
                    i_.then_inc(S["F_dT_psum"], 1)
                for w in range(LANES):
                    pe.wait_ge(S["F_dT"], l(w))
                    for i in range(8):
                        i_ = pe.transpose(PS[:, 2 * w + i // 4, (i % 4) * KEYS:(i % 4 + 1) * KEYS],
                                          fdT[w][0:KEYS, i * 8:(i + 1) * 8, :].rearrange("p i h -> p (i h)"),
                                          ident[0:KEYS, 0:KEYS])
                    i_.then_inc(S["F_d_psum"], 1)
                for w in range(LANES):
                    pe.wait_ge(S["F_d"], l(w))
                    for i in range(2):
                        i_ = mm(PS[:, 2 * w + i, 0:4 * KEYS], mix[:, 0, :], flat(fd[w][:, 4 * i:4 * i + 4, :]),
                                start=True, stop=True)
                    i_.then_inc(S["F_mix_psum"], 1)
                for w in range(LANES):
                    pe.wait_ge(S["F_p"], l(w))
                    for i in range(8):
                        i_ = mm(PS[0:KEYS, 2 * w + i // 4, (i % 4) * P:(i % 4 + 1) * P], fd[w][:, i, :], mix[:, 1, :],
                                start=True, stop=True)
                    i_.then_inc(S["F_pT_psum"], 1)
                for w in range(LANES):
                    u, b = divmod(w, 2)
                    pe.wait_ge(S["F_pT"], l(w))
                    for h in range(H16):
                        hs = slice((h % 2) * AD, (h % 2 + 1) * AD)
                        i_ = mm(PS[hs, 2 * w, (h // 2) * T:(h // 2 + 1) * T], fv[u][0:KEYS, b, h * AD:(h + 1) * AD],
                                fdT[w].rearrange("p a b -> p (a b)")[0:KEYS, h * T:(h + 1) * T], start=True, stop=True)
                    i_.then_inc(S["F_o_psum"], 1)
                for u in range(U):
                    pe.wait_ge(S["F_oT"], j * LANES + 2 * u + 2)
                    o = PS[:, 4 * u, 0:D]
                    mm(o, ones[0:1, :], rows[:, 1280:1280 + D], start=True, stop=False)
                    for c in range(8):
                        i_ = mm(o, foT[u][:, c, :], to[:, c, :], start=False, stop=c == 7)
                    i_.then_inc(S["F_y_psum"], 1)

        def act_F(act, cp):
            act.wait_ge(S["F_zero"], 1)
            with act.Fori(0, TILES // U) as j:
                n = lambda u: j * U + u + 1
                l = lambda w: j * LANES + w + 1
                for u in range(U):
                    act.wait_ge(S["F_tp"], n(u))
                    cp(flat(xnT[u]), PS[:, 4 * u, 0:D]).then_inc(S["F_xnT"], 1)
                for u in range(U):
                    act.wait_ge(S["F_q_psum"], n(u))
                    for bk in range(2):
                        for h in range(2):
                            hs = slice(h * AD, (h + 1) * AD)
                            i_ = cp(fqz[u][hs, 4 * bk:4 * bk + 4, :, :, h].rearrange("p c b i -> p c (b i)"),
                                    PS[hs, 4 * u + bk, :].rearrange("p (c t) -> p c t", c=4), AD ** -0.5)
                    i_.then_inc(S["F_qz"], 1)
                for w in range(LANES):
                    u, b = divmod(w, 2)
                    act.wait_ge(S["F_v_psum"], n(u))
                    cp(fv[u][0:T, b, :], bank(PS[b * T:(b + 1) * T, 4 * u:4 * u + 2, :], 1024)).then_inc(S["F_v"], 1)
                for w in range(LANES):
                    act.wait_ge(S["F_dT_psum"], l(w))
                    for bk in range(2):
                        i_ = cp(fdT[w][0:KEYS, :, 8 * bk:8 * bk + 8].rearrange("p i (c h) -> p c i h", h=2),
                                PS[0:KEYS, 2 * w + bk, :].rearrange("p (c i h) -> p c i h", c=4, h=2))
                    i_.then_inc(S["F_dT"], 1)
                for w in range(LANES):
                    act.wait_ge(S["F_sub"], l(w))
                    nc.scalar.activation(flat(fd[w]), flat(fd[w]), ACT.Exp).then_inc(S["F_exp"], 1)
                for w in range(LANES):
                    act.wait_ge(S["F_pT_psum"], l(w))
                    for bk in range(2):
                        i_ = cp(fdT[w].rearrange("p a b -> p (a b)")[0:KEYS, :].rearrange("p (h i) -> p i h", h=H16)[:, 32 * bk:32 * bk + 32, :],
                                PS[0:KEYS, 2 * w + bk, :].rearrange("p (i h) -> p i h", h=H16))
                    i_.then_inc(S["F_pT"], 1)

        def dve_F(dve, v):
            for u in range(U):
                i_ = v.memset(fqz[u].rearrange("p a b c d -> p (a b c d)"), 0.0)
            i_.then_inc(S["F_zero"], 1)
            dve.wait_ge(S["wF_in"], WF)
            with dve.Fori(0, TILES // U) as j:
                n = lambda u: j * U + u + 1
                l = lambda w: j * LANES + w + 1
                own = Own(dve, S["dve_turn"])
                m = v_ln(dve, v, own, j, "F0", lambda u: xtile(j, u), lambda u: xn[u])
                for u in range(U):
                    own.need(m[u])
                    v.nop().then_inc(S["F_xn"], 1)
                for u in range(U):
                    dve.wait_ge(S["F_k_psum"], n(u))
                    for bk in range(2):
                        i_ = v.tensor_copy(fk[u][:, 4 * bk:4 * bk + 4, :, 0:T],
                                           PS[:, 4 * u + 2 + bk, :].rearrange("p (c b t) -> p c b t", c=4, b=2))
                    i_.then_inc(S["F_k"], 1)
                for w in range(LANES):
                    dve.wait_ge(S["F_d_psum"], l(w))
                    for i in range(2):
                        i_ = v.tensor_copy(flat(fd[w][:, 4 * i:4 * i + 4, :]), PS[:, 2 * w + i, 0:4 * KEYS])
                    i_.then_inc(S["F_d"], 1)
                LATE = slice(6, 8)
                mk = [0] * LANES
                for w in range(LANES):
                    dve.wait_ge(S["F_mix_psum"], l(w))
                    for i in range(2):
                        mk[w] = own.mark(v.tensor_tensor(flat(fm[w][:, 4 * i:4 * i + 4, :]), PS[:, 2 * w + i, 0:4 * KEYS],
                                                         causal[:, i * 4 * KEYS:(i + 1) * 4 * KEYS], ALU.add))
                for w in range(LANES):
                    own.need(mk[w])
                    own.mark(v.tensor_reduce(fst[w][:, 0:8], fm[w], AXX, ALU.max))
                    mk[w] = own.mark(v.tensor_scalar(fd[w][:, LATE, :], fm[w][:, LATE, :], -1.0, None, ALU.mult))
                for r in range(3):
                    for i in range(2):
                        for w in range(LANES):
                            src = fd[w][:, 6 + i, :]
                            own.need(mk[w])
                            k8 = own.mark(v.max(f8[w][:, i, :], src))
                            if r < 2:
                                own.need(k8)
                                nk = own.mark(v.match_replace(src, f8[w][:, i, :], src, LOW))
                            else:
                                nk = k8
                            if i == 1:
                                mk[w] = nk
                for w in range(LANES):
                    own.need(mk[w])
                    own.mark(v.tensor_scalar(fst[w][:, 8:10], f8[w][:, :, 0], -1.0, None, ALU.mult))
                    v.tensor_tensor(fd[w], fm[w], fst[w][:, 0:8].unsqueeze(2).to_broadcast([P, 8, KEYS]), ALU.subtract
                                    ).then_inc(S["F_sub"], 1)
                for w in range(LANES):
                    dve.wait_ge(S["F_exp"], l(w))
                    for i in range(2):
                        mk[w] = own.mark(v.scalar_tensor_tensor(fd[w][:, 6 + i, :], fm[w][:, 6 + i, :], fst[w][:, 8 + i:9 + i],
                                                                fd[w][:, 6 + i, :], ALU.is_ge, ALU.mult))
                for w in range(LANES):
                    own.need(mk[w])
                    mk[w] = own.mark(v.tensor_reduce(fst[w][:, 16:24], fd[w], AXX, ALU.add))
                for w in range(LANES):
                    own.need(mk[w])
                    mk[w] = own.mark(v.reciprocal(fst[w][:, 24:32], fst[w][:, 16:24]))
                for w in range(LANES):
                    own.need(mk[w])
                    v.tensor_tensor(fd[w], fd[w], fst[w][:, 24:32].unsqueeze(2).to_broadcast([P, 8, KEYS]), ALU.mult
                                    ).then_inc(S["F_p"], 1)
                for w in range(LANES):
                    u, b = divmod(w, 2)
                    dve.wait_ge(S["F_o_psum"], l(w))
                    v.tensor_copy(foT[u][:, :, b * T:(b + 1) * T], PS[:, 2 * w, :].rearrange("p (c i) -> p c i", c=8)
                                  ).then_inc(S["F_oT"], 1)
                for u in range(U):
                    dve.wait_ge(S["F_y_psum"], n(u))
                    v.memset(spare(), 0.0)
                    v.tensor_tensor(xtile(j, u), xtile(j, u), PS[:, 4 * u, 0:D], ALU.add).then_inc(S["F_end"], 1)
                own.end()
                dve.wait_ge(S["F_end"], n(U - 1) + 1)
                v.memset(spare(), 0.0)

        def pe_G(pe, mm, mm2):
            pe.wait_ge(S["wG_in"], 32)
            pe.nop().then_inc(S["G_end"], 1)
            with pe.Fori(0, TILES // U) as j:
                n = lambda u: j * U + u + 1
                for u in range(U):
                    pe.wait_ge(S["G_end"], j * U + 1)
                    pe.wait_ge(S["G_xn"], n(u))
                    pe_turn(pe, u, 0, xn[u]).then_inc(S["G_tp"], 1)
                for u in range(U):
                    pe.wait_ge(S["G_xnT"], n(u))
                    for c in range(8):
                        cs = slice(c * P, (c + 1) * P)
                        i_ = mm2(PS[:, 4 * u + 2 + c // 4, (c % 4) * P:(c % 4 + 1) * P],
                                 [w1_1[:, k, cs] for k in range(2)], [xnT[u][:, k, :] for k in range(2)])
                        if c % 4 == 3:
                            i_.then_inc(S["G_hid_psum"], 1)
                for u in range(U):
                    o = PS[:, 4 * u, 0:D]
                    mm(o, ones[0:1, :], rows[:, 1536:1536 + D], start=True, stop=False)
                    for c in range(8):
                        if c % 4 == 0:
                            pe.wait_ge(S["G_hid"], (j * U + u) * 2 + c // 4 + 1)
                        i_ = mm(o, ghid[u][:, c, :], w2_1[:, c, :], start=False, stop=c == 7)
                    i_.then_inc(S["G_ffn_psum"], 1)

        def act_G(act, cp):
            with act.Fori(0, TILES // U) as j:
                n = lambda u: j * U + u + 1
                for u in range(U):
                    act.wait_ge(S["G_tp"], n(u))
                    cp(flat(xnT[u]), PS[:, 4 * u, 0:D]).then_inc(S["G_xnT"], 1)
                for u in range(U):
                    for c in range(8):
                        if c % 4 == 0:
                            act.wait_ge(S["G_hid_psum"], (j * U + u) * 2 + c // 4 + 1)
                        i_ = nc.scalar.activation(ghid[u][:, c, :], PS[:, 4 * u + 2 + c // 4, (c % 4) * P:(c % 4 + 1) * P],
                                                  ACT.Relu, bias=cols[:, 1, c:c + 1])
                        if c % 4 == 3:
                            i_.then_inc(S["G_hid"], 1)

        def dve_G(dve, v):
            with dve.Fori(0, TILES // U) as j:
                n = lambda u: j * U + u + 1
                own = Own(dve, S["dve_turn"])
                m = v_ln(dve, v, own, j, "G0", lambda u: xtile(j, u), lambda u: xn[u])
                for u in range(U):
                    own.need(m[u])
                    v.nop().then_inc(S["G_xn"], 1)
                for u in range(U):
                    dve.wait_ge(S["G_ffn_psum"], n(u))
                    m[u] = own.mark(v.tensor_tensor(xn[u], xn[u], PS[:, 4 * u, 0:D], ALU.add))
                for u in range(U):
                    own.need(m[u])
                    v.nop().then_inc(S["G_end"], 1)
                m = v_ln(dve, v, own, j, "G1", lambda u: xn[u], lambda u: work[u], m)
                m = v_affine(v, own, m, lambda u: work[u], 6)
                for u in range(U):
                    own.need(m[u])
                    m[u] = own.mark(v.tensor_tensor(xtile(j, u), xtile(j, u), work[u], ALU.add))
                own.end()


        def pe_rest(pe, mm, mm2):
            pe.wait_ge(S["A_done"], 4)
            for ph, f in (("B", pe_B), ("C", pe_C), ("D", pe_D), ("E", pe_E), ("F", pe_F), ("G", pe_G)):
                if ph in stages:
                    f(pe, mm, mm2)
                    pe.drain().then_inc(S[ph + "_done"], 1)
                    pe.wait_ge(S[ph + "_done"], 4)
            pe.drain().then_inc(S["all_done"], 1)

        def act_rest(act, cp):
            act.wait_ge(S["A_done"], 4)
            for ph, f in (("B", act_B), ("C", act_C), ("D", act_D), ("E", act_E), ("F", act_F), ("G", act_G)):
                if ph in stages:
                    f(act, cp)
                    act.drain().then_inc(S[ph + "_done"], 1)
                    act.wait_ge(S[ph + "_done"], 4)
            act.drain().then_inc(S["all_done"], 1)

        def dve_rest(dve, v):
            dve.wait_ge(S["A_done"], 4)
            for ph, f in (("B", dve_B), ("C", dve_C), ("D", dve_D), ("E", dve_E), ("F", dve_F), ("G", dve_G)):
                if ph in stages:
                    f(dve, v)
                    dve.drain().then_inc(S[ph + "_done"], 1)
                    dve.wait_ge(S[ph + "_done"], 4)
            dve.drain().then_inc(S["all_done"], 1)

        def tail_loads(sp, load):
            if "C" in stages:
                load(rope[:], ins["rope"].rearrange("p (a b) -> p a b", a=2), "wC_in")
                load(head_of_row[:], ins["head_of_row"], "wC_in")
            sp.wait_ge(S["B_done"], 4)
            if "D" in stages:
                for c in range(2):
                    load(wgate[:, c, 0:NE, :], ins["L0_ffn_w_gate"][:, c * P:(c + 1) * P, :].rearrange("e p i -> p e i"), "wD_in")
                for c in range(2):
                    load(wup[:, c, 0:NE, :], ins["L0_ffn_w_up"][:, c * P:(c + 1) * P, :].rearrange("e p i -> p e i"), "wD_in")
                load(wgate[:, :, NE, :], ins["L0_ffn_sw_gate"].rearrange("(c p) i -> p c i", p=P), "wD_in")
                load(wup[:, :, NE, :], ins["L0_ffn_sw_up"].rearrange("(c p) i -> p c i", p=P), "wD_in")
                load(wdown[:, 0:NE, :], ins["L0_ffn_w_down"].rearrange("e i h -> i e h"), "wD_in")
                load(wdown[:, NE, :], ins["L0_ffn_sw_down"], "wD_in")
                load(router, ins["router_T"].rearrange("(c p) e -> p c e", p=P), "wD_in")
                load(earlier[:], ins["earlier"].rearrange("p (a b) -> p a b", a=8), "wD_in")
                sp.wait_ge(S["C_done"], 4)
                load(pick, ins["pick"].rearrange("p (a b) -> p a b", a=NE), "wD_in")
                load(rbias, ins["L0_ffn_correction_bias"].partition_broadcast(P), "wD_in")
            if "E" in stages:
                load(wq1, ins["L1_xattn_Wq"].rearrange("(c p) n -> p c n", p=P), "wE_in")
                for w_, n in ((wk1, "L1_xattn_Wk"), (wv1, "L1_xattn_Wv")):
                    load(w_[:, 0, :], ins[n][0:P, :], "wE_in")
                    load(w_[0:CD - P, 1, :], ins[n][P:CD, :], "wE_in")
                load(wo1, ins["L1_xattn_Wo"].rearrange("(c p) n -> p c n", p=P), "wE_in")
                load(pair_diag[:], ins["pair_diag"], "wE_in")
                load(fold, ins["fold"], "wE_in")
            if "G" in stages:
                load(w1_1, ins["L1_ffn_w1"].rearrange("(c p) n -> p c n", p=P), "wG_in")
                load(w2_1, ins["L1_ffn_w2"].rearrange("(c p) n -> p c n", p=P), "wG_in")
            sp.wait_ge(S["D_done"], 4)
            if "F" in stages:
                load(tq, ins["L1_attn_Wq"].rearrange("(c p) n -> p c n", p=P), "wF_in")
                load(tk, ins["L1_attn_Wk"].rearrange("(c p) n -> p c n", p=P), "wF_in")
                load(tv, ins["L1_attn_Wv"].rearrange("(c p) n -> p c n", p=P), "wF_in")
                load(to, ins["L1_attn_Wo"].rearrange("(c p) n -> p c n", p=P), "wF_in")
                load(causal[:], ins["causal"], "wF_in")
                sp.wait_ge(S["mix_zero"], 1)
                for f, n in enumerate(("L1_attn_pre_proj", "L1_attn_post_proj")):
                    for i in range(8):
                        load(mix[i * H16:(i + 1) * H16, f, i * H16:(i + 1) * H16], ins[n], "wF_in")
            if "E" in stages:
                sp.wait_ge(S["E_ready"], 1)
                def context(t, b):
                    one = bass.ds(t * 2 + b, 1)
                    load(ectx[b][:, 0, :], ins["ctxT"][one, 0:P, :].rearrange("a p j -> p (a j)"), f"E_ctx{b}_in")
                    load(ectx[b][0:CD - P, 1, :], ins["ctxT"][one, P:CD, :].rearrange("a p j -> p (a j)"), f"E_ctx{b}_in")

                def stack_keys(g, m):
                    sp.wait_ge(S["E_klo"], g * 6 + 2 * m + 3)
                    for j in range(NPAIR[m]):
                        rs = slice(32 * j, 32 * j + 32)
                        for k, part in enumerate((ehi[rs, m, :], elo[m][rs], ehi[rs, m, :])):
                            load(ekst[32 * k:32 * k + 32, 3 * m + j, :], part, f"E_kst{m}")

                def steps(t, last):
                    for b in range(2):
                        g = t * 2 + b
                        sp.wait_ge(S["E_sT_psum"], g * NJ + 1)
                        load(ekst[96:97, :, :].rearrange("p a b -> p (a b)"),
                             maskbias16_dram[bass.ds(t * 2 + b, 1), :], "E_bias_in")
                        stack_keys(g, 0)
                        if b == 0:
                            sp.wait_ge(S["E_qlo"], t + 1)
                            for j in range(3):
                                rs, n = slice(32 * j, 32 * j + 32), 3 if j < 2 else 2
                                for k, part in enumerate((eqhi, eqhi, eqlo)):
                                    load(eqst[32 * k:32 * k + 32, j:8:3, :], part[rs, 0:n, :], "E_qst")
                        stack_keys(g, 1)
                        stack_keys(g, 2)
                        if not last:
                            sp.wait_ge(S["E_v_psum"], g * 7 + 15)
                            context(t + 1, b)

                context(0, 0)
                context(0, 1)
                with sp.Fori(0, TILES - 1) as t:
                    steps(t, False)
                steps(TILES - 1, True)
            if "F" in stages:
                sp.wait_ge(S["E_done"], 4)
                for u in range(U):
                    for b in range(2):
                        load(fk[u][:, :, b, T:KEYS], ins["mem_kT"], "wF_in")
                        load(fv[u][T:KEYS, b, :], ins["L1_attn_mem_v"], "wF_in")


        block = ctx.enter_context(nc.Block())

        @block.sync
        def _(sp):
            def load(dst, src, name):
                sp.dma_start(dst, src).then_inc(S[name], 16)

            load(masku8, ins["ctx_mask"], "mask_in")
            load(textu8[0:T, :], ins["text_maskT"], "mask_in")
            load(textu8[T:P, :], ins["text_maskT"], "mask_in")
            load(X[:], ins["x"].rearrange("(t p) d -> p t d", p=P), "x_in")
            load(ident[:], ins["ident"], "wA_in")
            load(twice_eye[:], ins["twice_eye"], "wA_in")
            load(wq0, ins["L0_xattn_Wq"].rearrange("(c p) n -> p c n", p=P), "wA_in")
            load(wk0t, ins["L0_xattn_WkT"], "wA_in")
            sp.wait_ge(S["maskbias"], 1)
            sp.dma_start(maskbias_dram, maskrow).then_inc(S["maskbias_out"], 16)
            for p in range(8):
                sp.dma_start(maskbias16_dram[:, p * J:(p + 1) * J], maskrow16).then_inc(S["maskbias_out"], 16)
            sp.wait_ge(S["maskbias_out"], 144)

            def context(t, first):
                for b in range(2):
                    one = bass.ds(t * 2 + b, 1)
                    if not first:
                        sp.wait_ge(S["scores_psum"], t * 4 + 2 * b - 2)
                    load(ctxT[b][:, 0, :], ins["ctxT"][one, 0:P, :].rearrange("a p j -> p (a j)"), f"ctxT{b}_in")
                    load(ctxT[b][0:CD - P, 1, :], ins["ctxT"][one, P:CD, :].rearrange("a p j -> p (a j)"), f"ctxT{b}_in")
                    load(ctxT[b][CD - P:CD - P + 1, 1, :], maskbias_dram[one, :], f"ctxT{b}_in")
                for b in range(2):
                    one = bass.ds(t * 2 + b, 1)
                    if not first:
                        sp.wait_ge(S["cx_psum"], t * 2 + b - 1)
                    load(ctxN[b][:, 0:NJ - 1, :],
                         ins["ctx"][one, 0:(NJ - 1) * P, :].rearrange("a (c p) d -> p (a c) d", p=P), f"ctxN{b}_in")
                    load(ctxN[b][0:JL, NJ - 1, :],
                         ins["ctx"][one, (NJ - 1) * P:J, :].rearrange("a p d -> p (a d)"), f"ctxN{b}_in")

            context(0, True)
            with sp.Fori(1, TILES) as t:
                context(t, False)
            sp.wait_ge(S["A_done"], 4)
            if "C" in stages:
                load(aq, ins["L0_attn_wq"].rearrange("(c p) n -> p c n", p=P), "wC_in")
                load(adown, ins["L0_attn_w_down"].rearrange("(c p) n -> p c n", p=P), "wC_in")
                load(akv[:, 0:D], ins["L0_attn_wk_up"], "wC_in")
                load(akv[:, D:2 * D], ins["L0_attn_wv_up"], "wC_in")
                load(ao, ins["L0_attn_wo"].rearrange("(c p) n -> p c n", p=P), "wC_in")
            tail_loads(sp, load)
            sp.wait_ge(S["all_done"], 4)
            sp.dma_start(out.rearrange("(t p) d -> p t d", p=P), X[:]).then_inc(S["out"], 16)
            sp.wait_ge(S["out"], 16)

        @block.tensor
        def _(pe):
            mm = pe.matmul

            def mm2(out_, lhs, rhs):
                mm(out_, lhs[0], rhs[0], start=True, stop=False)
                return mm(out_, lhs[1], rhs[1], start=False, stop=True)

            pe.nop().then_inc(S["meanT_psum"], 2)
            pe.wait_ge(S["valid_diag"], 1)
            pe.wait_ge(S["ones"], 1)
            mm(PS[:, 0, 0:B], ones[0:B, :], small[0:B, 16:16 + B], start=True, stop=True).then_inc(S["valid_psum"], 1)
            pe.wait_ge(S["wA_in"], 16 * 4)

            def q_transposes(t):
                pe.wait_ge(S["xa"], t + 1)
                for c in range(2):
                    i_ = pe.transpose(PS[:, 6, c * P:(c + 1) * P], xa[:, c * P:(c + 1) * P], ident[:])
                i_.then_inc(S["xa_tp"], 1)

            def q_product(t):
                pe.wait_ge(S["xaT"], t + 1)
                mm2(PS[:, 7, 0:P], [wq0[:, c, :] for c in range(2)], [xaT[:, c, :] for c in range(2)]
                    ).then_inc(S["q_psum"], 1)

            def q_context(t):
                pe.wait_ge(S["qsplit"], t + 1)
                mm(PS[:, 6, :], wk0t[:, 0:P], qsplit.rearrange("p a b -> p (a b)"), start=True, stop=True)
                mm(PS[0:CD - P, 7, :], wk0t[:, P:CD], qsplit.rearrange("p a b -> p (a b)"), start=True, stop=True
                   ).then_inc(S["qctx_psum"], 1)

            def score(t, r):
                b, hp = r // 2, r % 2
                if r == 0:
                    pe.wait_ge(S["qctx"], t + 1)
                if hp == 0:
                    pe.wait_ge(S[f"ctxT{b}_in"], t * 48 + 48)
                pe.wait_ge(S["scores_sb"], t * 4 + r + 1)
                q0 = qctx[:, 0, b, 2 * hp:2 * hp + 2, :].rearrange("p a b -> p (a b)")
                q1 = qctx[0:CD - P + 1, 1, b, 2 * hp:2 * hp + 2, :].rearrange("p a b -> p (a b)")
                for n in range(4):
                    js = slice(n * 512, min(J, (n + 1) * 512))
                    o = PS[:, n, 0:js.stop - js.start]
                    mm(o, q0, ctxT[b][:, 0, js], start=True, stop=False)
                    i_ = mm(o, q1, ctxT[b][0:CD - P + 1, 1, js],
                            start=False, stop=True)
                i_.then_inc(S["scores_psum"], 1)

            def mean(t, b, between=None):
                pe.wait_ge(S["probs"], t * 4 + 2 * b + 4)
                pe.wait_ge(S["rowdiag"], t * 4 + 2 * b + 2)
                pe.wait_ge(S["meanT"], t * 2 + b + 1)
                pe.wait_ge(S["cx_out"], t * 2 + b + 1)
                for c in range(NJ):
                    if c == 8 and between is not None:
                        between()
                    r = P if c < NJ - 1 else JL
                    o = PS[0:r, 4 + c // 8, (c % 8) * T:(c % 8) * T + T]
                    for hp in range(2):
                        i_ = mm(o, probs[hp][:, c * P:c * P + r], rowdiag[b][hp], start=hp == 0, stop=hp == 1)
                i_.then_inc(S["meanT_psum"], 1)

            def gather(t, b):
                pe.wait_ge(S["meanT"], t * 2 + b + 2)
                pe.wait_ge(S[f"ctxN{b}_in"], t * 32 + 32)
                for o, ds in ((PS[:, 5, 320:320 + T], slice(0, P)), (PS[0:CD - P, 5, 384:384 + T], slice(P, CD))):
                    for c in range(NJ):
                        r = P if c < NJ - 1 else JL
                        i_ = mm(o, ctxN[b][0:r, c, ds], meanT[0:r, c, :], start=c == 0, stop=c == NJ - 1)
                i_.then_inc(S["cx_psum"], 1)

            def tile(t, first=False, last=False):
                if not last:
                    q_transposes(t + 1)
                score(t, 2)
                if not first:
                    gather(t - 1, 1)
                if not last:
                    q_product(t + 1)
                score(t, 3)
                mean(t, 0, None if last else lambda: q_context(t + 1))
                if not last:
                    score(t + 1, 0)
                gather(t, 0)
                if not last:
                    score(t + 1, 1)
                mean(t, 1)

            q_transposes(0)
            q_product(0)
            q_context(0)
            score(0, 0)
            score(0, 1)
            tile(0, first=True)
            with pe.Fori(1, TILES - 1) as t:
                tile(t)
            tile(TILES - 1, last=True)
            gather(TILES - 1, 1)
            pe.wait_ge(S["kern"], 1)
            pe.wait_ge(S["cx_out"], 2 * TILES + 1)
            for c in range(2):
                i_ = pe.transpose(PS[0:T, 0, c * P:(c + 1) * P], kern[:, c, :], ident[:])
            i_.then_inc(S["kern_tp"], 1)
            pe.wait_ge(S["kernT"], 1)
            pe.wait_ge(S["wB_in"], WB)
            for f in range(2):
                i_ = mm(PS[:, 1, f * D:(f + 1) * D], kdft[0:T, f, :], kernT[0:T, :], start=True, stop=True)
            i_.then_inc(S["kfreq_psum"], 1)
            pe.drain().then_inc(S["A_done"], 1)
            pe_rest(pe, mm, mm2)

        @block.scalar
        def _(act):
            def cp(o, i, scale=1.0):
                return nc.scalar.activation(o, i, ACT.Copy, scale=scale)

            act.dma_start(ssm[:, 0, :], ins["L0_xattn_A_re"].rearrange("(c p) n -> p c n", p=P)).then_inc(S["ssm_in"], 16)
            act.dma_start(ssm[:, 1, :], ins["L0_xattn_A_im"].rearrange("(c p) n -> p c n", p=P)).then_inc(S["ssm_in"], 16)
            act.dma_start(ssm[:, 2, :], ins["L0_xattn_C_re"].rearrange("(c p) n -> p c n", p=P)).then_inc(S["ssm_in"], 16)
            act.dma_start(ssm[:, 3, :], ins["L0_xattn_C_im"].rearrange("(c p) n -> p c n", p=P)).then_inc(S["ssm_in"], 16)
            act.dma_start(ldt, ins["L0_xattn_log_dt"]).then_inc(S["ssm_in"], 16)
            act.dma_start(small[:, 2:4], ins["L0_xattn_D_skip"]).then_inc(S["ssm_in"], 16)
            nb = [0]

            def loadB(dst, src):
                nb[0] += 16
                act.dma_start(dst, src).then_inc(S["wB_in"], 16)
            loadB(wv0[:, 0, :], ins["L0_xattn_Wv"][0:P, :])
            loadB(wv0[0:CD - P, 1, :], ins["L0_xattn_Wv"][P:CD, :])
            loadB(film[:, 0], ins["L0_xattn_W_film_in"].rearrange("(c p) n -> p c n", p=P))
            loadB(film[:, 1], ins["L0_xattn_W_film_out"].rearrange("(c p) n -> p c n", p=P))
            loadB(w1_0, ins["L0_xattn_W1"].rearrange("(c p) n -> p c n", p=P))
            loadB(w2_0, ins["L0_xattn_W2"].rearrange("(c p) n -> p c n", p=P))
            loadB(dft[:], ins["dft"].rearrange("p (a b c) -> p a b c", a=2, b=2))
            loadB(idft[:], ins["idft"].rearrange("p (a b) -> p a b", a=2))
            loadB(kdft[:], ins["kdft"].rearrange("p (a b) -> p a b", a=2))
            for i, n in enumerate(["L0_xattn_g_norm_in", "L0_xattn_b_norm_in", "L0_xattn_g_ffn", "L0_xattn_b_ffn",
                                   "L0_xattn_g_norm_out", "L0_xattn_b_norm_out", "L1_ffn_gamma", "L1_ffn_beta"]):
                loadB(gains[:, i, :], ins[n].partition_broadcast(P))
            loadB(gate[:], ins["L0_xattn_mod_gate"].partition_broadcast(P))
            loadB(cols[:, 0, :], ins["L0_xattn_b1"])
            loadB(cols[:, 1, :], ins["L1_ffn_b1"])
            for a, n in ((0, "L0_xattn_b_film_in"), (512, "L0_xattn_b_film_out"), (1024, "L0_xattn_b2"),
                         (1280, "L1_attn_bo"), (1536, "L1_ffn_b2")):
                w = 512 if a < 1024 else D
                loadB(rows[:, a:a + w], ins[n].rearrange("(a n) -> a n", a=1))
            assert nb[0] == WB, nb[0]
            act.wait_ge(S["angles"], 1)
            nc.scalar.activation(tm[4], tm[2], ACT.Sin, scale=0.5)
            nc.scalar.activation(tm[5], tm[3], ACT.Sin).then_inc(S["sines"], 1)
            for n in ("scores_sb", "meanT", "cx_out"):
                act.nop().then_inc(S[n], 1)

            def xaT_out(t):
                act.wait_ge(S["xa_tp"], t + 1)
                cp(xaT.rearrange("p a b -> p (a b)"), PS[:, 6, 0:D]).then_inc(S["xaT"], 1)

            def q_out(t):
                act.wait_ge(S["q_psum"], t + 1)
                for h in range(XH):
                    rs = slice(h * XD, (h + 1) * XD)
                    i_ = cp(qsplit[rs, h, :], PS[rs, 7, 0:P], 1.0 / float(np.sqrt(XD)))
                i_.then_inc(S["qsplit"], 1)

            def qctx_out(t, first=False):
                act.wait_ge(S["qctx_psum"], t + 1)
                if not first:
                    act.wait_ge(S["scores_psum"], t * 4)
                cp(qctx[:, 0].rearrange("p b h i -> p h b i"), PS[:, 6, :].rearrange("p (h b i) -> p h b i", h=XH, b=2))
                cp(qctx[0:CD - P, 1].rearrange("p b h i -> p h b i"),
                   PS[0:CD - P, 7, :].rearrange("p (h b i) -> p h b i", h=XH, b=2)).then_inc(S["qctx"], 1)

            def copy(t, r):
                act.wait_ge(S["probs"], t * 4 + r + 1)
                act.wait_ge(S["scores_psum"], t * 4 + r + 1)
                cp(scores[r % 2], bank(PS[:, 0:4, :], J)).then_inc(S["scores_sb"], 1)

            def exps(t, r):
                q = r % 2
                act.wait_ge(S["topk"], t * 4 + r + 1)
                nc.scalar.activation(topx[:, q, :], tops[:, q, :], ACT.Exp, bias=rowst[:, q, 0:1],
                                     accum_out=rowst[:, q, 1:2]).then_inc(S["zsum"], 1)
                nc.scalar.activation(scores[q], scores[q], ACT.Exp, bias=rowst[:, q, 0:1])
                nc.scalar.activation(rest[q], rest[q], ACT.Exp, bias=rowst[:, q, 0:1]).then_inc(S["exps"], 1)

            def mean_out(t, b):
                act.wait_ge(S["meanT_psum"], t * 2 + b + 3)
                cp(meanT[:, 0:8, :].rearrange("p a b -> p (a b)"), PS[:, 4, :])
                cp(meanT[:, 8:12, :].rearrange("p a b -> p (a b)"), PS[:, 5, 0:4 * T])
                cp(meanT[0:JL, 12, :], PS[0:JL, 5, 4 * T:5 * T]).then_inc(S["meanT"], 1)

            def cx_out(t, b):
                act.wait_ge(S["cx_psum"], t * 2 + b + 1)
                nc.scalar.activation(spare(), ones[:, 0:1], ACT.Copy)
                cp(CX[:, 0, bass.ds(t * P + b * T, T)], PS[:, 5, 320:320 + T])
                cp(CX[0:CD - P, 1, bass.ds(t * P + b * T, T)], PS[0:CD - P, 5, 384:384 + T]).then_inc(S["cx_out"], 1)

            def tile(t, first=False, last=False):
                exps(t, 0)
                if not first:
                    mean_out(t - 1, 1)
                if not last:
                    xaT_out(t + 1)
                copy(t, 2)
                exps(t, 1)
                if not first:
                    cx_out(t - 1, 1)
                if not last:
                    q_out(t + 1)
                copy(t, 3)
                if not last:
                    qctx_out(t + 1)
                exps(t, 2)
                mean_out(t, 0)
                if not last:
                    copy(t + 1, 0)
                exps(t, 3)
                cx_out(t, 0)
                if not last:
                    copy(t + 1, 1)

            xaT_out(0)
            q_out(0)
            qctx_out(0, first=True)
            copy(0, 0)
            copy(0, 1)
            tile(0, first=True)
            with act.Fori(1, TILES - 1) as t:
                tile(t)
            tile(TILES - 1, last=True)
            mean_out(TILES - 1, 1)
            cx_out(TILES - 1, 1)
            act.drain().then_inc(S["A_done"], 1)
            act_rest(act, cp)

        @block.vector
        def _(dve):
            v = nc.vector

            own = Own(dve, S["dve_setup"])
            dve.wait_ge(S["mask_in"], 48)
            own.step(v.tensor_scalar(maskrow, masku8, -1.0, BIG, ALU.add, ALU.mult))
            own.step(v.tensor_copy(maskrow16, maskrow))
            v.nop().then_inc(S["maskbias"], 1)
            own.step(v.tensor_reduce(small[0:B, 8:9], maskrow, AXX, ALU.max))
            own.step(v.tensor_scalar(small[0:B, 9:10], small[0:B, 8:9], -1.0, None, ALU.is_ge))
            dve.wait_ge(S["wA_in"], 64)
            own.step(v.tensor_scalar(small[0:B, 16:16 + B], ident[0:B, 0:B], small[0:B, 9:10], None, ALU.mult))
            v.nop().then_inc(S["valid_diag"], 1)
            dve.wait_ge(S["valid_psum"], 1)
            own.step(v.tensor_copy(valid[:], PS[:, 0, 0:B]))
            own.step(v.reciprocal(small[:, 32:32 + B], valid[:]))
            own.step(v.scalar_tensor_tensor(small[:, 48:48 + B], valid[:], 1.0 / XH, small[:, 32:32 + B], ALU.mult, ALU.mult))
            own.step(v.tensor_tensor(qmask[:], textu8, small[:, 48:48 + B], ALU.mult))

            own.step(v.memset(mix[:], 0.0))
            v.nop().then_inc(S["mix_zero"], 1)
            dve.wait_ge(S["x_in"], 16)
            for i in range(TILES):
                own.step(v.bn_stats(bnA[:, 0:6], X[:, i, :]))
                own.step(v.bn_aggr(bnA[:, 6:8], bnA[:, 0:6]))
                own.step(v.tensor_copy(lnA[:, 0:2, i], bnA[:, 6:8]))
            v.tensor_scalar(lnA[:, 1, :], lnA[:, 1, :], EPS, None, ALU.add).then_inc(S["A_var"], 1)

            def normed(t):
                v.tensor_scalar(xa, X[:, bass.ds(t, 1), :].rearrange("p a b -> p (a b)"), lnA[:, 0, bass.ds(t, 1)],
                                lnA[:, 2, bass.ds(t, 1)], ALU.subtract, ALU.mult).then_inc(S["xa"], 1)

            dve.wait_ge(S["A_rstd"], 1)
            normed(0)

            dve.wait_ge(S["ssm_in"], 96)
            MAGIC = 12582912.0

            def expm1(o, x, k, q, s, si):
                own.step(v.tensor_scalar(k, x, 1.4426950408889634, MAGIC, ALU.mult, ALU.add))
                own.step(v.tensor_scalar(k, k, -MAGIC, None, ALU.add))
                own.step(v.scalar_tensor_tensor(o, k, -0.693359375, x, ALU.mult, ALU.add))
                own.step(v.scalar_tensor_tensor(o, k, 2.12194440e-4, o, ALU.mult, ALU.add))
                own.step(v.tensor_scalar(q, o, 1.0 / 5040, None, ALU.mult))
                for c in (720, 120, 24, 6, 2, 1):
                    own.step(v.scalar_tensor_tensor(q, q, 1.0 / c, o, ALU.add, ALU.mult))
                own.step(v.tensor_scalar(si, k, 127.0, 8388608.0, ALU.add, ALU.mult))
                own.step(v.tensor_tensor(q, q, s, ALU.mult))
                own.step(v.scalar_tensor_tensor(o, s, -1.0, q, ALU.add, ALU.add))

            e = small
            expm1(e[:, 64:66], ldt, e[:, 66:68], e[:, 68:70], e[:, 70:72], e[:, 70:72].bitcast(I32))
            own.step(v.tensor_scalar(e[:, 64:66], e[:, 64:66], 1.0, None, ALU.add))
            for c in range(2):
                cs = slice(c * NST, (c + 1) * NST)
                own.step(v.tensor_scalar(tm[0][:, cs], ssm[:, 0, cs], e[:, 64 + c:65 + c], None, ALU.mult))
                own.step(v.tensor_scalar(tm[1][:, cs], ssm[:, 1, cs], e[:, 64 + c:65 + c], None, ALU.mult))
            twopi = 2 * np.pi
            c1 = 6.28125
            c2 = float(np.float32(np.round((twopi - c1) * 2 ** 22) / 2 ** 22))
            c3 = float(twopi - c1 - c2)
            own.step(v.tensor_scalar(tm[3], tm[1], 1 / twopi, MAGIC, ALU.mult, ALU.add))
            own.step(v.tensor_scalar(tm[3], tm[3], -MAGIC, None, ALU.add))
            own.step(v.scalar_tensor_tensor(tm[2], tm[3], -c1, tm[1], ALU.mult, ALU.add))
            own.step(v.scalar_tensor_tensor(tm[2], tm[3], -c2, tm[2], ALU.mult, ALU.add))
            own.step(v.scalar_tensor_tensor(tm[2], tm[3], -c3, tm[2], ALU.mult, ALU.add))
            own.step(v.scalar_tensor_tensor(tm[3], tm[2], -1.0, tm[2], ALU.mult, ALU.max))
            own.step(v.tensor_scalar(tm[3], tm[3], -0.5, float(np.pi / 2), ALU.mult, ALU.add))
            v.nop().then_inc(S["angles"], 1)
            expm1(tm[1], tm[0], tm[6], tm[7], tm[8], tm[8].bitcast(I32))
            dve.wait_ge(S["sines"], 1)
            own.step(v.scalar_tensor_tensor(tm[6], tm[4], 2.0, tm[5], ALU.mult, ALU.mult))
            own.step(v.scalar_tensor_tensor(tm[7], tm[4], -2.0, tm[4], ALU.mult, ALU.mult))
            own.step(v.scalar_tensor_tensor(wpow[:, 0, 1, :], tm[7], 1.0, tm[1], ALU.add, ALU.mult))
            own.step(v.tensor_tensor(tm[0], wpow[:, 0, 1, :], tm[7], ALU.add))
            own.step(v.scalar_tensor_tensor(wpow[:, 1, 1, :], tm[1], 1.0, tm[6], ALU.add, ALU.mult))
            own.step(v.tensor_scalar(wpow[:, 0, 1, :], tm[0], 1.0, None, ALU.add))
            own.step(v.memset(wpow[:, 0, 0, :], 1.0))
            own.step(v.memset(wpow[:, 1, 0, :], 0.0))
            own.step(v.memset(wbig[:, 0, 0, :], 1.0))
            own.step(v.memset(wbig[:, 1, 0, :], 0.0))
            are, aim, cre, cim = (ssm[:, i, :] for i in range(4))
            wi = wpow[:, 1, 1, :]
            own.step(v.tensor_tensor(tm[1], are, are, ALU.mult))
            own.step(v.tensor_tensor(tm[2], aim, aim, ALU.mult))
            own.step(v.tensor_tensor(tm[1], tm[1], tm[2], ALU.add))
            own.step(v.reciprocal(tm[2], tm[1]))
            own.step(v.tensor_tensor(tm[3], tm[0], are, ALU.mult))
            own.step(v.tensor_tensor(tm[4], wi, aim, ALU.mult))
            own.step(v.tensor_tensor(tm[3], tm[3], tm[4], ALU.add))
            own.step(v.scalar_tensor_tensor(tm[3], tm[3], 2.0, tm[2], ALU.mult, ALU.mult))
            own.step(v.tensor_tensor(tm[4], wi, are, ALU.mult))
            own.step(v.tensor_tensor(tm[5], tm[0], aim, ALU.mult))
            own.step(v.tensor_tensor(tm[4], tm[4], tm[5], ALU.subtract))
            own.step(v.scalar_tensor_tensor(tm[4], tm[4], 2.0, tm[2], ALU.mult, ALU.mult))
            own.step(v.tensor_tensor(tm[5], cre, tm[3], ALU.mult))
            own.step(v.tensor_tensor(tm[6], cim, tm[4], ALU.mult))
            own.step(v.tensor_tensor(tm[0], tm[5], tm[6], ALU.subtract))
            own.step(v.tensor_tensor(tm[5], cre, tm[4], ALU.mult))
            own.step(v.tensor_tensor(tm[6], cim, tm[3], ALU.mult))
            own.step(v.tensor_tensor(tm[1], tm[5], tm[6], ALU.add))
            v.nop().then_inc(S["ssm_base"], 1)

            def row_scale(own, t, r):
                q, b, hp = r % 2, r // 2, r % 2
                dve.wait_ge(S["zsum"], t * 4 + r + 1)
                own.step(v.reciprocal(rowst[:, q, 2:3], rowst[:, q, 1:2]))
                dve.wait_ge(S["meanT_psum"], t * 2 + b + 1)
                v.tensor_scalar(rowdiag[b][hp], twice_eye[:], rowst[:, q, 2:3], qmask[:, bass.ds(t * 2 + b, 1)],
                                ALU.mult, ALU.mult).then_inc(S["rowdiag"], 1)

            def topk(own, t, r, before=None):
                q = r % 2
                dve.wait_ge(S["probs"], t * 4 + r + 1)
                dve.wait_ge(S["scores_sb"], t * 4 + r + 2)
                nc.vector.memset(spare(), 0.0)
                src = scores[q]
                for i in range(KTOP // 8):
                    t8 = tops[:, q, i * 8:i * 8 + 8]
                    own.need(own.mark(v.max(t8, src)))
                    if i == 0:
                        v.tensor_scalar(rowst[:, q, 0:1], t8[:, 0:1], -1.0, None, ALU.mult)
                    last = v.match_replace(rest[q], t8, src, LOW)
                    if i < KTOP // 8 - 1:
                        own.need(own.mark(last))
                    src = rest[q]
                    if i == 1 and before is not None:
                        row_scale(own, *before)
                last.then_inc(S["topk"], 1)

            def lags(t, c):
                dve.wait_ge(S["kprod"], t * 2 + c + 1)
                nc.vector.memset(spare(), 0.0)
                v.tensor_reduce(kern[:, c, bass.ds(t * 8, 8)], prod, AXX, ALU.add).then_inc(S["kpart"], 1)

            def tile(t, first=False, last=False):
                own = Own(dve, S["dve_turn"])
                topk(own, t, 0, None if first else (t - 1, 3))
                if not last:
                    dve.wait_ge(S["xa_tp"], t + 1)
                    normed(t + 1)
                topk(own, t, 1, (t, 0))
                topk(own, t, 2, (t, 1))
                if not first:
                    lags(t - 1, 0)
                topk(own, t, 3, (t, 2))
                if not first:
                    lags(t - 1, 1)
                own.end()

            tile(0, first=True)
            with dve.Fori(1, TILES - 1) as t:
                tile(t)
            tile(TILES - 1, last=True)
            own = Own(dve, S["dve_turn"])
            row_scale(own, TILES - 1, 3)
            own.end()
            for c in range(2):
                lags(TILES - 1, c)
            own = Own(dve, S["dve_setup2"])
            dve.wait_ge(S["kpart"], 2 * TILES + 1)
            for c in range(2):
                own.step(v.tensor_tensor(kern[:, c, 0:1], kern[:, c, 0:1], small[:, 2 + c:3 + c], ALU.add))
            v.nop().then_inc(S["kern"], 1)
            dve.wait_ge(S["kern_tp"], 1)
            v.tensor_copy(kernT[0:T, :], PS[0:T, 0, 0:D]).then_inc(S["kernT"], 1)
            dve.wait_ge(S["kfreq_psum"], 1)
            v.tensor_copy(kfreq[:], PS[:, 1, :]).then_inc(S["kfreq"], 1)
            dve.drain().then_inc(S["A_done"], 1)
            dve_rest(dve, v)

        @block.gpsimd
        def _(pool):
            g = nc.gpsimd
            own = Own(pool, S["pool_setup"])
            own.step(g.memset(ones[:], 1.0))
            own.step(g.memset(mhalf[:], -0.5))
            own.step(g.memset(qsplit, 0.0))
            own.step(g.memset(qctx[CD - P:CD - P + 1, 1], 1.0))
            g.nop().then_inc(S["ones"], 1)
            g.nop().then_inc(S["probs"], 2)
            g.nop().then_inc(S["kpart"], 1)

            def cmul(o, x, y, tmp):
                own.step(g.tensor_tensor(tmp[0], x[0], y[0], ALU.mult))
                own.step(g.tensor_tensor(tmp[1], x[1], y[1], ALU.mult))
                own.step(g.tensor_tensor(tmp[2], x[0], y[1], ALU.mult))
                own.step(g.tensor_tensor(tmp[3], x[1], y[0], ALU.mult))
                own.step(g.tensor_tensor(o[0], tmp[0], tmp[1], ALU.subtract))
                own.step(g.tensor_tensor(o[1], tmp[2], tmp[3], ALU.add))

            def wide(pw, a, n):
                return pw[:, 0, a:a + n, :], pw[:, 1, a:a + n, :]

            tmp = [coef[:, i // 4, (i % 4) * 2:(i % 4) * 2 + 2, :] for i in range(8)]
            tmp1 = [x[:, 0:1] for x in tmp]

            def powers(pw):
                cmul(wide(pw, 2, 1), wide(pw, 1, 1), wide(pw, 1, 1), tmp1)
                cmul(wide(pw, 3, 1), wide(pw, 2, 1), wide(pw, 1, 1), tmp1)
                cmul(wide(pw, 4, 1), wide(pw, 2, 1), wide(pw, 2, 1), tmp1)
                f4 = [pw[:, i, 4:5, :].to_broadcast([P, 2, P]) for i in range(2)]
                cmul(wide(pw, 5, 2), wide(pw, 1, 2), f4, tmp)
                cmul(wide(pw, 7, 1), wide(pw, 3, 1), wide(pw, 4, 1), tmp1)

            def coefficients(b):
                x = [wpow[:, i, b, :] for i in range(2)]
                cmul([coef[:, i, b, :] for i in range(2)], x, [tm[0], tm[1]], [tm[3], tm[4], tm[5], tm[6]])

            pool.wait_ge(S["A_var"], 1)
            g.tensor_tensor(lnA[:, 2, :], lnA[:, 1, :], mhalf[:].to_broadcast([P, TILES]), ALU.pow).then_inc(S["A_rstd"], 1)

            def prob(t, r):
                pool.wait_ge(S["meanT_psum"], t * 2 + r // 2 + 2)
                pool.wait_ge(S["exps"], t * 4 + r + 1)
                g.tensor_tensor(probs[r % 2], scores[r % 2], rest[r % 2], ALU.subtract).then_inc(S["probs"], 1)

            def lag_terms(own, t, c):
                cs = slice(c * NST, (c + 1) * NST)
                pool.wait_ge(S["kpart"], t * 2 + c + 1)
                nc.gpsimd.tensor_tensor(spare(), mhalf[:], mhalf[:], ALU.add)
                x = [wbig[:, i, bass.ds(t, 1), cs].to_broadcast([P, 8, NST]) for i in range(2)]
                g.tensor_tensor(prod, coef[:, 0, :, cs], x[0], ALU.mult)
                own.step(g.tensor_tensor(prod2, coef[:, 1, :, cs], x[1], ALU.mult))
                g.tensor_tensor(prod, prod, prod2, ALU.subtract).then_inc(S["kprod"], 1)

            pool.wait_ge(S["ssm_base"], 1)
            powers(wpow)
            prob(0, 0)
            cmul(wide(wbig, 1, 1), wide(wpow, 4, 1), wide(wpow, 4, 1), tmp1)
            powers(wbig)
            prob(0, 1)
            for b in range(4):
                coefficients(b)
            prob(0, 2)
            for b in range(4, 8):
                coefficients(b)
            prob(0, 3)
            with pool.Fori(1, TILES) as t:
                own = Own(pool, S["pool_A"])
                prob(t, 0)
                prob(t, 1)
                lag_terms(own, t - 1, 0)
                prob(t, 2)
                lag_terms(own, t - 1, 1)
                prob(t, 3)
                own.end()
            own = Own(pool, S["pool_A"])
            for c in range(2):
                lag_terms(own, TILES - 1, c)
            own.end()
            pool.drain().then_inc(S["A_done"], 1)
            for phase, lns in (("B", 4), ("C", 1), ("D", 1), ("E", 1), ("F", 1), ("G", 2)):
                if phase not in stages:
                    continue
                pool.wait_ge(S[chr(ord(phase) - 1) + "_done"], 4)
                if phase > "B":
                    for s_ in S.of_phase_before(phase):
                        pool.sem_clear(s_)
                with pool.Fori(0, TILES // U) as j:
                    for i in range(lns):
                        for u in range(U):
                            pool.wait_ge(S[f"{phase}{i}_var"], j * U + u + 1)
                            b_ = bn[0 if phase == "E" else u]
                            g.tensor_tensor(b_[:, 9:10], b_[:, 8:9], mhalf[:], ALU.pow
                                            ).then_inc(S[f"{phase}{i}_rstd"], 1)
                pool.drain().then_inc(S[phase + "_done"], 1)
            g.drain().then_inc(S["all_done"], 1)


_PLAIN = ["x", "ctx", "L0_xattn_Wq", "L0_xattn_Wv", "L0_xattn_W_film_in", "L0_xattn_b_film_in", "L0_xattn_W_film_out",
          "L0_xattn_b_film_out", "L0_xattn_g_norm_in", "L0_xattn_b_norm_in", "L0_xattn_g_norm_out",
          "L0_xattn_b_norm_out", "L0_xattn_g_ffn", "L0_xattn_b_ffn", "L0_xattn_W1", "L0_xattn_b1", "L0_xattn_W2",
          "L0_xattn_b2", "L0_xattn_log_dt", "L0_xattn_A_re", "L0_xattn_A_im", "L0_xattn_C_re", "L0_xattn_C_im",
          "L0_xattn_D_skip", "L0_attn_wq", "L0_attn_w_down", "L0_attn_wk_up", "L0_attn_wv_up", "L0_attn_wo",
          "L0_ffn_correction_bias", "L0_ffn_w_gate", "L0_ffn_w_up", "L0_ffn_w_down", "L0_ffn_sw_gate",
          "L0_ffn_sw_up", "L0_ffn_sw_down", "L1_xattn_Wq", "L1_xattn_Wk", "L1_xattn_Wv", "L1_xattn_Wo",
          "L1_attn_Wq", "L1_attn_Wk", "L1_attn_Wv", "L1_attn_pre_proj", "L1_attn_post_proj", "L1_attn_mem_v",
          "L1_attn_Wo", "L1_attn_bo", "L1_ffn_w1", "L1_ffn_b1", "L1_ffn_w2", "L1_ffn_b2", "L1_ffn_gamma",
          "L1_ffn_beta"]
STAGES = "ABCDEFG"


def kernel(**inputs):
    import numpy as _np
    import concourse.bacc as _bacc
    from concourse import mybir as _mybir
    from concourse.bass_utils import run_bass_kernel_spmd as _run

    a = {n: _np.asarray(v) for n, v in inputs.items()}
    a["x"] = a["x"].reshape(B * T, D)
    a["ctx"] = a["ctx_768"]
    a["ctxT"] = a["ctx_768"].transpose(0, 2, 1)
    a["ctx_mask"] = a["mask_BxS2_bf1"]
    a["text_maskT"] = a["mask_BxS_bf1"].T
    a["L0_xattn_WkT"] = a["L0_xattn_Wk"].T
    a["L0_xattn_mod_gate"] = a["L0_xattn_mod_gate"].reshape(1)
    a["router_T"] = a["L0_ffn_router_weight"].T
    for n in ("L1_ffn_w1", "L1_ffn_b1", "L1_ffn_w2", "L1_ffn_b2"):
        a[n] = a[n][0]
    for n in ("L0_xattn_log_dt", "L0_xattn_D_skip", "L0_xattn_b1", "L1_ffn_b1"):
        a[n] = a[n].reshape(-1, P).T
    mk = a["L1_attn_mem_k"].reshape(8, 2, MEM, AD)
    a["mem_kT"] = mk.transpose(1, 3, 0, 2).reshape(P, 8, MEM)
    a["L1_attn_mem_v"] = a["L1_attn_mem_v"].transpose(1, 0, 2).reshape(MEM, 16 * AD)
    names = _PLAIN + ["ctxT", "ctx_mask", "text_maskT", "L0_xattn_WkT", "L0_xattn_mod_gate", "router_T", "mem_kT"]
    table = constants()
    a.update(table)
    nc = _bacc.Bacc("TRN2", target_bir_lowering=False, num_devices=1)
    arrays, ins = {}, {}
    for n in names + list(table):
        v = _np.ascontiguousarray(a[n])
        arrays[f"in_{n}"] = v
        ins[n] = nc.dram_tensor(f"in_{n}", v.shape, _mybir.dt.from_np(v.dtype), kind="ExternalInput").ap()
    out = nc.dram_tensor("out", (B * T, D), _mybir.dt.float32, kind="ExternalOutput").ap()
    perceiver(nc, ins, out, STAGES)
    r = _run(nc, [arrays], core_ids=[0])
    return r.results[0]["out"].reshape(B, T, D)
```
